# Optimizing a Trainium2 kernel written in Bass

```python
import numpy as np
import jax
import jax.numpy as jnp

def _softmax(x, axis=-1):
    return jax.nn.softmax(x, axis=axis)

def _gelu(x):
    return jax.nn.gelu(x, approximate=True)

def _silu(x):
    return jax.nn.silu(x)

def _sigmoid(x):
    return jax.nn.sigmoid(x)

def _layernorm(x, axis=-1, eps=1e-05):
    m = jnp.mean(x, axis=axis, keepdims=True)
    v = jnp.var(x, axis=axis, keepdims=True)
    return (x - m) / jnp.sqrt(v + eps)

def _scatter_add(tgt, idx, src, axis=0):
    return tgt.at[idx].add(src)

def _segment_sum(src, seg, n):
    return jax.ops.segment_sum(src, seg, n)
kernel_name = 'mk_prb_d2_jaxref_r8_49ae02'

def setup_inputs(seed: int=0):
    np.random.seed(seed)
    _w = jnp.asarray

    def _L0_attn_setup():
        import jax, jax.numpy as jnp
        import numpy as np
        B, S, D, H, R = (2, 256, 128, 16, 64)
        HD = D // H
        VOCAB = 2 * R + 1
        key = jax.random.key(seed)
        ks = jax.random.split(key, 7)
        s = 0.02
        return {'x': jax.random.normal(ks[0], (B, S, D), jnp.float32), 'W_qkv': jax.random.normal(ks[1], (D, 3 * D), jnp.float32) * s, 'b_qkv': jnp.zeros((3 * D,), jnp.float32), 'W_out': jax.random.normal(ks[2], (D, D), jnp.float32) * s, 'b_out': jnp.zeros((D,), jnp.float32), 'rel_emb_k': jax.random.normal(ks[3], (VOCAB, HD), jnp.float32) * s, 'rel_emb_v': jax.random.normal(ks[4], (VOCAB, HD), jnp.float32) * s}
    _L0_attn_in = _L0_attn_setup()

    def _L0_ffn_setup():
        import jax, jax.numpy as jnp
        import numpy as np
        DIM = 128
        MOE_HID = 64
        SHARED_HID = 256
        N_EXPERTS = 16
        TOP_K = 2
        NORM_TOPK_PROB = True
        key = jax.random.key(seed)
        ks = jax.random.split(key, 9)
        s = 0.02
        x = jax.random.normal(ks[0], (2, 128, DIM), dtype=jnp.float32)
        Wg = jax.random.normal(ks[1], (N_EXPERTS, DIM), dtype=jnp.float32) * s
        We_gate = jax.random.normal(ks[2], (N_EXPERTS, MOE_HID, DIM), dtype=jnp.float32) * s
        We_up = jax.random.normal(ks[3], (N_EXPERTS, MOE_HID, DIM), dtype=jnp.float32) * s
        We_down = jax.random.normal(ks[4], (N_EXPERTS, DIM, MOE_HID), dtype=jnp.float32) * s
        Ws_gate = jax.random.normal(ks[5], (SHARED_HID, DIM), dtype=jnp.float32) * s
        Ws_up = jax.random.normal(ks[6], (SHARED_HID, DIM), dtype=jnp.float32) * s
        Ws_down = jax.random.normal(ks[7], (DIM, SHARED_HID), dtype=jnp.float32) * s
        Wsg = jax.random.normal(ks[8], (1, DIM), dtype=jnp.float32) * s
        return {'x': x, 'Wg': Wg, 'We_gate': We_gate, 'We_up': We_up, 'We_down': We_down, 'Ws_gate': Ws_gate, 'Ws_up': Ws_up, 'Ws_down': Ws_down, 'Wsg': Wsg}
    _L0_ffn_in = _L0_ffn_setup()

    def _L1_attn_setup():
        import math
        import jax, jax.numpy as jnp
        import numpy as np
        D_MODEL = 128
        N_HEADS = 16
        HEAD_DIM = D_MODEL // N_HEADS
        B, L = (1, 512)

        def _slopes(n_heads):
            ratio = 2.0 ** (-8.0 / n_heads)
            return jnp.asarray([ratio ** (i + 1) for i in range(n_heads)], dtype=jnp.float32)
        key = jax.random.key(seed)
        ks = jax.random.split(key, 5)
        scale = 1.0 / math.sqrt(D_MODEL)
        return {'x': jax.random.normal(ks[0], (B, L, D_MODEL), dtype=jnp.float32), 'q_w': jax.random.normal(ks[1], (D_MODEL, D_MODEL), dtype=jnp.float32) * scale, 'k_w': jax.random.normal(ks[2], (D_MODEL, D_MODEL), dtype=jnp.float32) * scale, 'v_w': jax.random.normal(ks[3], (D_MODEL, D_MODEL), dtype=jnp.float32) * scale, 'o_w': jax.random.normal(ks[4], (D_MODEL, D_MODEL), dtype=jnp.float32) * scale}
    _L1_attn_in = _L1_attn_setup()

    def _L1_ffn_setup():
        import math
        import jax, jax.numpy as jnp
        import numpy as np
        NUM_EXPERTS = 16
        TOP_K = 2
        CAPACITY_FACTOR = 1.25
        key = jax.random.key(seed)
        k1, k2, k3, k4 = jax.random.split(key, 4)
        d, dff, E = (128, 512, NUM_EXPERTS)
        x = jax.random.normal(k1, (4, 256, d), dtype=jnp.float32)
        router_w = jax.random.normal(k2, (E, d), dtype=jnp.float32) * d ** (-0.5)
        router_b = jnp.zeros((E,), dtype=jnp.float32)
        w1 = jax.random.normal(k3, (E, d, dff), dtype=jnp.float32) * 0.02
        b1 = jnp.zeros((E, dff), dtype=jnp.float32)
        w2 = jax.random.normal(k4, (E, dff, d), dtype=jnp.float32) * 0.02
        b2 = jnp.zeros((E, d), dtype=jnp.float32)
        return {'x': x, 'router_w': router_w, 'router_b': router_b, 'w1': w1, 'b1': b1, 'w2': w2, 'b2': b2}
    _L1_ffn_in = _L1_ffn_setup()
    _d = {'L0_attn_x': _L0_attn_in['x'], 'L0_attn_W_qkv': _L0_attn_in['W_qkv'], 'L0_attn_b_qkv': _L0_attn_in['b_qkv'], 'L0_attn_W_out': _L0_attn_in['W_out'], 'L0_attn_b_out': _L0_attn_in['b_out'], 'L0_attn_rel_emb_k': _L0_attn_in['rel_emb_k'], 'L0_attn_rel_emb_v': _L0_attn_in['rel_emb_v'], 'L0_ffn_Wg': _L0_ffn_in['Wg'], 'L0_ffn_We_gate': _L0_ffn_in['We_gate'], 'L0_ffn_We_up': _L0_ffn_in['We_up'], 'L0_ffn_We_down': _L0_ffn_in['We_down'], 'L0_ffn_Ws_gate': _L0_ffn_in['Ws_gate'], 'L0_ffn_Ws_up': _L0_ffn_in['Ws_up'], 'L0_ffn_Ws_down': _L0_ffn_in['Ws_down'], 'L0_ffn_Wsg': _L0_ffn_in['Wsg'], 'L1_attn_q_w': _L1_attn_in['q_w'], 'L1_attn_k_w': _L1_attn_in['k_w'], 'L1_attn_v_w': _L1_attn_in['v_w'], 'L1_attn_o_w': _L1_attn_in['o_w'], 'L1_ffn_router_w': _L1_ffn_in['router_w'], 'L1_ffn_router_b': _L1_ffn_in['router_b'], 'L1_ffn_w1': _L1_ffn_in['w1'], 'L1_ffn_b1': _L1_ffn_in['b1'], 'L1_ffn_w2': _L1_ffn_in['w2'], 'L1_ffn_b2': _L1_ffn_in['b2']}
    _x0 = _d['L0_attn_x']
    _d['L0_attn_x'] = jax.random.normal(jax.random.fold_in(jax.random.key(seed), 1), (32, 256, 128), dtype=_x0.dtype)
    del _x0
    return _d

def reference(L0_attn_x, L0_attn_W_qkv, L0_attn_b_qkv, L0_attn_W_out, L0_attn_b_out, L0_attn_rel_emb_k, L0_attn_rel_emb_v, L0_ffn_Wg, L0_ffn_We_gate, L0_ffn_We_up, L0_ffn_We_down, L0_ffn_Ws_gate, L0_ffn_Ws_up, L0_ffn_Ws_down, L0_ffn_Wsg, L1_attn_q_w, L1_attn_k_w, L1_attn_v_w, L1_attn_o_w, L1_ffn_router_w, L1_ffn_router_b, L1_ffn_w1, L1_ffn_b1, L1_ffn_w2, L1_ffn_b2):

    def _L0_attn_ref(x, W_qkv, b_qkv, W_out, b_out, rel_emb_k, rel_emb_v):
        import jax, jax.numpy as jnp
        import numpy as np
        B, S, D, H, R = (2, 256, 128, 16, 64)
        HD = D // H
        VOCAB = 2 * R + 1
        b, s, d = x.shape
        hd = d // H
        idx = jnp.arange(s)
        dist = jnp.clip(idx[None, :] - idx[:, None], -R, R) + R
        pe_k = rel_emb_k[dist]
        pe_v = rel_emb_v[dist]
        qkv = (x @ W_qkv + b_qkv).reshape(b, s, 3, H, hd)
        qkv = jnp.transpose(qkv, (2, 0, 3, 1, 4))
        q, k, v = (qkv[0], qkv[1], qkv[2])
        q = q / jnp.sqrt(jnp.asarray(hd, x.dtype))
        score = jnp.einsum('bhqd,bhkd->bhqk', q, k) + jnp.einsum('bhqd,qkd->bhqk', q, pe_k)
        attn = jax.nn.softmax(score, axis=-1)
        ctx = jnp.einsum('bhqk,bhkd->bhqd', attn, v) + jnp.einsum('bhqk,qkd->bhqd', attn, pe_v)
        ctx = jnp.transpose(ctx, (0, 2, 1, 3)).reshape(b, s, d)
        return ctx @ W_out + b_out

    def _L0_ffn_ref(x, Wg, We_gate, We_up, We_down, Ws_gate, Ws_up, Ws_down, Wsg):
        import jax, jax.numpy as jnp
        import numpy as np
        DIM = 128
        MOE_HID = 64
        SHARED_HID = 256
        N_EXPERTS = 16
        TOP_K = 2
        NORM_TOPK_PROB = True
        B, S, D = x.shape
        xt = x.reshape(-1, D)
        gates = jax.nn.softmax(xt @ Wg.T, axis=-1)
        scores, inds = jax.lax.top_k(gates, TOP_K)
        if NORM_TOPK_PROB:
            scores = scores / jnp.sum(scores, axis=-1, keepdims=True)
        g = jnp.einsum('td,ehd->teh', xt, We_gate)
        u = jnp.einsum('td,ehd->teh', xt, We_up)
        h = jax.nn.silu(g) * u
        y_all = jnp.einsum('teh,edh->ted', h, We_down)
        y_sel = jnp.take_along_axis(y_all, inds[:, :, None], axis=1)
        y = jnp.sum(y_sel * scores[:, :, None], axis=1)
        shared = jax.nn.silu(xt @ Ws_gate.T) * (xt @ Ws_up.T) @ Ws_down.T
        y = y + jax.nn.sigmoid(xt @ Wsg.T) * shared
        return y.reshape(B, S, D)

    def _L1_attn_ref(x, q_w, k_w, v_w, o_w):
        import math
        import jax, jax.numpy as jnp
        import numpy as np
        D_MODEL = 128
        N_HEADS = 16
        HEAD_DIM = D_MODEL // N_HEADS
        B, L = (1, 512)

        def _slopes(n_heads):
            ratio = 2.0 ** (-8.0 / n_heads)
            return jnp.asarray([ratio ** (i + 1) for i in range(n_heads)], dtype=jnp.float32)
        b, l, _ = x.shape

        def proj(w):
            return (x @ w).reshape(b, l, N_HEADS, HEAD_DIM).transpose(0, 2, 1, 3)
        q, k, v = (proj(q_w), proj(k_w), proj(v_w))
        scale = math.sqrt(HEAD_DIM)
        scores = jnp.einsum('bhid,bhjd->bhij', q, k) / scale
        pos = jnp.arange(l)
        distance = jnp.abs(pos[None, :] - pos[:, None]).astype(jnp.float32)
        alibi = -distance[None, :, :] * _slopes(N_HEADS)[:, None, None]
        scores = scores + alibi[None]
        causal = pos[None, :] <= pos[:, None]
        scores = jnp.where(causal[None, None], scores, -jnp.inf)
        attn = jax.nn.softmax(scores, axis=-1)
        out = jnp.einsum('bhij,bhjd->bhid', attn, v)
        out = out.transpose(0, 2, 1, 3).reshape(b, l, D_MODEL)
        return out @ o_w

    def _L1_ffn_ref(x, router_w, router_b, w1, b1, w2, b2):
        import math
        import jax, jax.numpy as jnp
        import numpy as np
        NUM_EXPERTS = 16
        TOP_K = 2
        CAPACITY_FACTOR = 1.25
        E, k = (NUM_EXPERTS, TOP_K)
        B, S, d = x.shape
        tokens = B * S
        capacity = max(1, int(math.ceil(CAPACITY_FACTOR * tokens * k / E)))
        x2d = x.reshape(tokens, d)
        logits = x2d @ router_w.T + router_b
        vals, idx = jax.lax.top_k(logits, k)
        gates = jax.nn.softmax(vals, axis=-1)
        flat_e = idx.reshape(-1)
        oh = (flat_e[:, None] == jnp.arange(E)[None, :]).astype(jnp.int32)
        pos = jnp.take_along_axis(jnp.cumsum(oh, axis=0) - 1, flat_e[:, None], axis=1)[:, 0]
        kept = pos < capacity
        kept2 = kept.reshape(tokens, k)
        denom = jnp.sum(gates * kept2, axis=-1, keepdims=True)
        gates = jnp.where(kept2, gates / (denom + 1e-09), 0.0)
        slot = flat_e * capacity + pos
        slot_safe = jnp.where(kept, slot, E * capacity)
        x_rep = jnp.repeat(x2d, k, axis=0)
        buf = jnp.zeros((E * capacity + 1, d), x.dtype).at[slot_safe].set(x_rep)
        packed = buf[:E * capacity].reshape(E, capacity, d)
        h = jax.nn.gelu(jnp.einsum('ecd,edf->ecf', packed, w1) + b1[:, None, :], approximate=False)
        expert_out = jnp.einsum('ecf,efd->ecd', h, w2) + b2[:, None, :]
        eflat = expert_out.reshape(E * capacity, d)
        gathered = eflat[jnp.clip(slot, 0, E * capacity - 1)]
        w = (gates.reshape(-1) * kept.astype(x.dtype))[:, None]
        out = (gathered * w).reshape(tokens, k, d).sum(axis=1)
        return out.reshape(B, S, d)
    x = L0_attn_x
    xn = _layernorm(x, axis=-1)
    x = x + _L0_attn_ref(xn, L0_attn_W_qkv, L0_attn_b_qkv, L0_attn_W_out, L0_attn_b_out, L0_attn_rel_emb_k, L0_attn_rel_emb_v) + _L0_ffn_ref(xn, L0_ffn_Wg, L0_ffn_We_gate, L0_ffn_We_up, L0_ffn_We_down, L0_ffn_Ws_gate, L0_ffn_Ws_up, L0_ffn_Ws_down, L0_ffn_Wsg)
    xn = _layernorm(x, axis=-1)
    x = x + _L1_attn_ref(xn, L1_attn_q_w, L1_attn_k_w, L1_attn_v_w, L1_attn_o_w) + _L1_ffn_ref(xn, L1_ffn_router_w, L1_ffn_router_b, L1_ffn_w1, L1_ffn_b1, L1_ffn_w2, L1_ffn_b2)
    return x

_drawn_inputs = setup_inputs


def setup_inputs(seed=0):
    import zlib

    import numpy as np

    out = dict(_drawn_inputs(seed))
    spreads = {'L0_attn_b_qkv': (0.0, 0.8),
     'L0_attn_b_out': (0.0, 0.308),
     'L1_ffn_router_b': (0.0, 0.689),
     'L1_ffn_b1': (0.0, 1.543),
     'L1_ffn_b2': (0.0, 0.419)}
    factors = {'L0_attn_W_qkv': 8.0,
     'L0_attn_rel_emb_k': 59.81,
     'L0_attn_rel_emb_v': 60.336,
     'L0_ffn_Wg': 8.0,
     'L0_ffn_We_gate': 8.0,
     'L0_ffn_We_up': 8.0,
     'L0_ffn_We_down': 8.0,
     'L0_ffn_Ws_gate': 8.0,
     'L0_ffn_Ws_up': 8.0,
     'L0_ffn_Ws_down': 8.0,
     'L0_ffn_Wsg': 8.0,
     'L1_ffn_w1': 4.932}
    for name, (base, spread) in spreads.items():
        noise = np.random.default_rng([zlib.crc32(name.encode()), seed]).standard_normal(out[name].shape)
        drawn = base * np.exp(spread * noise) if base else spread * noise
        out[name] = jnp.asarray(drawn.astype(out[name].dtype))
    for name, factor in factors.items():
        out[name] = (out[name] * factor).astype(out[name].dtype)
    return out
```

```python
import math
from contextlib import ExitStack

import numpy as np
import concourse.bass as bass
from concourse import mybir
from concourse.alu_op_type import AluOpType as ALU

F32 = mybir.dt.float32
BF16 = mybir.dt.bfloat16
I32 = mybir.dt.int32
U32 = mybir.dt.uint32
ACT = mybir.ActivationFunctionType
AX = mybir.AxisListType

P = 128
S = 256
D = 128
H = 16
C = 8
R = 64
QG = 8
GS = 2
NS = S // (QG * GS)
KT = S // P
E = 16
HID = 64
SH = 256
NK = E * HID // P + SH // P
FF = 512
EPS = 1e-5
MAGIC = 0x5F3759DF
OW = D + QG * C

CONSTS = {"ident": P, "mask_head_rows": H, "mask_rep": 2 * QG * 2, "mask_head": H, "mask_query": QG,
          "pick_query": QG, "iota": E, "dump": 4}
NCONST = sum(CONSTS.values())
WEIGHTS = {"wqkv": 3 * D, "wout": D, "wgate": E * HID + SH, "wup": E * HID + SH, "wdown": NK * D,
           "wrouter0": E, "wshared_gate": 1, "bq": 1, "bk": 1, "bq_rep": H // 2,
           "q1": D, "k1": D, "v1": D, "o1": D, "wrouter1": E, "b1": E * FF // P}
NWEIGHT = sum(WEIGHTS.values())
ROWS = {"bv": D, "bout": D, "brouter1": E}
NROW = sum(ROWS.values())

JOBS_A = [(0, "router0", "mid"), (0, "up0", "mid"), (1, "up1", "mid"), (1, "up2", "mid"), (2, "up3", "mid"),
          (3, "gateT", "mid"), (3, "xnT", "front"), (4, "up4", "mid"), (4, "up5", "mid"),
          (5, "out", "tail"), (5, "spread0", "mid"), (6, "qk", "front"), (6, "v", "front"),
          (7, "up6", "mid"), (7, "spread1", "mid"), (8, "xn2T", "tail"), (8, "up7", "mid"),
          (9, "rep0", "front"), (9, "spread2", "mid"), (10, "router1", "tail"), (10, "rep1", "front"),
          (11, "rep2", "front"), (11, "spread3", "mid"), (12, "prefix", "tail"), (12, "rep3", "front"),
          (13, "up8", "mid"), (13, "up9", "mid"), (14, "shared", "mid")]
JOBS_B = [(5, "out", "tail"), (8, "qk", "front"), (9, "v", "front")]

SECTIONS = {"pro": {"front"}, "first": {"mid", "front"}, "mid": {"tail", "mid", "front"},
            "last": {"tail", "mid"}, "end": {"tail"}}


class Tally:

    def __init__(self, nb, events):
        self.nb, self.events = nb, events

    def total(self, kind):
        return sum(s in SECTIONS[kind] for _, s in self.events)

    def __call__(self, kind, b, name):
        present = [n for n, s in self.events if s in SECTIONS[kind]]
        rank = present.index(name) + 1
        if kind == "pro":
            return rank
        if kind == "first":
            return rank + self.total("pro")
        base = rank + self.total("pro") + self.total("first")
        if kind == "end":
            return base + self.total("mid") * (self.nb - 2) + self.total("last")
        return (b - 1) * self.total("mid") + base


def bodies(engine, nb, body):
    body("pro", -1, 1)
    body("first", 0, 0)
    with engine.Fori(0, (nb - 2) // 2) as i:
        b = engine.snap(2 * i + 1)
        body("mid", b, 1)
        body("mid", b + 1, 0)
    body("last", nb - 1, 1)
    body("end", nb, 0)


def program(nc, io, nb, cap):
    T = nb * S
    NT = T // P
    SLOTS = E * cap
    JT = cap // P
    ctx = ExitStack()
    with ctx:
        def sb(name, shape, dt=F32):
            return ctx.enter_context(nc.sbuf_tensor(name, shape, dt))

        def sem(name):
            return ctx.enter_context(nc.semaphore(name))

        packed = nc.dram_tensor("packed", (SLOTS + 2 * T, D), F32).ap()
        expert_out = nc.dram_tensor("expert_out", (SLOTS, D), F32).ap()
        NU = 2 * S - 1
        rel_k_ext = nc.dram_tensor("rel_k_ext", (C, NU), F32).ap()
        rel_v_ext = nc.dram_tensor("rel_v_ext", (NU, C), F32).ap()

        consts = sb("consts", [P, NCONST])
        weights = sb("weights", [P, NWEIGHT])
        rows = sb("rows", [P, NROW])
        cview, at = {}, 0
        for name, n in CONSTS.items():
            cview[name] = consts[:, at:at + n]
            at += n
        wview, at = {}, 0
        for name, n in WEIGHTS.items():
            wview[name] = weights[:, at:at + n]
            at += n
        rview, at = {}, 0
        for name, n in ROWS.items():
            rview[name] = rows[:, at:at + n]
            at += n
        ident = cview["ident"]
        spread = sb("spread", [E, E * HID])
        tri = sb("tri", [P, 2 * P], BF16)
        alibi_l = sb("alibi_l", [3 * QG, P], BF16)
        alibi_r = sb("alibi_r", [3 * QG, S - QG + S], BF16)
        residual = sb("residual", [P, NT, D])
        xnT1 = sb("xnT1", [P, T])
        slot_ids = sb("slot_ids", [P, NT, 2], U32)
        slot_w = sb("slot_w", [P, NT, 2])

        load_sem = sem("load")
        x_first = sem("x_first")
        x_rest = sem("x_rest")
        zeroed = sem("zeroed")

        with ExitStack() as pa:
            def sa(name, shape, dt=F32):
                return pa.enter_context(nc.sbuf_tensor(name, shape, dt))

            def pa_bank(name):
                return pa.enter_context(nc.psum_tensor(name, [P, 512], F32))

            S_ps = [pa_bank(f"scores{i}") for i in range(2)]
            PT_ps = [pa_bank(f"probsT{i}") for i in range(2)]
            O_ps = pa_bank("values")
            CTX_ps = pa_bank("context")
            M_ps = [pa_bank(f"spare{i}") for i in range(2)]

            rel_k = sa("rel_k", [P, 2 * S - QG])
            rel_v = sa("rel_v", [P, S + P, C])
            wq_rep = sa("wq_rep", [P, H // 2, P])
            wshared = sa("wshared", [P, P])
            bq_s = sa("bq_s", [P, 1])
            bq_rep_s = sa("bq_rep_s", [P, H // 2])
            tri_f = sa("tri_f", [P, 2 * P])
            alibi_lf = sa("alibi_lf", [3 * QG, P])
            alibi_rf = sa("alibi_rf", [3 * QG, 2 * S - QG])
            xnT = [sa(f"xnT_{i}", [P, S]) for i in range(2)]
            qT = [sa(f"qT_{i}", [P, S]) for i in range(2)]
            kT = [sa(f"kT_{i}", [P, S]) for i in range(2)]
            vv = [sa(f"v_{i}", [P, KT, D]) for i in range(2)]
            q_rep = [sa(f"q_rep_{i}", [P, H // 2, S]) for i in range(2)]
            hid = [sa(f"hid_{i}", [P, NK, S]) for i in range(2)]
            xn = sa("xn", [P, 2, D])
            q_blk = [sa(f"q_blk_{i}", [P, GS, P]) for i in range(2)]
            q_rel = [sa(f"q_rel_{i}", [P, GS, P]) for i in range(2)]
            probs = [sa(f"probs_{i}", [P, GS, S]) for i in range(2)]
            probsT = [sa(f"probsT_s{i}", [P, KT, GS, P]) for i in range(2)]
            nmax = [sa(f"nmax_{i}", [P, GS]) for i in range(4)]
            rsum = [sa(f"rsum_{i}", [P, GS]) for i in range(4)]
            rinv = [sa(f"rinv_{i}", [P, GS]) for i in range(4)]
            pick = [sa(f"pick_{i}", [P, GS, QG]) for i in range(4)]
            rel_m = [sa(f"rel_m_{i}", [P, GS, QG, C]) for i in range(2)]
            rel_s = [sa(f"rel_s_{i}", [P, GS, C]) for i in range(2)]
            z1 = [sa(f"z1_{i}", [P, GS, D]) for i in range(2)]
            zz = [sa(f"zz_{i}", [P, GS, D]) for i in range(2)]
            ctxT = sa("ctxT", [P, S])
            th = [sa(f"th_{i}", [P, S]) for i in range(2)]
            ga = sa("ga", [P, S])
            gate_bc = sa("gate_bc", [P, E // 2, S])
            shared_bc = sa("shared_bc", [P, S])
            shared_th = sa("shared_th", [P, S])
            gates = sa("gates", [P, 2, E])
            gatesT = sa("gatesT", [E, S])
            x1a = sa("x1a", [P, 2, D])
            x1 = sa("x1", [P, 2, D])
            xn2 = sa("xn2", [P, 2, D])
            xn2T = sa("xn2T", [P, S])
            stats = sa("stats", [P, 2, 6])
            mv = sa("mv", [P, 2, 2])
            nw = sa("nw", [P, 5, 2])
            top = [{n: sa(f"{n}_{i}", sh, dt) for n, sh, dt in
                    (("logit", [P, 2, E], F32), ("m8", [P, 2, 8], F32), ("i8", [P, 2, 8], U32), ("idx", [P, 2, 2], F32),
                     ("gap", [P, 2], F32), ("ex", [P, 2], F32), ("den", [P, 2], F32), ("g", [P, 2, 2], F32),
                     ("oh", [P, 2, 2, E], F32), ("t0", [P, 2, E], F32), ("t1", [P, 2, E], F32))} for i in range(2)]
            chosen = sa("chosen", [P, 2, E], BF16)
            counts = sa("counts", [P, E])
            pos = sa("pos", [P, 2, E])
            posk = sa("posk", [P, 2, 2, E])
            pk = sa("pk", [P, 2, 2])
            kept = sa("kept", [P, 2, 2])
            slot = sa("slot", [P, 2, 2])
            sk = sa("sk", [P, 2, 2])
            dumpk = sa("dumpk", [P, 2, 2])
            dump_at = sa("dump_at", [P, 2, 2])
            gk = sa("gk", [P, 2, 2])
            gden = sa("gden", [P, 2])
            scat_f = sa("scat_f", [P, 2, 2])
            scat = sa("scat", [P, 2, 2], U32)
            zeros = hid[1]

            cleared = sem("zeros_cleared")
            act_ready = sem("biases_scaled")
            dve_ready = sem("weights_repeated")
            built = sem("queries_built")
            scored = sem("scores_ready")
            maxed = sem("max_ready")
            exped = sem("probs_ready")
            turned = sem("probsT_ready")
            moved = sem("probsT_moved")
            valued = sem("values_ready")
            picked = sem("pick_ready")
            merged = sem("z1_ready")
            masked = sem("z_ready")
            ctxed = sem("context_done")
            ctx_moved = sem("context_moved")
            full = [sem("spare0_full"), sem("spare1_full")]
            free = [sem("spare0_free"), sem("spare1_free")]
            th_done = sem("tanh_done")
            hid_done = sem("hidden_done")
            xn_done = sem("xn_done")
            gates_done = sem("gates_done")
            gap_done = sem("gap_done")
            ex_done = sem("ex_done")
            xn2_done = sem("xn2_done")
            chosen_done = sem("chosen_done")
            xnT1_done = sem("xnT1_done")
            slots_done = sem("slots_done")
            scattered = sem("scattered")
            rows_known = sem("rows_known")
            chain = sem("dve_chain")
            ext_sem = sem("ext")
            row_sem = sem("row_loaded")
            row_extended = sem("row_extended")
            rel_k_row = sa("rel_k_row", [C, NU])

            bank_of = {name: i % 2 for i, (_, name, _) in enumerate(JOBS_A)}
            bank_events = [[(n, s) for _, n, s in JOBS_A if bank_of[n] == i] for i in range(2)]
            bank_tally = [Tally(nb, ev) for ev in bank_events]
            ups = [(n, s) for _, n, s in JOBS_A if n.startswith("up")]
            th_tally = Tally(nb, ups)
            spr_tally = Tally(nb, [(n, s) for _, n, s in JOBS_A if n.startswith("spread") or n == "shared"])
            one_front = Tally(nb, [("x", "front")])
            one_tail = Tally(nb, [("x", "tail")])
            one_mid = Tally(nb, [("x", "mid")])
            two = Tally(nb, [("router0", "mid"), ("router1", "tail")])
            idx_of = {n: i for i, (_, n, _) in enumerate(JOBS_A)}

            def jobs(kind, step):
                return [n for s, n, sec in JOBS_A if s == step and sec in SECTIONS[kind]]

            def present(kind, s, lag):
                return kind in (("first", "mid", "last") if s >= lag else ("mid", "last", "end"))

            def steps(kind):
                return range(NS)

            block = pa.enter_context(nc.Block())

            @block.sync
            def _(sp):
                sp.dma_start(residual[:, 0:4, :], io["x"][0:512, :].rearrange("(n p) d -> p n d", p=P)).then_inc(x_first, 16)
                sp.dma_start(consts[:, :], io["consts"]).then_inc(load_sem, 16)
                sp.dma_start(weights[:, :], io["weights"]).then_inc(load_sem, 16)
                sp.dma_start(rows[:, :], io["rows"].partition_broadcast(P)).then_inc(load_sem, 16)
                sp.dma_start(spread[:, :], io["spread"]).then_inc(load_sem, 16)
                sp.dma_start(tri_f[:, :], io["tri"]).then_inc(load_sem, 16)
                sp.dma_start(alibi_lf[:, :], io["alibi_l"]).then_inc(load_sem, 16)
                sp.dma_start(alibi_rf[:, :], io["alibi_r"]).then_inc(load_sem, 16)
                lo, n = S - 1 - R, 2 * R + 1
                ek, ev = io["rel_k"], io["rel_v"]
                sp.dma_start(rel_k_row[:, lo:lo + n], ek).then_inc(row_sem, 16)
                sp.dma_start(rel_v_ext[lo:lo + n, :], ev).then_inc(ext_sem, 16)
                sp.dma_start(rel_v_ext[0:lo, :], ev[0:1, :].to_broadcast((lo, C))).then_inc(ext_sem, 16)
                sp.dma_start(rel_v_ext[lo + n:NU, :], ev[n - 1:n, :].to_broadcast((lo, C))).then_inc(ext_sem, 16)
                sp.wait_ge(row_extended, 2)
                sp.dma_start(rel_k_ext, rel_k_row[:, :]).then_inc(ext_sem, 16)
                sp.wait_ge(ext_sem, 64)
                W = 2 * S - QG
                for hp in range(2):
                    for q in range(QG):
                        p0 = hp * QG * C + q * C
                        sp.dma_start(rel_k[p0:p0 + C, :], rel_k_ext[:, QG - 1 - q:QG - 1 - q + W]).then_inc(load_sem, 16)
                sp.dma_start(rel_v[:, :, :].rearrange("p s c -> p (s c)"),
                             bass.AP(tensor=rel_v_ext.tensor, offset=0, ap=[[C, P], [1, (S + P) * C]])).then_inc(load_sem, 16)
                for n in range(4, NT, 4):
                    m = min(4, NT - n)
                    sp.dma_start(residual[:, n:n + m, :],
                                 io["x"][P * n:P * (n + m), :].rearrange("(n p) d -> p n d", p=P)).then_inc(x_rest, 16)
                sp.wait_ge(cleared, 1)
                nz = NK * S // D * P
                flat = zeros[:, :, :].rearrange("p a b -> p (a b)")
                for r0 in range(0, SLOTS, nz):
                    m = min(nz, SLOTS - r0)
                    sp.dma_start(packed[r0:r0 + m, :].rearrange("(p a) d -> p (a d)", p=P),
                                 flat[:, 0:m // P * D]).then_inc(zeroed, 16)
            LOADS = 16 * (7 + 2 * QG + 1)
            NZERO = 16 * -(-SLOTS // (NK * S // D * P))
            XREST = 16 * len(range(4, NT, 4))

            @block.gpsimd
            def _(pool):
                pool.wait_ge(load_sem, LOADS)

                def build(kind, s, par, t1):
                    pool.tensor_tensor(q_blk[s % 2][:, :, :].rearrange("p g (q h) -> p (g q) h", h=H),
                                       qT[par][:, 16 * s:16 * s + 16].unsqueeze(2).to_broadcast((P, 16, H)),
                                       cview["mask_head_rows"].unsqueeze(1).to_broadcast((P, 16, H)), ALU.mult)
                    pool.tensor_tensor(q_rel[s % 2][:, :, :].rearrange("p g (q j k) -> p (g q) j k", j=H // 2, k=2),
                                       q_rep[par][:, :, 16 * s:16 * s + 16].rearrange("p j q -> p q j").unsqueeze(3)
                                       .to_broadcast((P, 16, H // 2, 2)),
                                       cview["mask_rep"].rearrange("p (q k) -> p q k", k=2).unsqueeze(2)
                                       .to_broadcast((P, 16, H // 2, 2)), ALU.mult).then_inc(built, 1)

                def body(kind, b, par):
                    t0 = pool.snap(b * NS) if kind == "mid" else b * NS
                    if kind == "pro":
                        for j in ("qk", "rep0", "rep1", "rep2", "rep3"):
                            pool.wait_ge(free[bank_of[j]], bank_tally[bank_of[j]](kind, b, j))
                        build(kind, 0, 0, 1)
                        return
                    for s in steps(kind):
                        if kind != "end" and not (kind == "last" and s == NS - 1):
                            if s == NS - 1:
                                for j in ("qk", "rep0", "rep1", "rep2", "rep3"):
                                    pool.wait_ge(free[bank_of[j]], bank_tally[bank_of[j]](kind, b, j))
                            if not (kind == "first" and s == 0):
                                pool.wait_ge(scored, t0 + s)
                            build(kind, (s + 1) % NS, par if s < NS - 1 else 1 - par, None)
                        if present(kind, s, 2) and not (kind == "end" and s >= 2):
                            pool.wait_ge(merged, t0 + s - 1)
                            pool.tensor_tensor(zz[s % 2][:, :, :].rearrange("p g (h c) -> p g h c", c=C),
                                               z1[s % 2][:, :, :].rearrange("p g (h c) -> p g h c", c=C),
                                               cview["mask_head"].unsqueeze(1).unsqueeze(3).to_broadcast((P, GS, H, C)),
                                               ALU.mult).then_inc(masked, 1)
                        tail = "tail" in SECTIONS[kind]
                        if s == 10 and tail:
                            j = "xn2T"
                            pool.wait_ge(free[bank_of[j]], bank_tally[bank_of[j]](kind, b, j))
                            pool.tensor_copy(xnT1[:, bass.ds((b - 1) * S, S)], xn2T[:, :]).then_inc(xnT1_done, 1)
                        if s == 14 and tail:
                            pool.sem_clear(rows_known)
                            pool.wait_ge(slots_done, one_tail(kind, b, "x"))
                            pool.tensor_tensor(scat_f[:, :, :], dumpk[:, :, :], sk[:, :, :], ALU.add).then_inc(rows_known, 1)
                            pool.wait_ge(rows_known, 1)
                            pool.tensor_copy(scat[:, :, :], scat_f[:, :, :]).then_inc(rows_known, 1)
                            pool.wait_ge(rows_known, 2)
                            if kind == "mid" and par == 1:
                                pool.wait_ge(zeroed, NZERO)
                            for i in range(2):
                                for k in range(2):
                                    pool.indirect_dma_start(
                                        out=packed, out_offset=bass.IndirectOffsetOnAxis(ap=scat[:, i, k:k + 1], axis=0),
                                        in_=xn2[:, i, :], in_offset=None).then_inc(scattered, 16)
                pool.dma_start(xn2[:, 0, :], io["x"][0:P, :]).then_inc(scattered, 16)
                bodies(pool, nb, body)
                pool.wait_ge(scattered, 64 * nb + 16)

            @block.scalar
            def _(act):
                act.wait_ge(load_sem, LOADS)
                act.mul(bq_s[:, :], wview["bq"], C ** -0.5)
                act.mul(bq_rep_s[:, :], wview["bq_rep"], C ** -0.5).then_inc(act_ready, 1)
                act.wait_ge(act_ready, 1)

                def move(kind, b, par, name):
                    bank = bank_of[name]
                    m, n = M_ps[bank], bank_tally[bank](kind, b, name)
                    if name.startswith("up"):
                        k = int(name[2:])
                        act.wait_ge(full[bank], n)
                        act.activation(th[k % 2][:, :], m[:, 0:S], ACT.Tanh, scale=0.5).then_inc(th_done, 1)
                    elif name == "router0" or name == "router1":
                        i = 0 if name == "router0" else 1
                        act.wait_ge(gap_done, two(kind, b, name))
                        act.activation(top[i]["ex"][:, :], top[i]["gap"][:, :], ACT.Exp).then_inc(ex_done, 1)
                    elif name == "gateT":
                        act.wait_ge(full[bank], n)
                        act.copy(gatesT[:, :], m[0:E, 0:S]).then_inc(free[bank], 1)
                    elif name.startswith("spread"):
                        j = int(name[6:])
                        act.wait_ge(full[bank], n)
                        act.copy(gate_bc[:, 2 * j:2 * j + 2, :], m[:, 0:2 * S].rearrange("p (a b) -> p a b", a=2)).then_inc(free[bank], 1)
                    elif name == "shared":
                        act.wait_ge(full[bank], n)
                        act.activation(shared_th[:, :], m[:, 0:S], ACT.Tanh, scale=0.5).then_inc(free[bank], 1)
                    elif name == "xnT":
                        act.wait_ge(full[bank], n)
                        act.copy(xnT[1 - par][:, :], m[:, 0:S]).then_inc(free[bank], 1)
                    elif name == "xn2T":
                        act.wait_ge(full[bank], n)
                        act.copy(xn2T[:, :], m[:, 0:S]).then_inc(free[bank], 1)
                    elif name == "qk":
                        act.wait_ge(full[bank], n)
                        act.activation(qT[1 - par][:, :], m[:, 0:S], ACT.Identity, bias=bq_s[:, 0:1], scale=C ** -0.5)
                        act.activation(kT[1 - par][:, :], m[:, S:2 * S], ACT.Identity, bias=wview["bk"]).then_inc(free[bank], 1)
                    elif name.startswith("rep"):
                        j = int(name[3:])
                        act.wait_ge(full[bank], n)
                        for i in range(2):
                            ins = act.activation(q_rep[1 - par][:, 2 * j + i, :], m[:, i * S:(i + 1) * S], ACT.Identity,
                                                 bias=bq_rep_s[:, 2 * j + i:2 * j + i + 1], scale=C ** -0.5)
                        ins.then_inc(free[bank], 1)

                def body(kind, b, par):
                    t0 = act.snap(b * NS) if kind == "mid" else b * NS
                    for s in steps(kind):
                        if s:
                            for name in jobs(kind, s - 1):
                                move(kind, b, par, name)
                        if s == 3 and "tail" in SECTIONS[kind]:
                            act.wait_ge(ctxed, t0)
                            act.copy(ctxT[:, :], CTX_ps[:, 0:S]).then_inc(ctx_moved, 1)
                        if present(kind, s, 0):
                            act.wait_ge(maxed, t0 + s + 1)
                            for g in range(GS):
                                ins = act.activation(probs[s % 2][:, g, :], S_ps[s % 2][:, g * S:(g + 1) * S], ACT.Exp,
                                                     bias=nmax[s % 4][:, g:g + 1], accum_out=rsum[s % 4][:, g:g + 1])
                            ins.then_inc(exped, 1)
                        if present(kind, s, 1) and not (kind == "end" and s >= 1):
                            act.wait_ge(turned, t0 + s)
                            act.copy(probsT[(s - 1) % 2][:, :, :, :].rearrange("p a b c -> p (a b c)"),
                                     PT_ps[(s - 1) % 2][:, :]).then_inc(moved, 1)
                bodies(act, nb, body)

            @block.vector
            def _(dve):
                dve.memset(zeros[:, :, :], 0.0).then_inc(cleared, 1)
                lo, n = S - 1 - R, 2 * R + 1
                dve.wait_ge(row_sem, 16)
                dve.tensor_copy(rel_k_row[:, 0:lo], rel_k_row[:, lo:lo + 1].to_broadcast((C, lo))).then_inc(row_extended, 1)
                dve.tensor_copy(rel_k_row[:, lo + n:NU], rel_k_row[:, lo + n - 1:lo + n].to_broadcast((C, lo))).then_inc(row_extended, 1)
                dve.wait_ge(load_sem, LOADS)
                dve.tensor_copy(wq_rep[:, :, :].rearrange("p j (k q c) -> p (j k) q c", k=2, q=QG),
                                wview["wqkv"][:, 0:D].rearrange("p (h c) -> p h c", c=C).unsqueeze(2)
                                .to_broadcast((P, H, QG, C)))
                for half, whole in ((tri, tri_f), (alibi_l, alibi_lf), (alibi_r, alibi_rf)):
                    dve.tensor_copy(half[:, :], whole[:, :])
                dve.tensor_copy(wshared[:, :], wview["wshared_gate"].to_broadcast((P, P))).then_inc(dve_ready, 1)
                dve.tensor_copy(dump_at[:, :, :], cview["dump"].rearrange("p (i k) -> p i k", k=2))
                dve.memset(counts[:, :], 0.0).then_inc(dve_ready, 1)
                dve.wait_ge(dve_ready, 2)
                links = [0]

                def link(ins):
                    links[0] += 1
                    ins.then_inc(chain, 1)
                    dve.wait_ge(chain, links[0])

                def layernorm(tile_of, normalised, done):
                    for i in range(2):
                        ins = dve.bn_stats(stats[:, i, :], tile_of(i))
                    link(ins)
                    for i in range(2):
                        ins = dve.bn_aggr(mv[:, i, :], stats[:, i, :])
                    link(ins)
                    v, y, a, c = nw[:, 0, :], nw[:, 1, :], nw[:, 2, :], nw[:, 3, :]
                    link(dve.tensor_scalar(v, mv[:, :, 1], EPS, None, ALU.add))
                    link(dve.tensor_scalar(a.bitcast(I32), v.bitcast(I32), 1, None, ALU.logical_shift_right))
                    link(dve.tensor_scalar(y.bitcast(I32), a.bitcast(I32), -1.0, float(MAGIC), ALU.mult, ALU.add))
                    for _ in range(3):
                        link(dve.tensor_tensor(a, y, y, ALU.mult))
                        link(dve.scalar_tensor_tensor(c, a, -0.5, v, ALU.mult, ALU.mult))
                        link(dve.scalar_tensor_tensor(y, c, 1.5, y, ALU.add, ALU.mult))
                    for i in range(2):
                        ins = dve.tensor_scalar(normalised[:, i, :], tile_of(i), mv[:, i, 0:1], y[:, i:i + 1], ALU.subtract, ALU.mult)
                    ins.then_inc(done, 1)

                def top_two(kind, b, i, name, bank, bias):
                    q = top[i]
                    m = M_ps[bank][:, 0:2 * E].rearrange("p (t e) -> p t e", e=E)
                    if bias is None:
                        ins = dve.tensor_copy(q["logit"][:, :, :], m)
                    else:
                        ins = dve.tensor_tensor(q["logit"][:, :, :], m, bias.unsqueeze(1).to_broadcast((P, 2, E)), ALU.add)
                    link(ins)
                    dve.max(q["m8"][:, 0, :], q["logit"][:, 0, :]).then_inc(free[bank], 1)
                    link(dve.max(q["m8"][:, 1, :], q["logit"][:, 1, :]))
                    dve.tensor_tensor(q["gap"][:, :], q["m8"][:, :, 1], q["m8"][:, :, 0], ALU.subtract).then_inc(gap_done, 1)
                    for j in range(2):
                        ins = dve.max_index(q["i8"][:, j, :], q["m8"][:, j, :], q["logit"][:, j, :])
                    link(ins)
                    link(dve.tensor_copy(q["idx"][:, :, :], q["i8"][:, :, 0:2]))
                    for k in range(2):
                        ins = dve.tensor_tensor(q["oh"][:, :, k, :], cview["iota"].unsqueeze(1).to_broadcast((P, 2, E)),
                                                q["idx"][:, :, k:k + 1].to_broadcast((P, 2, E)), ALU.is_equal)
                    dve.wait_ge(ex_done, two(kind, b, name))
                    link(dve.tensor_scalar(q["den"][:, :], q["ex"][:, :], 1.0, None, ALU.add))
                    link(dve.reciprocal(q["g"][:, :, 0], q["den"][:, :]))
                    link(dve.tensor_tensor(q["g"][:, :, 1], q["g"][:, :, 0], q["ex"][:, :], ALU.mult))

                def handle(kind, b, par, name):
                    if name not in ("gateT", "xnT", "xn2T", "qk", "rep0", "rep1", "rep2", "rep3", "spread0",
                                    "spread1", "spread2", "spread3", "shared"):
                        bank = bank_of[name]
                        m, n = M_ps[bank], bank_tally[bank](kind, b, name)
                        dve.wait_ge(full[bank], n)
                    if name == "router0":
                        top_two(kind, b, 0, name, bank, None)
                        q = top[0]
                        for k, t in ((0, q["t0"]), (1, q["t1"])):
                            ins = dve.tensor_tensor(t[:, :, :], q["oh"][:, :, k, :],
                                                    q["g"][:, :, k:k + 1].to_broadcast((P, 2, E)), ALU.mult)
                        link(ins)
                        dve.tensor_tensor(gates[:, :, :], q["t0"][:, :, :], q["t1"][:, :, :], ALU.add).then_inc(gates_done, 1)
                    elif name.startswith("up"):
                        k = int(name[2:])
                        dve.wait_ge(th_done, th_tally(kind, b, name))
                        link(dve.scalar_tensor_tensor(ga[:, :], th[k % 2][:, :], 1.0, m[:, 0:S], ALU.add, ALU.mult))
                        ins = dve.tensor_tensor(hid[par][:, k, :], ga[:, :], m[:, S:2 * S], ALU.mult)
                        ins.then_inc(free[bank], 1)
                        dve.wait_ge(free[bank], n)
                    elif name.startswith("spread"):
                        j = int(name[6:])
                        bk = bank_of[name]
                        dve.wait_ge(free[bk], bank_tally[bk](kind, b, name))
                        dve.tensor_tensor(hid[par][:, 2 * j:2 * j + 2, :], hid[par][:, 2 * j:2 * j + 2, :],
                                          gate_bc[:, 2 * j:2 * j + 2, :], ALU.mult).then_inc(hid_done, 1)
                    elif name == "shared":
                        bk = bank_of[name]
                        dve.wait_ge(free[bk], bank_tally[bk](kind, b, name))
                        link(dve.tensor_scalar(shared_bc[:, :], shared_th[:, :], 0.25, 0.25, ALU.mult, ALU.add))
                        dve.tensor_tensor(hid[par][:, NK - 2:NK, :], hid[par][:, NK - 2:NK, :],
                                          shared_bc[:, :].unsqueeze(1).to_broadcast((P, 2, S)), ALU.mult).then_inc(hid_done, 1)
                    elif name == "v":
                        dve.tensor_tensor(vv[1 - par][:, :, :], m[:, 0:S].rearrange("p (a d) -> p a d", a=KT),
                                          rview["bv"].unsqueeze(1).to_broadcast((P, KT, D)), ALU.add).then_inc(free[bank], 1)
                    elif name == "out":
                        here = bass.ds((b - 1) * 2, 2)
                        dve.tensor_tensor(x1a[:, :, :], m[:, 0:S].rearrange("p (a d) -> p a d", a=2),
                                          residual[:, here, :], ALU.add).then_inc(free[bank], 1)
                        dve.wait_ge(free[bank], n)
                        link(dve.tensor_tensor(x1[:, :, :], x1a[:, :, :], rview["bout"].unsqueeze(1).to_broadcast((P, 2, D)), ALU.add))
                        dve.tensor_copy(residual[:, here, :], x1[:, :, :])
                        dve.wait_ge(scattered, 64 * (one_tail(kind, b, "x") - 1) + 16)
                        layernorm(lambda i: x1[:, i, :], xn2, xn2_done)
                    elif name == "router1":
                        top_two(kind, b, 1, name, bank, rview["brouter1"])
                        q = top[1]
                        dve.tensor_tensor(chosen[:, :, :], q["oh"][:, :, 0, :], q["oh"][:, :, 1, :], ALU.add).then_inc(chosen_done, 1)
                    elif name == "prefix":
                        q = top[1]
                        link(dve.tensor_tensor(pos[:, :, :], m[:, 0:2 * E].rearrange("p (t e) -> p t e", e=E),
                                               counts[:, :].unsqueeze(1).to_broadcast((P, 2, E)), ALU.add))
                        dve.tensor_tensor(counts[:, :], counts[:, :], m[:, 2 * E:3 * E], ALU.add).then_inc(free[bank], 1)
                        dve.wait_ge(free[bank], n)
                        link(dve.tensor_tensor(posk[:, :, :, :], q["oh"][:, :, :, :],
                                               pos[:, :, :].unsqueeze(2).to_broadcast((P, 2, 2, E)), ALU.mult))
                        link(dve.tensor_reduce(pk[:, :, :], posk[:, :, :, :], AX.X, ALU.add))
                        link(dve.tensor_scalar(kept[:, :, :], pk[:, :, :], float(cap), None, ALU.is_lt))
                        link(dve.scalar_tensor_tensor(slot[:, :, :], q["idx"][:, :, :], float(cap), pk[:, :, :], ALU.mult, ALU.add))
                        link(dve.tensor_tensor(sk[:, :, :], slot[:, :, :], kept[:, :, :], ALU.mult))
                        dve.tensor_copy(slot_ids[:, bass.ds((b - 1) * 2, 2), :], sk[:, :, :])
                        link(dve.tensor_tensor(dumpk[:, :, :], dump_at[:, :, :], kept[:, :, :], ALU.mult))
                        link(dve.tensor_tensor(dumpk[:, :, :], dump_at[:, :, :], dumpk[:, :, :], ALU.subtract))
                        dve.tensor_scalar(dump_at[:, :, :], dump_at[:, :, :], float(S), None, ALU.add).then_inc(slots_done, 1)
                        link(dve.tensor_tensor(gk[:, :, :], q["g"][:, :, :], kept[:, :, :], ALU.mult))
                        link(dve.tensor_tensor(gden[:, :], gk[:, :, 0], gk[:, :, 1], ALU.add))
                        link(dve.tensor_scalar(gden[:, :], gden[:, :], 1e-9, None, ALU.add))
                        link(dve.reciprocal(gden[:, :], gden[:, :]))
                        link(dve.tensor_tensor(slot_w[:, bass.ds((b - 1) * 2, 2), :], gk[:, :, :],
                                               gden[:, :].unsqueeze(2).to_broadcast((P, 2, 2)), ALU.mult))

                def body(kind, b, par):
                    t0 = dve.snap(b * NS) if kind == "mid" else b * NS
                    if kind != "pro":
                        dve.sem_clear(chain)
                        links[0] = 0
                    if kind == "pro":
                        dve.wait_ge(x_first, 16)
                    if kind == "last" or (kind == "mid" and par == 1):
                        dve.wait_ge(x_rest, XREST)
                        dve.wait_ge(zeroed, NZERO)
                    for s in steps(kind):
                        if s:
                            for name in jobs(kind, s - 1):
                                handle(kind, b, par, name)
                        if present(kind, s, 0):
                            dve.wait_ge(scored, t0 + s + 1)
                            dve.tensor_reduce(nmax[s % 4][:, :], S_ps[s % 2][:, :].rearrange("p (g k) -> p g k", g=GS),
                                              AX.X, ALU.max, negate=True).then_inc(maxed, 1)
                        if present(kind, s, 1) and not (kind == "end" and s >= 1):
                            r = (s - 1) % 4
                            dve.wait_ge(exped, t0 + s)
                            link(dve.reciprocal(rinv[r][:, :], rsum[r][:, :]))
                            dve.tensor_tensor(pick[r][:, :, :], cview["pick_query"].unsqueeze(1).to_broadcast((P, GS, QG)),
                                              rinv[r][:, :].unsqueeze(2).to_broadcast((P, GS, QG)), ALU.mult).then_inc(picked, 1)
                        if present(kind, s, 2) and not (kind == "end" and s >= 2):
                            o = O_ps[:, 0:GS * OW].rearrange("p (g w) -> p g w", g=GS)
                            dve.wait_ge(valued, t0 + s - 1)
                            link(dve.tensor_tensor(rel_m[s % 2][:, :, :, :],
                                                   o[:, :, D:OW].rearrange("p g (q c) -> p g q c", c=C),
                                                   cview["mask_query"].unsqueeze(1).unsqueeze(3).to_broadcast((P, GS, QG, C)),
                                                   ALU.mult))
                            link(dve.tensor_reduce(rel_s[s % 2][:, :, :],
                                                   rel_m[s % 2][:, :, :, :].rearrange("p g q c -> p g c q"), AX.X, ALU.add))
                            dve.tensor_tensor(z1[s % 2][:, :, :].rearrange("p g (h c) -> p g h c", c=C),
                                              o[:, :, 0:D].rearrange("p g (h c) -> p g h c", c=C),
                                              rel_s[s % 2][:, :, :].unsqueeze(2).to_broadcast((P, GS, H, C)),
                                              ALU.add).then_inc(merged, 1)
                        if s == 0 and "front" in SECTIONS[kind]:
                            layernorm(lambda i: residual[:, bass.ds((b + 1) * 2 + i, 1), :].rearrange("p a d -> p (a d)"), xn, xn_done)
                bodies(dve, nb, body)

            @block.tensor
            def _(pe):
                pe.wait_ge(load_sem, LOADS)
                pe.wait_ge(dve_ready, 1)

                def project(kind, b, par, name):
                    bank = bank_of[name]
                    tally = bank_tally[bank]
                    m, n = M_ps[bank], tally(kind, b, name)
                    if not (isinstance(n, int) and n == 1):
                        pe.wait_ge(free[bank], n - 1)
                    w = wview

                    def moved_by(job):
                        pe.wait_ge(free[bank_of[job]], bank_tally[bank_of[job]](kind, b, job))

                    def mm(out, lhsT, rhs, start=True, stop=True):
                        return pe.matmul(out, lhsT, rhs, start=start, stop=stop)
                    if name == "router0":
                        for i in range(2):
                            ins = mm(m[:, i * E:(i + 1) * E], xnT[par][:, i * P:(i + 1) * P], w["wrouter0"])
                    elif name.startswith("up"):
                        k = int(name[2:])
                        mm(m[:, 0:S], w["wgate"][:, k * P:(k + 1) * P], xnT[par][:, :])
                        ins = mm(m[:, S:2 * S], w["wup"][:, k * P:(k + 1) * P], xnT[par][:, :])
                    elif name == "gateT":
                        pe.wait_ge(gates_done, one_mid(kind, b, "x"))
                        for i in range(2):
                            ins = pe.transpose(m[0:E, i * P:(i + 1) * P], gates[:, i, :], ident)
                    elif name.startswith("spread"):
                        j = int(name[6:])
                        if j == 0:
                            moved_by("gateT")
                        for i in range(2):
                            k = 2 * j + i
                            ins = mm(m[:, i * S:(i + 1) * S], spread[:, k * P:(k + 1) * P], gatesT[:, :])
                    elif name == "shared":
                        ins = mm(m[:, 0:S], wshared[:, :], xnT[par][:, :])
                    elif name == "xnT":
                        pe.wait_ge(xn_done, one_front(kind, b, "x"))
                        for i in range(2):
                            ins = pe.transpose(m[:, i * P:(i + 1) * P], xn[:, i, :], ident)
                    elif name == "xn2T":
                        pe.wait_ge(xn2_done, one_tail(kind, b, "x"))
                        for i in range(2):
                            ins = pe.transpose(m[:, i * P:(i + 1) * P], xn2[:, i, :], ident)
                    elif name == "qk":
                        moved_by("xnT")
                        mm(m[:, 0:S], w["wqkv"][:, 0:D], xnT[1 - par][:, :])
                        ins = mm(m[:, S:2 * S], w["wqkv"][:, D:2 * D], xnT[1 - par][:, :])
                    elif name == "v":
                        for i in range(KT):
                            ins = mm(m[:, i * D:(i + 1) * D], xnT[1 - par][:, i * P:(i + 1) * P], w["wqkv"][:, 2 * D:3 * D])
                    elif name.startswith("rep"):
                        j = int(name[3:])
                        for i in range(2):
                            ins = mm(m[:, i * S:(i + 1) * S], wq_rep[:, 2 * j + i, :], xnT[1 - par][:, :])
                    elif name == "out":
                        pe.wait_ge(ctx_moved, one_tail(kind, b, "x"))
                        nh = spr_tally("mid", 1, "shared") - spr_tally("first", 0, "shared")
                        pe.wait_ge(hid_done, nh * b)
                        for i in range(2):
                            o = m[:, i * D:(i + 1) * D]
                            mm(o, ctxT[:, i * P:(i + 1) * P], w["wout"], stop=False)
                            for k in range(NK):
                                ins = mm(o, hid[1 - par][:, k, i * P:(i + 1) * P], w["wdown"][:, k * D:(k + 1) * D],
                                         start=False, stop=(k == NK - 1))
                    elif name == "router1":
                        moved_by("xn2T")
                        for i in range(2):
                            ins = mm(m[:, i * E:(i + 1) * E], xn2T[:, i * P:(i + 1) * P], w["wrouter1"])
                    elif name == "prefix":
                        pe.wait_ge(chosen_done, one_tail(kind, b, "x"))
                        before, every = tri[:, 0:P], tri[:, P:2 * P]
                        mm(m[:, 0:E], before, chosen[:, 0, :])
                        mm(m[:, E:2 * E], before, chosen[:, 1, :], stop=False)
                        mm(m[:, E:2 * E], every, chosen[:, 0, :], start=False)
                        mm(m[:, 2 * E:3 * E], every, chosen[:, 0, :], stop=False)
                        ins = mm(m[:, 2 * E:3 * E], every, chosen[:, 1, :], start=False)
                    ins.then_inc(full[bank], 1)

                def body(kind, b, par):
                    t0 = pe.snap(b * NS) if kind == "mid" else b * NS
                    for s in steps(kind):
                        if present(kind, s, 0):
                            pe.wait_ge(built, t0 + s + 1)
                            if not (kind == "first" and s < 2):
                                pe.wait_ge(exped, t0 + s - 1)
                            for g in range(GS):
                                o = S_ps[s % 2][:, g * S:(g + 1) * S]
                                G = GS * s + g
                                off = S - QG - QG * G
                                pe.matmul(o, q_blk[s % 2][:, g, :], kT[par][:, :], start=True, stop=False)
                                ins = pe.matmul(o, q_rel[s % 2][:, g, :], rel_k[:, off:off + S], start=False, stop=True)
                            ins.then_inc(scored, 1)
                        if present(kind, s, 1) and not (kind == "end" and s >= 1):
                            r = (s - 1) % 2
                            pe.wait_ge(exped, t0 + s)
                            if not (kind == "first" and s < 3):
                                pe.wait_ge(moved, t0 + s - 2)
                            for kt in range(KT):
                                for g in range(GS):
                                    ins = pe.transpose(PT_ps[r][:, (kt * GS + g) * P:(kt * GS + g + 1) * P],
                                                       probs[r][:, g, kt * P:(kt + 1) * P], ident)
                            ins.then_inc(turned, 1)
                        if present(kind, s, 2) and not (kind == "end" and s >= 2):
                            r, sq = s % 2, (s - 2) % NS
                            vp = vv[par if s >= 2 else 1 - par]
                            if s == 2:
                                pk_ = {"first": ("pro", -1), "mid": ("mid", b - 1), "last": ("mid", b - 1)}[kind]
                                if kind == "mid" and par == 1:
                                    bank = bank_of["v"]
                                    tl = bank_tally[bank]
                                    pe.wait_ge(free[bank], tl("mid", b, "v") - tl.total("mid"))
                                else:
                                    pe.wait_ge(free[bank_of["v"]], bank_tally[bank_of["v"]](pk_[0], pk_[1], "v"))
                            pe.wait_ge(moved, t0 + s - 1)
                            if not (kind == "first" and s < 3):
                                pe.wait_ge(merged, t0 + s - 2)
                            for g in range(GS):
                                G = GS * sq + g
                                for kt in range(KT):
                                    pe.matmul(O_ps[:, g * OW:g * OW + D], probsT[r][:, kt, g, :], vp[:, kt, :],
                                              start=(kt == 0), stop=(kt == KT - 1))
                                for kt in range(KT):
                                    off = S - QG + kt * P - QG * G
                                    ins = pe.matmul(O_ps[:, g * OW + D:(g + 1) * OW], probsT[r][:, kt, g, :],
                                                    rel_v[:, off:off + QG, :].rearrange("p q c -> p (q c)"),
                                                    start=(kt == 0), stop=(kt == KT - 1))
                            ins.then_inc(valued, 1)
                        for name in jobs(kind, s):
                            project(kind, b, par, name)
                        if present(kind, s, 3) and not (kind == "end" and s >= 3):
                            sq = (s - 3) % NS
                            pe.wait_ge(picked, t0 + s - 2)
                            pe.wait_ge(masked, t0 + s - 2)
                            if s == 3 and "tail" in SECTIONS[kind]:
                                pe.wait_ge(ctx_moved, one_tail(kind, b, "x"))
                            for g in range(GS):
                                G = GS * sq + g
                                ins = pe.matmul(CTX_ps[:, QG * G:QG * G + QG], zz[(s - 3) % 2][:, g, :],
                                                pick[(s - 3) % 4][:, g, :], start=True, stop=True)
                            ins.then_inc(ctxed, 1)
                bodies(pe, nb, body)

        with ExitStack() as pb:
            def sbb(name, shape, dt=F32):
                return pb.enter_context(nc.sbuf_tensor(name, shape, dt))

            def bank_b(name):
                return pb.enter_context(nc.psum_tensor(name, [P, 512], F32))

            S_ps = [bank_b(f"scores1_{i}") for i in range(2)]
            PT_ps = [bank_b(f"probsT1_{i}") for i in range(2)]
            O_ps = bank_b("values1")
            CTX_ps = bank_b("context1")
            M_ps = [bank_b(f"spare1_{i}") for i in range(2)]
            xt = [sbb(f"xt1_{i}", [P, S]) for i in range(2)]
            qT = [sbb(f"qT1_{i}", [P, S]) for i in range(2)]
            kT = [sbb(f"kT1_{i}", [P, S]) for i in range(2)]
            vv = [sbb(f"v1_{i}", [P, KT, D]) for i in range(2)]
            q_blk = [sbb(f"q_blk1_{i}", [P, GS, P]) for i in range(2)]
            probs = [sbb(f"probs1_{i}", [P, GS, S]) for i in range(2)]
            probsT = [sbb(f"probsT1_s{i}", [P, KT, GS, P]) for i in range(2)]
            nmax = [sbb(f"nmax1_{i}", [P, GS]) for i in range(4)]
            rsum = [sbb(f"rsum1_{i}", [P, GS]) for i in range(4)]
            rinv = [sbb(f"rinv1_{i}", [P, GS]) for i in range(4)]
            pick = [sbb(f"pick1_{i}", [P, GS, QG]) for i in range(4)]
            zz = [sbb(f"zz1_{i}", [P, GS, D]) for i in range(2)]
            ctxT = sbb("ctxT1", [P, S])
            bsem = {n: pb.enter_context(nc.semaphore(n + "_b")) for n in
                    ("built", "scored", "maxed", "exped", "turned", "moved", "valued", "picked", "merged",
                     "ctxed", "ctx_moved", "full0", "full1", "free0", "free1", "xt_done", "chain")}
            (built, scored, maxed, exped, turned, moved, valued, picked, merged, ctxed, ctx_moved, full0, full1,
             free0, free1, xt_done, chain) = bsem.values()
            full, free = [full0, full1], [free0, free1]
            bank_of = {name: i % 2 for i, (_, name, _) in enumerate(JOBS_B)}
            bank_tally = [Tally(nb, [(n, s) for _, n, s in JOBS_B if bank_of[n] == i]) for i in range(2)]
            one_front = Tally(nb, [("x", "front")])
            one_tail = Tally(nb, [("x", "tail")])

            def jobs(kind, step):
                return [n for s, n, sec in JOBS_B if s == step and sec in SECTIONS[kind]]

            def present(kind, s, lag):
                return kind in (("first", "mid", "last") if s >= lag else ("mid", "last", "end"))

            def ktiles(s):
                return (GS * QG * (s % NS + 1) - 1) // P + 1

            block = pb.enter_context(nc.Block())

            @block.gpsimd
            def _(pool):
                def build(s, par):
                    pool.tensor_tensor(q_blk[s % 2][:, :, :].rearrange("p g (q h) -> p (g q) h", h=H),
                                       qT[par][:, 16 * s:16 * s + 16].unsqueeze(2).to_broadcast((P, 16, H)),
                                       cview["mask_head_rows"].unsqueeze(1).to_broadcast((P, 16, H)), ALU.mult).then_inc(built, 1)

                def body(kind, b, par):
                    t0 = pool.snap(b * NS) if kind == "mid" else b * NS
                    if kind == "pro":
                        pool.tensor_copy(xt[0][:, :], xnT1[:, 0:S]).then_inc(xt_done, 1)
                        pool.wait_ge(free[bank_of["qk"]], bank_tally[bank_of["qk"]](kind, b, "qk"))
                        build(0, 0)
                        return
                    if kind == "end":
                        return
                    for s in range(NS):
                        if s == 3 and "front" in SECTIONS[kind]:
                            pool.tensor_copy(xt[1 - par][:, :], xnT1[:, bass.ds((b + 1) * S, S)]).then_inc(xt_done, 1)
                        if not (kind == "last" and s == NS - 1):
                            if s == NS - 1:
                                pool.wait_ge(free[bank_of["qk"]], bank_tally[bank_of["qk"]](kind, b, "qk"))
                            if not (kind == "first" and s == 0):
                                pool.wait_ge(scored, t0 + s)
                            build((s + 1) % NS, par if s < NS - 1 else 1 - par)
                bodies(pool, nb, body)

            @block.scalar
            def _(act):
                def move(kind, b, par, name):
                    bank = bank_of[name]
                    m, n = M_ps[bank], bank_tally[bank](kind, b, name)
                    if name == "qk":
                        act.wait_ge(full[bank], n)
                        act.mul(qT[1 - par][:, :], m[:, 0:S], C ** -0.5)
                        act.copy(kT[1 - par][:, :], m[:, S:2 * S]).then_inc(free[bank], 1)
                    elif name == "v":
                        act.wait_ge(full[bank], n)
                        act.copy(vv[1 - par][:, :, :].rearrange("p a d -> p (a d)"), m[:, 0:S]).then_inc(free[bank], 1)

                def body(kind, b, par):
                    t0 = act.snap(b * NS) if kind == "mid" else b * NS
                    for s in range(NS):
                        if s:
                            for name in jobs(kind, s - 1):
                                move(kind, b, par, name)
                        if s == 3 and "tail" in SECTIONS[kind]:
                            act.wait_ge(ctxed, t0)
                            act.copy(ctxT[:, :], CTX_ps[:, 0:S]).then_inc(ctx_moved, 1)
                        if present(kind, s, 0):
                            w = ktiles(s) * P
                            act.wait_ge(maxed, t0 + s + 1)
                            for g in range(GS):
                                ins = act.activation(probs[s % 2][:, g, 0:w], S_ps[s % 2][:, g * w:(g + 1) * w], ACT.Exp,
                                                     bias=nmax[s % 4][:, g:g + 1], accum_out=rsum[s % 4][:, g:g + 1])
                            ins.then_inc(exped, 1)
                        if present(kind, s, 1) and not (kind == "end" and s >= 1):
                            w = ktiles(s - 1) * GS * P
                            act.wait_ge(turned, t0 + s)
                            act.copy(probsT[(s - 1) % 2][:, :, :, :].rearrange("p a b c -> p (a b c)")[:, 0:w],
                                     PT_ps[(s - 1) % 2][:, 0:w]).then_inc(moved, 1)
                bodies(act, nb, body)

            @block.vector
            def _(dve):
                links = [0]

                def link(ins):
                    links[0] += 1
                    ins.then_inc(chain, 1)
                    dve.wait_ge(chain, links[0])

                def body(kind, b, par):
                    t0 = dve.snap(b * NS) if kind == "mid" else b * NS
                    dve.sem_clear(chain)
                    links[0] = 0
                    for s in range(NS):
                        if present(kind, s, 0):
                            w = ktiles(s) * P
                            dve.wait_ge(scored, t0 + s + 1)
                            dve.tensor_reduce(nmax[s % 4][:, :], S_ps[s % 2][:, 0:GS * w].rearrange("p (g k) -> p g k", g=GS),
                                              AX.X, ALU.max, negate=True).then_inc(maxed, 1)
                        if present(kind, s, 1) and not (kind == "end" and s >= 1):
                            r = (s - 1) % 4
                            dve.wait_ge(exped, t0 + s)
                            link(dve.reciprocal(rinv[r][:, :], rsum[r][:, :]))
                            dve.tensor_tensor(pick[r][:, :, :], cview["pick_query"].unsqueeze(1).to_broadcast((P, GS, QG)),
                                              rinv[r][:, :].unsqueeze(2).to_broadcast((P, GS, QG)), ALU.mult).then_inc(picked, 1)
                        if present(kind, s, 2) and not (kind == "end" and s >= 2):
                            dve.wait_ge(valued, t0 + s - 1)
                            dve.tensor_tensor(zz[s % 2][:, :, :].rearrange("p g (h c) -> p g h c", c=C),
                                              O_ps[:, 0:GS * D].rearrange("p (g h c) -> p g h c", g=GS, c=C),
                                              cview["mask_head"].unsqueeze(1).unsqueeze(3).to_broadcast((P, GS, H, C)),
                                              ALU.mult).then_inc(merged, 1)
                        if s and "out" in jobs(kind, s - 1):
                            bank = bank_of["out"]
                            here = bass.ds((b - 1) * 2, 2)
                            dve.wait_ge(full[bank], bank_tally[bank](kind, b, "out"))
                            dve.tensor_tensor(residual[:, here, :], M_ps[bank][:, 0:S].rearrange("p (a d) -> p a d", a=2),
                                              residual[:, here, :], ALU.add).then_inc(free[bank], 1)
                bodies(dve, nb, body)

            @block.tensor
            def _(pe):
                def project(kind, b, par, name):
                    bank = bank_of[name]
                    m, n = M_ps[bank], bank_tally[bank](kind, b, name)
                    if not (isinstance(n, int) and n == 1):
                        pe.wait_ge(free[bank], n - 1)
                    if name == "qk":
                        pe.wait_ge(xt_done, one_front(kind, b, "x"))
                        pe.matmul(m[:, 0:S], wview["q1"], xt[1 - par][:, :], start=True, stop=True)
                        ins = pe.matmul(m[:, S:2 * S], wview["k1"], xt[1 - par][:, :], start=True, stop=True)
                    elif name == "v":
                        for i in range(KT):
                            ins = pe.matmul(m[:, i * D:(i + 1) * D], xt[1 - par][:, i * P:(i + 1) * P], wview["v1"],
                                            start=True, stop=True)
                    elif name == "out":
                        pe.wait_ge(ctx_moved, one_tail(kind, b, "x"))
                        for i in range(2):
                            ins = pe.matmul(m[:, i * D:(i + 1) * D], ctxT[:, i * P:(i + 1) * P], wview["o1"],
                                            start=True, stop=True)
                    ins.then_inc(full[bank], 1)

                def body(kind, b, par):
                    t0 = pe.snap(b * NS) if kind == "mid" else b * NS
                    for s in range(NS):
                        if present(kind, s, 0):
                            w = ktiles(s) * P
                            pe.wait_ge(built, t0 + s + 1)
                            if not (kind == "first" and s < 2):
                                pe.wait_ge(exped, t0 + s - 1)
                            for g in range(GS):
                                o = S_ps[s % 2][:, g * w:(g + 1) * w]
                                off = S - QG - QG * (GS * s + g)
                                pe.matmul(o, q_blk[s % 2][:, g, :], kT[par][:, 0:w], start=True, stop=False)
                                ins = pe.matmul(o, alibi_l[:, :], alibi_r[:, off:off + w], start=False, stop=True)
                            ins.then_inc(scored, 1)
                        if present(kind, s, 1) and not (kind == "end" and s >= 1):
                            r = (s - 1) % 2
                            pe.wait_ge(exped, t0 + s)
                            if not (kind == "first" and s < 3):
                                pe.wait_ge(moved, t0 + s - 2)
                            for kt in range(ktiles(s - 1)):
                                for g in range(GS):
                                    ins = pe.transpose(PT_ps[r][:, (kt * GS + g) * P:(kt * GS + g + 1) * P],
                                                       probs[r][:, g, kt * P:(kt + 1) * P], ident)
                            ins.then_inc(turned, 1)
                        if present(kind, s, 2) and not (kind == "end" and s >= 2):
                            r, n = s % 2, ktiles(s - 2)
                            vp = vv[par if s >= 2 else 1 - par]
                            if s == 2:
                                bank = bank_of["v"]
                                tl = bank_tally[bank]
                                if kind == "first":
                                    pe.wait_ge(free[bank], tl("pro", -1, "v"))
                                elif kind == "last":
                                    pe.wait_ge(free[bank], tl("mid", b - 1, "v"))
                                else:
                                    pe.wait_ge(free[bank], tl("mid", b, "v") - tl.total("mid"))
                            pe.wait_ge(moved, t0 + s - 1)
                            if not (kind == "first" and s < 3):
                                pe.wait_ge(merged, t0 + s - 2)
                            for g in range(GS):
                                for kt in range(n):
                                    ins = pe.matmul(O_ps[:, g * D:(g + 1) * D], probsT[r][:, kt, g, :], vp[:, kt, :],
                                                    start=(kt == 0), stop=(kt == n - 1))
                            ins.then_inc(valued, 1)
                        for name in jobs(kind, s):
                            project(kind, b, par, name)
                        if present(kind, s, 3) and not (kind == "end" and s >= 3):
                            sq = (s - 3) % NS
                            pe.wait_ge(picked, t0 + s - 2)
                            pe.wait_ge(merged, t0 + s - 2)
                            if s == 3 and "tail" in SECTIONS[kind]:
                                pe.wait_ge(ctx_moved, one_tail(kind, b, "x"))
                            for g in range(GS):
                                G = GS * sq + g
                                ins = pe.matmul(CTX_ps[:, QG * G:QG * G + QG], zz[(s - 3) % 2][:, g, :],
                                                pick[(s - 3) % 4][:, g, :], start=True, stop=True)
                            ins.then_inc(ctxed, 1)
                bodies(pe, nb, body)

        with ExitStack() as pc:
            def sc(name, shape, dt=F32):
                return pc.enter_context(nc.sbuf_tensor(name, shape, dt))

            def bank_c(name):
                return pc.enter_context(nc.psum_tensor(name, [P, 512], F32))

            T_ps = [bank_c(f"slotsT{i}") for i in range(2)]
            U_ps = [bank_c(f"up_{i}") for i in range(4)]
            Y_ps = [bank_c(f"down{i}") for i in range(2)]
            FT = FF // P
            b2 = sc("b2", [P, E, D])
            b1e = [sc(f"b1e{i}", [P, FT]) for i in range(2)]
            b1_moved = pc.enter_context(nc.semaphore("b1_moved"))
            xe = [sc(f"xe{i}", [P, JT, D]) for i in range(2)]
            w1 = [sc(f"w1_{i}", [P, FF]) for i in range(2)]
            w2 = [sc(f"w2_{i}", [P, FT, D]) for i in range(2)]
            xeT = sc("xeT", [P, cap])
            he = sc("he", [P, FT, cap])
            ye = [sc(f"ye{i}", [P, JT, D]) for i in range(2)]
            csem = {n: pc.enter_context(nc.semaphore(n + "_c")) for n in
                    ("b2_in", "in0", "in1", "out0", "out1", "tr", "tr_moved", "up", "gelu", "down", "y_moved")}
            b2_in, in0, in1, out0, out1, tr, tr_moved, up, gelu, down, y_moved = csem.values()
            loaded, stored = [in0, in1], [out0, out1]
            QT = [(j, min(4, JT - j)) for j in range(0, JT, 4)]
            NQ = len(QT)

            with nc.Block() as block:
                def experts(engine, body):
                    body(0, 0, True)
                    body(1, 1, True)
                    with engine.Fori(1, E // 2) as pair:
                        e = engine.snap(pair * 2)
                        body(e, 0, False)
                        body(e + 1, 1, False)

                packed_t = packed[0:SLOTS, :].rearrange("(e p j) d -> e p j d", p=P, j=JT)
                out_t = expert_out.rearrange("(e p j) d -> e p j d", p=P, j=JT)

                @block.sync
                def _(sp):
                    sp.dma_start(b2[:, :, :].rearrange("p e d -> p (e d)"), io["b2"].partition_broadcast(P)).then_inc(b2_in, 16)

                    def body(e, i, first):
                        if not first:
                            sp.wait_ge(down, (e - 1) * NQ)
                        sp.dma_start(xe[i][:, :, :], packed_t[bass.ds(e, 1)].rearrange("a p j d -> p (a j) d")).then_inc(loaded[i], 16)
                        sp.dma_start(w1[i][:, :], io["w1"][bass.ds(e, 1)].rearrange("a p f -> p (a f)")).then_inc(loaded[i], 16)
                        sp.dma_start(w2[i][:, :, :], io["w2"][bass.ds(e, 1)].rearrange("a (m p) d -> p (a m) d", p=P)).then_inc(loaded[i], 16)
                    experts(sp, body)

                @block.tensor
                def _(pe):
                    def body(e, i, first):
                        pe.wait_ge(loaded[i], 48 if first else e * 24 + (48 if i == 0 else 24))
                        for q, (j0, n) in enumerate(QT):
                            if not (first and i == 0 and q < 2):
                                pe.wait_ge(tr_moved, e * NQ + q - 1)
                            for j in range(n):
                                ins = pe.transpose(T_ps[(i * NQ + q) % 2][:, j * P:(j + 1) * P], xe[i][:, j0 + j, :], ident)
                            ins.then_inc(tr, 1)
                        for q, (j0, n) in enumerate(QT):
                            pe.wait_ge(tr_moved, e * NQ + q + 1)
                            for f in range(FT):
                                if not (first and i == 0 and q == 0):
                                    pe.wait_ge(gelu, (e * NQ + q) * FT + f - FT + 1)
                                pe.matmul(U_ps[f][:, 0:n * P], w1[i][:, f * P:(f + 1) * P], xeT[:, j0 * P:(j0 + n) * P],
                                          start=True, stop=True).then_inc(up, 1)
                        for q, (j0, n) in enumerate(QT):
                            pe.wait_ge(gelu, (e * NQ + q + 1) * FT)
                            if not (first and i == 0 and q < 2):
                                pe.wait_ge(y_moved, e * NQ + q - 1)
                            for j in range(n):
                                for f in range(FT):
                                    ins = pe.matmul(Y_ps[(i * NQ + q) % 2][:, j * D:(j + 1) * D],
                                                    he[:, f, (j0 + j) * P:(j0 + j + 1) * P], w2[i][:, f, :],
                                                    start=(f == 0), stop=(f == FT - 1))
                            ins.then_inc(down, 1)
                    experts(pe, body)

                @block.scalar
                def _(act):
                    def body(e, i, first):
                        for q, (j0, n) in enumerate(QT):
                            for f in range(FT):
                                act.wait_ge(up, (e * NQ + q) * FT + f + 1)
                                if q == 0 and f == 0 and not (first and i == 0):
                                    act.wait_ge(down, e * NQ)
                                act.activation(he[:, f, j0 * P:(j0 + n) * P], U_ps[f][:, 0:n * P], ACT.Gelu,
                                               bias=b1e[i][:, f:f + 1]).then_inc(gelu, 1)
                    b1v = wview["b1"].rearrange("p (e f) -> p e f", f=FT)

                    def with_bias(e, i, first):
                        act.copy(b1e[i][:, :], b1v[:, bass.ds(e, 1), :].rearrange("p a f -> p (a f)")).then_inc(b1_moved, 1)
                        act.wait_ge(b1_moved, e + 1)
                        body(e, i, first)
                    experts(act, with_bias)

                @block.vector
                def _(dve):
                    dve.wait_ge(b2_in, 16)

                    def body(e, i, first):
                        for q, (j0, n) in enumerate(QT):
                            dve.wait_ge(tr, e * NQ + q + 1)
                            if q == 0 and not (first and i == 0):
                                dve.wait_ge(up, e * NQ * FT)
                            dve.tensor_copy(xeT[:, j0 * P:(j0 + n) * P], T_ps[(i * NQ + q) % 2][:, 0:n * P]).then_inc(tr_moved, 1)
                        for q, (j0, n) in enumerate(QT):
                            dve.wait_ge(down, e * NQ + q + 1)
                            if q == 0 and not first:
                                dve.wait_ge(stored[i], e * 8 if i == 0 else (e - 1) * 8)
                            dve.tensor_tensor(ye[i][:, j0:j0 + n, :], Y_ps[(i * NQ + q) % 2][:, 0:n * D].rearrange("p (j d) -> p j d", d=D),
                                              b2[:, bass.ds(e, 1), :].to_broadcast((P, n, D)), ALU.add).then_inc(y_moved, 1)
                    experts(dve, body)

                @block.gpsimd
                def _(pool):
                    def body(e, i, first):
                        pool.wait_ge(y_moved, (e + 1) * NQ)
                        pool.dma_start(out_t[bass.ds(e, 1)].rearrange("a p j d -> p (a j) d"), ye[i][:, :, :]).then_inc(stored[i], 16)
                    experts(pool, body)
                    for i in range(2):
                        pool.wait_ge(stored[i], 16 * (E // 2))

            NR = 4
            rows0 = [sc(f"rows0_{i}", [P, D]) for i in range(NR)]
            rows1 = [sc(f"rows1_{i}", [P, D]) for i in range(NR)]
            part = [sc(f"part_{i}", [P, D]) for i in range(NR)]
            total = [sc(f"total_{i}", [P, D]) for i in range(NR)]
            idc = [sc(f"idc_{i}", [P, 2], U32) for i in range(NR)]
            gathered = [pc.enter_context(nc.semaphore(f"gathered{i}")) for i in range(NR)]
            written = [pc.enter_context(nc.semaphore(f"written{i}")) for i in range(NR)]
            first_sum = pc.enter_context(nc.semaphore("first_sum"))
            summed = pc.enter_context(nc.semaphore("summed"))
            ids_at = pc.enter_context(nc.semaphore("ids_at"))
            with nc.Block() as block:
                def tiles(engine, body):
                    for i in range(NR):
                        body(i, i, True)
                    with engine.Fori(1, NT // NR) as turn:
                        t = engine.snap(turn * NR)
                        for i in range(NR):
                            body(t + i, i, False)

                @block.gpsimd
                def _(pool):
                    def body(t, i, first):
                        pool.sem_clear(ids_at)
                        if not first:
                            pool.wait_ge(summed, t - NR + 1)
                        pool.tensor_copy(idc[i][:, :], slot_ids[:, bass.ds(t, 1), :].rearrange("p a k -> p (a k)")).then_inc(ids_at, 1)
                        pool.wait_ge(ids_at, 1)
                        for k, r in enumerate((rows0, rows1)):
                            pool.indirect_dma_start(out=r[i][:, :], out_offset=None, in_=expert_out,
                                                    in_offset=bass.IndirectOffsetOnAxis(ap=idc[i][:, k:k + 1], axis=0)).then_inc(gathered[i], 16)
                    tiles(pool, body)

                @block.vector
                def _(dve):
                    def body(t, i, first):
                        dve.wait_ge(gathered[i], 32 if first else (t - i) * (32 // NR) + 32)
                        if not first:
                            dve.wait_ge(written[i], (t - i) * (16 // NR))
                        w = slot_w[:, bass.ds(t, 1), :].rearrange("p a k -> p (a k)")
                        dve.scalar_tensor_tensor(part[i][:, :], rows0[i][:, :], w[:, 0:1],
                                                 residual[:, bass.ds(t, 1), :].rearrange("p a d -> p (a d)"),
                                                 ALU.mult, ALU.add).then_inc(first_sum, 1)
                        dve.wait_ge(first_sum, t + 1)
                        dve.scalar_tensor_tensor(total[i][:, :], rows1[i][:, :], w[:, 1:2], part[i][:, :],
                                                 ALU.mult, ALU.add).then_inc(summed, 1)
                    tiles(dve, body)

                @block.sync
                def _(sp):
                    def body(t, i, first):
                        sp.wait_ge(summed, t + 1)
                        sp.dma_start(io["out"][bass.ds(t * P, P), :], total[i][:, :]).then_inc(written[i], 16)
                    tiles(sp, body)
                    for i in range(NR):
                        sp.wait_ge(written[i], 16 * (NT // NR))


def shape_constants(nb, cap):
    T = nb * S
    p = np.arange(P)
    c = {
        "ident": np.eye(P),
        "mask_head_rows": p[:, None] // C == np.arange(H),
        "mask_rep": ((p[:, None, None] // (QG * C) == np.arange(2)[None, None, :])
                     & (p[:, None, None] // C % QG == np.arange(2 * QG)[None, :, None] % QG)).reshape(P, -1),
        "mask_head": p[:, None] % H == np.arange(H),
        "mask_query": p[:, None] // H == QG - 1 - np.arange(QG),
        "pick_query": p[:, None] // H == np.arange(QG),
        "iota": np.broadcast_to(np.arange(E), (P, E)),
        "dump": (E * cap + p[:, None, None] + P * np.arange(2)[None, :, None] + T * np.arange(2)[None, None, :]).reshape(P, 4),
    }
    consts = np.concatenate([np.asarray(c[n], np.float32) for n in CONSTS], axis=1)
    spread = 0.5 * (np.arange(E * HID)[None, :] // HID == np.arange(E)[:, None])
    tri = np.concatenate([p[:, None] < p[None, :], np.ones((P, P))], axis=1)
    ratio = 2.0 ** (-8.0 / H)
    slopes = np.asarray([ratio ** (i + 1) for i in range(H)], np.float32)
    parts, rest = [], slopes.astype(np.float64)
    for _ in range(3):
        part = (rest.astype(np.float32).view(np.uint32) & np.uint32(0xFFFF0000)).view(np.float32).astype(np.float64)
        parts.append(part)
        rest = rest - part
    own = np.arange(QG)[:, None] == p[None, :] // H
    alibi_l = np.concatenate([own * np.tile(part, QG)[None, :] for part in parts], axis=0)
    j = np.arange(2 * S - QG)
    dist = j[None, :] - (S - QG) - np.arange(QG)[:, None]
    alibi_r = np.tile(np.where(dist <= 0, dist, -1e30), (3, 1))
    named = {"consts": consts, "spread": spread, "tri": tri, "alibi_l": alibi_l, "alibi_r": alibi_r}
    return {n: v.astype(np.float32) for n, v in named.items()}


def capacity(tokens):
    return max(1, int(math.ceil(1.25 * tokens * 2 / E)))


def kernel(**inputs):
    import concourse.bacc as bacc
    from concourse.bass_utils import run_bass_kernel_spmd

    a = {k: np.asarray(v) for k, v in inputs.items()}
    nb = a["L0_attn_x"].shape[0]
    T = nb * S
    cap = capacity(T)
    wqkv, bqkv = a["L0_attn_W_qkv"], a["L0_attn_b_qkv"]
    heads = bqkv[0:D].reshape(H // 2, 2, 1, C)
    w = {
        "wqkv": wqkv,
        "wout": a["L0_attn_W_out"],
        "wgate": np.concatenate([a["L0_ffn_We_gate"].reshape(E * HID, D), a["L0_ffn_Ws_gate"]], axis=0).T,
        "wup": np.concatenate([a["L0_ffn_We_up"].reshape(E * HID, D), a["L0_ffn_Ws_up"]], axis=0).T,
        "wdown": np.concatenate([a["L0_ffn_We_down"].transpose(0, 2, 1).reshape(E * HID, D), a["L0_ffn_Ws_down"].T],
                                axis=0).reshape(NK, P, D).transpose(1, 0, 2).reshape(P, NK * D),
        "wrouter0": a["L0_ffn_Wg"].T,
        "wshared_gate": a["L0_ffn_Wsg"].T,
        "bq": bqkv[0:D].reshape(P, 1),
        "bk": bqkv[D:2 * D].reshape(P, 1),
        "bq_rep": np.broadcast_to(heads, (H // 2, 2, QG, C)).reshape(H // 2, P).T,
        "q1": a["L1_attn_q_w"], "k1": a["L1_attn_k_w"], "v1": a["L1_attn_v_w"], "o1": a["L1_attn_o_w"],
        "wrouter1": a["L1_ffn_router_w"].T,
        "b1": a["L1_ffn_b1"].reshape(E, FF // P, P).transpose(2, 0, 1).reshape(P, -1),
    }
    arrays = {
        "x": a["L0_attn_x"].reshape(T, D),
        "weights": np.concatenate([w[n] for n in WEIGHTS], axis=1),
        "rows": np.concatenate([bqkv[2 * D:3 * D], a["L0_attn_b_out"], a["L1_ffn_router_b"]]),
        "rel_k": a["L0_attn_rel_emb_k"].T,
        "rel_v": a["L0_attn_rel_emb_v"],
        "w1": a["L1_ffn_w1"], "w2": a["L1_ffn_w2"], "b2": a["L1_ffn_b2"].reshape(-1),
        **shape_constants(nb, cap),
    }
    arrays = {"in_" + k: np.ascontiguousarray(v) for k, v in arrays.items()}
    nc = bacc.Bacc("TRN2", target_bir_lowering=False, num_devices=1)
    io = {k[3:]: nc.dram_tensor(k, v.shape, mybir.dt.from_np(v.dtype), kind="ExternalInput").ap() for k, v in arrays.items()}
    io["out"] = nc.dram_tensor("out_0", (T, D), F32, kind="ExternalOutput").ap()
    program(nc, io, nb, cap)
    r = run_bass_kernel_spmd(nc, [arrays], core_ids=[0])
    return r.results[0]["out_0"].reshape(nb, S, D)
```

```python
import math
from contextlib import ExitStack

import numpy as np
import concourse.bass as bass
from concourse import mybir
from concourse.alu_op_type import AluOpType as ALU

F32 = mybir.dt.float32
BF16 = mybir.dt.bfloat16
F32R = mybir.dt.float32r
I32 = mybir.dt.int32
U32 = mybir.dt.uint32
ACT = mybir.ActivationFunctionType
AX = mybir.AxisListType

P = 128
S = 256
D = 128
H = 16
C = 8
R = 64
QG = 8
GS = 2
NS = S // (QG * GS)
KT = S // P
E = 16
HID = 64
SH = 256
NK = E * HID // P + SH // P
FF = 512
EPS = 1e-5
MAGIC = 0x5F3759DF
OW = D + QG * C

CONSTS = {"ident": P, "mask_head_rows": H, "mask_head": H, "mask_query": QG,
          "pick_query": QG, "iota": E, "dump": 4}
NCONST = sum(CONSTS.values())
WEIGHTS = {"wqkv": 3 * D, "wv_q": 2 * D, "wout": D, "wgate": E * HID + SH, "wup": E * HID + SH, "wdown": NK * D,
           "wrouter0": E, "wshared_gate": 1, "bq": 1, "bk": 1, 
           "q1": D, "k1": D, "v1": D, "o1": D, "wrouter1": E, "b1": E * FF // P}
NWEIGHT = sum(WEIGHTS.values())
ROWS = {"bv": D, "bq_row": D, "bout": D, "brouter1": E}
NROW = sum(ROWS.values())

JOBS_A = [(0, "router0", "mid"), (0, "up0", "mid"), (1, "up1", "mid"), (1, "up2", "mid"), (2, "up3", "mid"), (2, "up4", "mid"),
          (3, "gateT", "mid"), (4, "out", "tail"), (5, "up5", "mid"), (5, "xnT", "front"), (6, "spread0", "mid"),
          (6, "qk", "front"), (7, "spread1", "mid"), (7, "xn2T", "tail"), (8, "router1", "tail"), (8, "vq", "front"),
          (9, "up6", "mid"), (9, "up7", "mid"), (10, "prefix", "tail"), (10, "up8", "mid"), (11, "spread2", "mid"),
          (11, "up9", "mid"), (12, "spread3", "mid"), (12, "shared", "mid")]
JOBS_B = [(5, "out", "tail"), (8, "qk", "front"), (9, "v", "front")]

SECTIONS = {"pro": {"front"}, "first": {"mid", "front"}, "mid": {"tail", "mid", "front"},
            "last": {"tail", "mid"}, "end": {"tail"}}


class Tally:

    def __init__(self, nb, events):
        self.nb, self.events = nb, events

    def total(self, kind):
        return sum(s in SECTIONS[kind] for _, s in self.events)

    def __call__(self, kind, b, name):
        present = [n for n, s in self.events if s in SECTIONS[kind]]
        rank = present.index(name) + 1
        if kind == "pro":
            return rank
        if kind == "first":
            return rank + self.total("pro")
        base = rank + self.total("pro") + self.total("first")
        if kind == "end":
            return base + self.total("mid") * (self.nb - 2) + self.total("last")
        return (b - 1) * self.total("mid") + base


def bodies(engine, nb, body):
    body("pro", -1, 1)
    body("first", 0, 0)
    with engine.Fori(0, (nb - 2) // 2) as i:
        b = engine.snap(2 * i + 1)
        body("mid", b, 1)
        body("mid", b + 1, 0)
    body("last", nb - 1, 1)
    body("end", nb, 0)


def program(nc, io, nb, cap):
    T = nb * S
    NT = T // P
    SLOTS = E * cap
    JT = cap // P
    ctx = ExitStack()
    with ctx:
        def sb(name, shape, dt=F32):
            return ctx.enter_context(nc.sbuf_tensor(name, shape, dt))

        def sem(name):
            return ctx.enter_context(nc.semaphore(name))

        packed = nc.dram_tensor("packed", (SLOTS + 2 * T, D), F32).ap()
        expert_out = nc.dram_tensor("expert_out", (SLOTS, D), F32).ap()
        xnT1 = nc.dram_tensor("xnT1", (nb, P, S), F32).ap()
        NU = 2 * S - 1
        rel_k_ext = nc.dram_tensor("rel_k_ext", (C, NU), F32).ap()
        q_rows = nc.dram_tensor("q_rows", (S, 2 * D), F32).ap()
        rel_v_ext = nc.dram_tensor("rel_v_ext", (NU, C), F32).ap()

        consts = sb("consts", [P, NCONST])
        weights = sb("weights", [P, NWEIGHT])
        rows = sb("rows", [P, NROW])
        cview, at = {}, 0
        for name, n in CONSTS.items():
            cview[name] = consts[:, at:at + n]
            at += n
        wview, at = {}, 0
        for name, n in WEIGHTS.items():
            wview[name] = weights[:, at:at + n]
            at += n
        rview, at = {}, 0
        for name, n in ROWS.items():
            rview[name] = rows[:, at:at + n]
            at += n
        ident = cview["ident"]
        spread = sb("spread", [2 * E, E * HID])
        tri = sb("tri", [P, 2 * P], BF16)
        alibi_l = sb("alibi_l", [3 * QG, P], BF16)
        alibi_r = sb("alibi_r", [3 * QG, S - QG + S], BF16)
        residual = sb("residual", [P, NT, D])
        slot_ids = sb("slot_ids", [P, NT, 2], U32)
        slot_w = sb("slot_w", [P, NT, 2])

        load_sem = sem("load")
        x_first = sem("x_first")
        x_rest = sem("x_rest")
        zeroed = sem("zeroed")

        with ExitStack() as pa:
            def sa(name, shape, dt=F32):
                return pa.enter_context(nc.sbuf_tensor(name, shape, dt))

            def pa_bank(name):
                return pa.enter_context(nc.psum_tensor(name, [P, 512], F32))

            S_ps = [pa_bank(f"scores{i}") for i in range(2)]
            PT_ps = [pa_bank(f"probsT{i}") for i in range(2)]
            O_ps = pa_bank("values")
            CTX_ps = pa_bank("context")
            M_ps = [pa_bank(f"spare{i}") for i in range(2)]

            rel_k2 = sa("rel_k2", [P, 2, 2 * S - QG])
            rel_v = sa("rel_v", [P, (S + P) // QG, QG * C])
            wshared = sa("wshared", [P, P])
            bq_s = sa("bq_s", [P, 1])
            bq_row_s = sa("bq_row_s", [P, D])
            xnT = [sa(f"xnT_{i}", [P, S]) for i in range(2)]
            qT = [sa(f"qT_{i}", [P, 2, S]) for i in range(2)]
            kT = [sa(f"kT_{i}", [P, 2, S]) for i in range(2)]
            v_new = sa("v_new", [P, KT, D])
            q_row = sa("q_row", [P, 2, D])
            q_row2 = sa("q_row2", [P, 2, 2, D])
            q_rel = [sa(f"q_rel_{i}", [P, S // QG, P]) for i in range(2)]
            vf = [sa(f"vf_{i}", [P, KT, 2, GS, OW]) for i in range(2)]
            hid = [sa(f"hid_{i}", [P, NK, S]) for i in range(2)]
            xn = sa("xn", [P, 2, D])
            q_blk = [sa(f"q_blk_{i}", [P, 2, GS, P]) for i in range(2)]
            probs = [sa(f"probs_{i}", [P, GS, S]) for i in range(2)]
            probsT = [sa(f"probsT_s{i}", [P, KT, GS, P]) for i in range(2)]
            nmax = [sa(f"nmax_{i}", [P, GS]) for i in range(4)]
            rsum = [sa(f"rsum_{i}", [P, GS]) for i in range(4)]
            rinv = [sa(f"rinv_{i}", [P, GS]) for i in range(4)]
            pick = [sa(f"pick_{i}", [P, GS, QG]) for i in range(4)]
            rel_m = [sa(f"rel_m_{i}", [P, GS, QG, C]) for i in range(2)]
            rel_s = [sa(f"rel_s_{i}", [P, GS, C]) for i in range(2)]
            z1 = [sa(f"z1_{i}", [P, GS, D]) for i in range(2)]
            zz = [sa(f"zz_{i}", [P, GS, D]) for i in range(2)]
            ctxT = sa("ctxT", [P, S])
            th = [sa(f"th_{i}", [P, S]) for i in range(2)]
            ga = sa("ga", [P, S])
            gate_bc = [sa(f"gate_bc_{i}", [P, 2, S]) for i in range(2)]
            shared_bc = sa("shared_bc", [P, S])
            shared_th = sa("shared_th", [P, S])
            gates = sa("gates", [P, 2, E])
            gates2 = sa("gates2", [P, 2, 2, E])
            gatesT = sa("gatesT", [2 * E, S])
            x1a = sa("x1a", [P, 2, D])
            x1 = sa("x1", [P, 2, D])
            xn2 = sa("xn2", [P, 2, D])
            xn2T = sa("xn2T", [P, S])
            stats = sa("stats", [P, 2, 6])
            mv = sa("mv", [P, 2, 2])
            nw = sa("nw", [P, 5, 2])
            top = [{n: sa(f"{n}_{i}", sh, dt) for n, sh, dt in
                    (("seen", [P, 2, E], F32), ("logit", [P, 2, E], F32), ("m8", [P, 2, 8], F32), ("i8", [P, 2, 8], U32), ("idx", [P, 2, 2], F32),
                     ("gap", [P, 2], F32), ("ex", [P, 2], F32), ("den", [P, 2], F32), ("g", [P, 2, 2], F32),
                     ("oh", [P, 2, 2, E], F32), ("t0", [P, 2, E], F32), ("t1", [P, 2, E], F32))} for i in range(2)]
            chosen = sa("chosen", [P, 2, E], BF16)
            counts = sa("counts", [P, E])
            before = sa("before", [P, 3, E])
            pos = sa("pos", [P, 2, E])
            posk = sa("posk", [P, 2, 2, E])
            pk = sa("pk", [P, 2, 2])
            kept = sa("kept", [P, 2, 2])
            slot = sa("slot", [P, 2, 2])
            sk = sa("sk", [P, 2, 2])
            dumpk = sa("dumpk", [P, 2, 2])
            dump_at = sa("dump_at", [P, 2, 2])
            gk = sa("gk", [P, 2, 2])
            gden = sa("gden", [P, 2])
            scat_f = sa("scat_f", [P, 2, 2])
            scat = sa("scat", [P, 2, 2], U32)
            zeros = hid[1]
            free_hid = hid[0][:, :, :].rearrange("p a b -> p (a b)")
            free_gate = gate_bc[0][:, :, :].rearrange("p a b -> p (a b)")
            W = 2 * S - QG
            at = E * HID
            spread_f = free_hid[0:2 * E, 0:at]
            rel_k_row = free_hid[0:C, at:at + NU]
            rel_k = free_hid[:, at + NU + 1:at + NU + 1 + W]
            alibi_rf = free_hid[0:3 * QG, at + NU + 1 + W:at + NU + 1 + 2 * W]
            tri_f = free_gate[:, 0:2 * P]
            alibi_lf = free_gate[0:3 * QG, 2 * P:3 * P]

            cleared = sem("zeros_cleared")
            act_ready = sem("biases_scaled")
            dve_ready = sem("weights_prepared")
            split_ready = sem("relative_keys_split")
            built = sem("queries_built")
            scored = sem("scores_ready")
            maxed = sem("max_ready")
            exped = sem("probs_ready")
            turned = sem("probsT_ready")
            moved = sem("probsT_moved")
            valued = sem("values_ready")
            picked = sem("pick_ready")
            merged = sem("z1_ready")
            masked = sem("z_ready")
            ctxed = sem("context_done")
            ctx_moved = sem("context_moved")
            full = [sem("spare0_full"), sem("spare1_full")]
            free = [sem("spare0_free"), sem("spare1_free")]
            th_done = sem("tanh_done")
            uppers_done = sem("upper_parts_done")
            values_done = sem("values_done")
            values_placed = sem("values_placed")
            q_split = sem("query_rows_split")
            q_stored = sem("query_rows_stored")
            q_placed = sem("query_blocks_placed")
            q_zeroed = sem("query_blocks_zeroed")
            placed = sem("relative_values_placed")
            hid_done = sem("hidden_done")
            xn_done = sem("xn_done")
            gates_done = sem("gates_done")
            gap_done = sem("gap_done")
            ex_done = sem("ex_done")
            xn2_done = sem("xn2_done")
            chosen_done = sem("chosen_done")
            xnT1_stored = sem("xnT1_stored")
            slots_done = sem("slots_done")
            scattered = sem("scattered")
            rows_known = sem("rows_known")
            chain = sem("dve_chain")
            ext_sem = sem("ext")
            row_sem = sem("row_loaded")
            row_extended = sem("row_extended")

            bank_of = {name: i % 2 for i, (_, name, _) in enumerate(JOBS_A)}
            bank_events = [[(n, s) for _, n, s in JOBS_A if bank_of[n] == i] for i in range(2)]
            bank_tally = [Tally(nb, ev) for ev in bank_events]
            ups = [(n, s) for _, n, s in JOBS_A if n.startswith("up")]
            th_tally = Tally(nb, ups)
            spr_tally = Tally(nb, [(n, s) for _, n, s in JOBS_A if n.startswith("spread") or n == "shared"])
            one_front = Tally(nb, [("x", "front")])
            one_tail = Tally(nb, [("x", "tail")])
            one_mid = Tally(nb, [("x", "mid")])
            two = Tally(nb, [("router0", "mid"), ("router1", "tail")])
            idx_of = {n: i for i, (_, n, _) in enumerate(JOBS_A)}

            def jobs(kind, step):
                return [n for s, n, sec in JOBS_A if s == step and sec in SECTIONS[kind]]

            def present(kind, s, lag):
                return kind in (("first", "mid", "last") if s >= lag else ("mid", "last", "end"))

            def steps(kind):
                return range(NS)

            block = pa.enter_context(nc.Block())

            @block.sync
            def _(sp):
                sp.dma_start(residual[:, 0:4, :], io["x"][0:512, :].rearrange("(n p) d -> p n d", p=P)).then_inc(x_first, 16)
                sp.dma_start(consts[:, :], io["consts"]).then_inc(load_sem, 16)
                sp.dma_start(weights[:, :], io["weights"]).then_inc(load_sem, 16)
                sp.dma_start(rows[:, :], io["rows"].partition_broadcast(P)).then_inc(load_sem, 16)
                sp.dma_start(spread_f[:, :], io["spread"]).then_inc(load_sem, 16)
                sp.dma_start(tri_f[:, :], io["tri"]).then_inc(load_sem, 16)
                sp.dma_start(alibi_lf[:, :], io["alibi_l"]).then_inc(load_sem, 16)
                sp.dma_start(alibi_rf[:, :], io["alibi_r"]).then_inc(load_sem, 16)
                lo, n = S - 1 - R, 2 * R + 1
                ek, ev = io["rel_k"], io["rel_v"]
                sp.dma_start(rel_k_row[:, lo:lo + n], ek).then_inc(row_sem, 16)
                sp.dma_start(rel_v_ext[lo:lo + n, :], ev).then_inc(ext_sem, 16)
                sp.dma_start(rel_v_ext[0:lo, :], ev[0:1, :].to_broadcast((lo, C))).then_inc(ext_sem, 16)
                sp.dma_start(rel_v_ext[lo + n:NU, :], ev[n - 1:n, :].to_broadcast((lo, C))).then_inc(ext_sem, 16)
                sp.wait_ge(row_extended, 2)
                sp.dma_start(rel_k_ext, rel_k_row[:, :]).then_inc(ext_sem, 16)
                sp.wait_ge(ext_sem, 64)
                for q in range(QG):
                    for part in range(2):
                        p0 = (2 * q + part) * C
                        sp.dma_start(rel_k[p0:p0 + C, :], rel_k_ext[:, QG - 1 - q:QG - 1 - q + W]).then_inc(load_sem, 16)
                sp.dma_start(rel_v[:, :, :].rearrange("p u w -> p (u w)"),
                             bass.AP(tensor=rel_v_ext.tensor, offset=0, ap=[[C, P], [1, (S + P) * C]])).then_inc(load_sem, 16)
                for n in range(4, NT, 4):
                    m = min(4, NT - n)
                    sp.dma_start(residual[:, n:n + m, :],
                                 io["x"][P * n:P * (n + m), :].rearrange("(n p) d -> p n d", p=P)).then_inc(x_rest, 16)
                sp.wait_ge(cleared, 1)
                nz = NK * S // D * P
                flat = zeros[:, :, :].rearrange("p a b -> p (a b)")
                for r0 in range(0, SLOTS, nz):
                    m = min(nz, SLOTS - r0)
                    sp.dma_start(packed[r0:r0 + m, :].rearrange("(p a) d -> p (a d)", p=P),
                                 flat[:, 0:m // P * D]).then_inc(zeroed, 16)
                sp.wait_ge(q_zeroed, 2)

                def body(kind, b, par):
                    if "front" in SECTIONS[kind]:
                        place_queries(kind, b, par)
                    if "tail" in SECTIONS[kind]:
                        bank = bank_of["xn2T"]
                        sp.wait_ge(free[bank], bank_tally[bank](kind, b, "xn2T"))
                        sp.dma_start(xnT1[bass.ds(b - 1, 1)].rearrange("a p s -> p (a s)"), xn2T[:, :]).then_inc(xnT1_stored, 16)

                def place_queries(kind, b, par):
                    sp.wait_ge(q_split, one_front(kind, b, "x"))
                    sp.dma_start(q_rows.rearrange("(i p) w -> p i w", p=P),
                                 q_row2[:, :, :, :].rearrange("p i k w -> p i (k w)")).then_inc(q_stored, 16)
                    sp.wait_ge(q_stored, (b + 2) * 16)
                    for q in range(QG):
                        sp.dma_start(q_rel[1 - par][2 * C * q:2 * C * (q + 1), :, H * q:H * (q + 1)],
                                     bass.AP(tensor=q_rows.tensor, offset=q * 2 * D,
                                             ap=[[H, 2 * C], [QG * 2 * D, S // QG], [1, H]])).then_inc(q_placed, 16)
                sp.dma_start(xn2T[:, :], io["x"][0:2 * P, :].rearrange("(p a) d -> p (a d)", a=2)).then_inc(xnT1_stored, 16)
                bodies(sp, nb, body)
                sp.wait_ge(xnT1_stored, 16 * nb + 16)
            LOADS = 16 * (7 + 2 * QG + 1)
            NZERO = 16 * -(-SLOTS // (NK * S // D * P))
            XREST = 16 * len(range(4, NT, 4))

            @block.gpsimd
            def _(pool):
                for i in range(2):
                    pool.memset(q_rel[i][:, :, :], 0.0).then_inc(q_zeroed, 1)
                pool.wait_ge(load_sem, LOADS)

                def build(s, par):
                    for part in range(2):
                        ins = pool.tensor_tensor(q_blk[s % 2][:, part, :, :].rearrange("p g (q h) -> p (g q) h", h=H).bitcast(F32R),
                                                 qT[par][:, part, 16 * s:16 * s + 16].unsqueeze(2).to_broadcast((P, 16, H)),
                                                 cview["mask_head_rows"].unsqueeze(1).to_broadcast((P, 16, H)), ALU.mult)
                    ins.then_inc(built, 1)

                def body(kind, b, par):
                    t0 = pool.snap(b * NS) if kind == "mid" else b * NS
                    if kind == "pro":
                        pool.wait_ge(free[bank_of["qk"]], bank_tally[bank_of["qk"]](kind, b, "qk"))
                        build(0, 0)
                        return
                    for s in steps(kind):
                        if kind != "end" and not (kind == "last" and s == NS - 1):
                            if s == NS - 1:
                                pool.wait_ge(free[bank_of["qk"]], bank_tally[bank_of["qk"]](kind, b, "qk"))
                            if not (kind == "first" and s == 0):
                                pool.wait_ge(scored, t0 + s)
                            build((s + 1) % NS, par if s < NS - 1 else 1 - par)
                        if present(kind, s, 2) and not (kind == "end" and s >= 2):
                            pool.wait_ge(merged, t0 + s - 1)
                            pool.tensor_tensor(zz[s % 2][:, :, :].rearrange("p g (h c) -> p g h c", c=C),
                                               z1[s % 2][:, :, :].rearrange("p g (h c) -> p g h c", c=C),
                                               cview["mask_head"].unsqueeze(1).unsqueeze(3).to_broadcast((P, GS, H, C)),
                                               ALU.mult).then_inc(masked, 1)
                        tail = "tail" in SECTIONS[kind]
                        if s == 12 and tail:
                            pool.sem_clear(rows_known)
                            pool.wait_ge(slots_done, one_tail(kind, b, "x"))
                            pool.tensor_tensor(scat_f[:, :, :], dumpk[:, :, :], sk[:, :, :], ALU.add).then_inc(rows_known, 1)
                            pool.wait_ge(rows_known, 1)
                            pool.tensor_copy(scat[:, :, :], scat_f[:, :, :]).then_inc(rows_known, 1)
                            pool.wait_ge(rows_known, 2)
                            if kind == "mid" and par == 1:
                                pool.wait_ge(zeroed, NZERO)
                        if s >= 12 and tail:
                            i, k = (s - 12) // 2, s % 2
                            pool.indirect_dma_start(
                                out=packed, out_offset=bass.IndirectOffsetOnAxis(ap=scat[:, i, k:k + 1], axis=0),
                                in_=xn2[:, i, :], in_offset=None).then_inc(scattered, 16)
                pool.dma_start(xn2[:, 0, :], io["x"][0:P, :]).then_inc(scattered, 16)
                bodies(pool, nb, body)
                pool.wait_ge(scattered, 64 * nb + 16)

            @block.scalar
            def _(act):
                act.wait_ge(load_sem, LOADS)
                act.mul(bq_s[:, :], wview["bq"], C ** -0.5)
                act.mul(bq_row_s[:, :], rview["bq_row"], C ** -0.5).then_inc(act_ready, 1)
                act.wait_ge(act_ready, 1)

                def move(kind, b, par, name):
                    bank = bank_of[name]
                    m, n = M_ps[bank], bank_tally[bank](kind, b, name)
                    if name.startswith("up"):
                        k = int(name[2:])
                        act.wait_ge(full[bank], n)
                        act.activation(th[k % 2][:, :], m[:, 0:S], ACT.Tanh, scale=0.5).then_inc(th_done, 1)
                    elif name == "gateT":
                        act.wait_ge(full[bank], n)
                        act.copy(gatesT[:, :].bitcast(F32R), m[0:2 * E, 0:S]).then_inc(free[bank], 1)
                    elif name.startswith("spread"):
                        j = int(name[6:])
                        act.wait_ge(full[bank], n)
                        if j >= 2:
                            act.wait_ge(hid_done, spr_tally(kind, b, f"spread{j - 2}"))
                        elif kind != "first":
                            act.wait_ge(hid_done, (4 + 1) * b)
                        act.copy(gate_bc[j % 2][:, :, :], m[:, 0:2 * S].rearrange("p (a b) -> p a b", a=2)).then_inc(free[bank], 1)
                    elif name == "shared":
                        act.wait_ge(full[bank], n)
                        act.activation(shared_th[:, :], m[:, 0:S], ACT.Tanh, scale=0.5).then_inc(free[bank], 1)
                    elif name == "xnT":
                        act.wait_ge(full[bank], n)
                        act.copy(xnT[1 - par][:, :], m[:, 0:S]).then_inc(free[bank], 1)
                    elif name == "xn2T":
                        act.wait_ge(full[bank], n)
                        act.wait_ge(xnT1_stored, 16 * one_tail(kind, b, "x"))
                        act.copy(xn2T[:, :], m[:, 0:S]).then_inc(free[bank], 1)
                    elif name == "qk":
                        act.wait_ge(full[bank], n)
                        act.activation(qT[1 - par][:, 0, :].bitcast(F32R), m[:, 0:S], ACT.Identity, bias=bq_s[:, 0:1])
                        act.activation(kT[1 - par][:, 0, :].bitcast(F32R), m[:, S:2 * S], ACT.Identity,
                                       bias=wview["bk"]).then_inc(uppers_done, 1)

                def body(kind, b, par):
                    t0 = act.snap(b * NS) if kind == "mid" else b * NS
                    for s in steps(kind):
                        if s:
                            for name in jobs(kind, s - 1):
                                move(kind, b, par, name)
                        if s == 3 and "tail" in SECTIONS[kind]:
                            act.wait_ge(ctxed, t0)
                            act.copy(ctxT[:, :], CTX_ps[:, 0:S]).then_inc(ctx_moved, 1)
                        if present(kind, s, 0):
                            act.wait_ge(maxed, t0 + s + 1)
                            for g in range(GS):
                                ins = act.activation(probs[s % 2][:, g, :], S_ps[s % 2][:, g * S:(g + 1) * S], ACT.Exp,
                                                     bias=nmax[s % 4][:, g:g + 1], accum_out=rsum[s % 4][:, g:g + 1])
                            ins.then_inc(exped, 1)
                        if present(kind, s, 1) and not (kind == "end" and s >= 1):
                            act.wait_ge(turned, t0 + s)
                            act.copy(probsT[(s - 1) % 2][:, :, :, :].rearrange("p a b c -> p (a b c)"),
                                     PT_ps[(s - 1) % 2][:, :]).then_inc(moved, 1)
                        if s == 9 and "front" in SECTIONS[kind]:
                            act.wait_ge(values_done, one_front(kind, b, "x"))
                            for a in range(KT):
                                ins = act.copy(vf[1 - par][:, a, :, :, 0:D].rearrange("p r g d -> p (r g) d"),
                                               v_new[:, a, :].unsqueeze(1).to_broadcast((P, 2 * GS, D)))
                            ins.then_inc(values_placed, 1)
                        for i, at, section in ((0, 2, "mid"), (1, 10, "tail")):
                            if s == at and section in SECTIONS[kind]:
                                act.wait_ge(gap_done, two(kind, b, f"router{i}"))
                                act.activation(top[i]["ex"][:, :], top[i]["gap"][:, :], ACT.Exp).then_inc(ex_done, 1)
                bodies(act, nb, body)

            @block.vector
            def _(dve):
                dve.memset(zeros[:, :, :], 0.0).then_inc(cleared, 1)
                lo, n = S - 1 - R, 2 * R + 1
                dve.wait_ge(row_sem, 16)
                dve.tensor_copy(rel_k_row[:, 0:lo], rel_k_row[:, lo:lo + 1].to_broadcast((C, lo))).then_inc(row_extended, 1)
                dve.tensor_copy(rel_k_row[:, lo + n:NU], rel_k_row[:, lo + n - 1:lo + n].to_broadcast((C, lo))).then_inc(row_extended, 1)
                dve.wait_ge(load_sem, LOADS)
                for wq in (wview["wqkv"][:, 0:D], wview["wv_q"][:, D:2 * D]):
                    dve.tensor_scalar(wq, wq, C ** -0.5, None, ALU.mult)
                dve.tensor_copy(rel_k2[:, 0, :].bitcast(F32R), rel_k[:, :]).then_inc(split_ready, 1)
                dve.wait_ge(split_ready, 1)
                dve.tensor_tensor(rel_k2[:, 1, :].bitcast(F32R), rel_k[:, :], rel_k2[:, 0, :], ALU.subtract)
                dve.tensor_copy(spread[:, :].bitcast(F32R), spread_f[:, :])
                for half, whole in ((tri, tri_f), (alibi_l, alibi_lf), (alibi_r, alibi_rf)):
                    dve.tensor_copy(half[:, :], whole[:, :])
                dve.tensor_copy(wshared[:, :], wview["wshared_gate"].to_broadcast((P, P))).then_inc(dve_ready, 1)
                dve.tensor_copy(dump_at[:, :, :], cview["dump"].rearrange("p (i k) -> p i k", k=2))
                dve.memset(counts[:, :], 0.0).then_inc(dve_ready, 1)
                dve.wait_ge(dve_ready, 2)
                links = [0]
                LATE = {"router0": "choose0", "router1": "choose1", "prefix": "slots", "vq": "split"}
                LATE.update({name: name for name in ("spread0", "spread1", "spread2", "spread3", "shared")})

                def link(ins):
                    links[0] += 1
                    ins.then_inc(chain, 1)
                    dve.wait_ge(chain, links[0])

                def layernorm_begin(tile_of):
                    for i in range(2):
                        ins = dve.bn_stats(stats[:, i, :], tile_of(i))
                    link(ins)
                    for i in range(2):
                        ins = dve.bn_aggr(mv[:, i, :], stats[:, i, :])
                    link(ins)
                    v, y, a, c = nw[:, 0, :], nw[:, 1, :], nw[:, 2, :], nw[:, 3, :]
                    link(dve.tensor_scalar(v, mv[:, :, 1], EPS, None, ALU.add))
                    link(dve.tensor_scalar(a.bitcast(I32), v.bitcast(I32), 1, None, ALU.logical_shift_right))
                    link(dve.tensor_scalar(y.bitcast(I32), a.bitcast(I32), -1.0, float(MAGIC), ALU.mult, ALU.add))
                    newton(1)

                def newton(times):
                    v, y, a, c = nw[:, 0, :], nw[:, 1, :], nw[:, 2, :], nw[:, 3, :]
                    for _ in range(times):
                        link(dve.tensor_tensor(a, y, y, ALU.mult))
                        link(dve.scalar_tensor_tensor(c, a, -0.5, v, ALU.mult, ALU.mult))
                        link(dve.scalar_tensor_tensor(y, c, 1.5, y, ALU.add, ALU.mult))

                def layernorm_end(tile_of, normalised, done):
                    newton(2)
                    y = nw[:, 1, :]
                    for i in range(2):
                        ins = dve.tensor_scalar(normalised[:, i, :], tile_of(i), mv[:, i, 0:1], y[:, i:i + 1], ALU.subtract, ALU.mult)
                    ins.then_inc(done, 1)

                def logits(i, bank, bias):
                    q = top[i]
                    m = M_ps[bank][:, 0:2 * E].rearrange("p (t e) -> p t e", e=E)
                    if bias is None:
                        ins = dve.tensor_copy(q["seen"][:, :, :], m)
                    else:
                        ins = dve.tensor_tensor(q["seen"][:, :, :], m, bias.unsqueeze(1).to_broadcast((P, 2, E)), ALU.add)
                    ins.then_inc(free[bank], 1)

                def top_two(kind, b, i, name):
                    q = top[i]
                    dve.wait_ge(free[bank_of[name]], bank_tally[bank_of[name]](kind, b, name))
                    link(dve.tensor_copy(q["logit"][:, :, :], q["seen"][:, :, :]))
                    dve.max(q["m8"][:, 0, :], q["logit"][:, 0, :])
                    link(dve.max(q["m8"][:, 1, :], q["logit"][:, 1, :]))
                    dve.tensor_tensor(q["gap"][:, :], q["m8"][:, :, 1], q["m8"][:, :, 0], ALU.subtract).then_inc(gap_done, 1)
                    for j in range(2):
                        ins = dve.max_index(q["i8"][:, j, :], q["m8"][:, j, :], q["logit"][:, j, :])
                    link(ins)
                    link(dve.tensor_copy(q["idx"][:, :, :], q["i8"][:, :, 0:2]))
                    for k in range(2):
                        ins = dve.tensor_tensor(q["oh"][:, :, k, :], cview["iota"].unsqueeze(1).to_broadcast((P, 2, E)),
                                                q["idx"][:, :, k:k + 1].to_broadcast((P, 2, E)), ALU.is_equal)
                    link(ins)

                def top_softmax(kind, b, i, name):
                    q = top[i]
                    dve.wait_ge(ex_done, two(kind, b, name))
                    link(dve.tensor_scalar(q["den"][:, :], q["ex"][:, :], 1.0, None, ALU.add))
                    link(dve.reciprocal(q["g"][:, :, 0], q["den"][:, :]))
                    link(dve.tensor_tensor(q["g"][:, :, 1], q["g"][:, :, 0], q["ex"][:, :], ALU.mult))

                def handle(kind, b, par, name):
                    if name not in ("gateT", "xnT", "xn2T", "spread0",
                                    "spread1", "spread2", "spread3", "shared", "gates", "weights",
                                    "choose0", "choose1", "slots", "split"):
                        bank = bank_of[name]
                        m, n = M_ps[bank], bank_tally[bank](kind, b, name)
                        dve.wait_ge(full[bank], n)
                    if name == "router0":
                        logits(0, bank, None)
                    elif name == "gates":
                        top_softmax(kind, b, 0, "router0")
                        q = top[0]
                        for k, t in ((0, q["t0"]), (1, q["t1"])):
                            ins = dve.tensor_tensor(t[:, :, :], q["oh"][:, :, k, :],
                                                    q["g"][:, :, k:k + 1].to_broadcast((P, 2, E)), ALU.mult)
                        link(ins)
                        link(dve.tensor_tensor(gates[:, :, :], q["t0"][:, :, :], q["t1"][:, :, :], ALU.add))
                        link(dve.tensor_copy(gates2[:, :, 0, :].bitcast(F32R), gates[:, :, :]))
                        dve.tensor_tensor(gates2[:, :, 1, :].bitcast(F32R), gates[:, :, :], gates2[:, :, 0, :],
                                          ALU.subtract).then_inc(gates_done, 1)
                    elif name.startswith("up"):
                        k = int(name[2:])
                        dve.wait_ge(th_done, th_tally(kind, b, name))
                        link(dve.scalar_tensor_tensor(ga[:, :], th[k % 2][:, :], 1.0, m[:, 0:S], ALU.add, ALU.mult))
                        ins = dve.tensor_tensor(hid[par][:, k, :], ga[:, :], m[:, S:2 * S], ALU.mult)
                        ins.then_inc(free[bank], 1)
                        dve.wait_ge(free[bank], n)
                    elif name.startswith("spread"):
                        j = int(name[6:])
                        bk = bank_of[name]
                        dve.wait_ge(free[bk], bank_tally[bk](kind, b, name))
                        dve.tensor_tensor(hid[par][:, 2 * j:2 * j + 2, :], hid[par][:, 2 * j:2 * j + 2, :],
                                          gate_bc[j % 2][:, :, :], ALU.mult).then_inc(hid_done, 1)
                    elif name == "shared":
                        bk = bank_of[name]
                        dve.wait_ge(free[bk], bank_tally[bk](kind, b, name))
                        link(dve.tensor_scalar(shared_bc[:, :], shared_th[:, :], 0.25, 0.25, ALU.mult, ALU.add))
                        dve.tensor_tensor(hid[par][:, NK - 2:NK, :], hid[par][:, NK - 2:NK, :],
                                          shared_bc[:, :].unsqueeze(1).to_broadcast((P, 2, S)), ALU.mult).then_inc(hid_done, 1)
                    elif name == "qk":
                        dve.wait_ge(uppers_done, one_front(kind, b, "x"))
                        dve.scalar_tensor_tensor(qT[1 - par][:, 1, :].bitcast(F32R), m[:, 0:S], bq_s[:, 0:1],
                                                 qT[1 - par][:, 0, :], ALU.add, ALU.subtract)
                        dve.scalar_tensor_tensor(kT[1 - par][:, 1, :].bitcast(F32R), m[:, S:2 * S], wview["bk"],
                                                 kT[1 - par][:, 0, :], ALU.add, ALU.subtract).then_inc(free[bank], 1)
                    elif name == "vq":
                        dve.tensor_tensor(v_new[:, :, :], m[:, 0:S].rearrange("p (a d) -> p a d", a=KT),
                                          rview["bv"].unsqueeze(1).to_broadcast((P, KT, D)), ALU.add).then_inc(values_done, 1)
                        dve.tensor_tensor(q_row[:, :, :], m[:, S:2 * S].rearrange("p (a d) -> p a d", a=2),
                                          bq_row_s[:, :].unsqueeze(1).to_broadcast((P, 2, D)), ALU.add).then_inc(free[bank], 1)
                    elif name == "split":
                        dve.wait_ge(free[bank_of["vq"]], bank_tally[bank_of["vq"]](kind, b, "vq"))
                        if kind != "pro":
                            dve.wait_ge(q_placed, (b + 1) * (16 * QG))
                        link(dve.tensor_copy(q_row2[:, :, 0, :].bitcast(F32R), q_row[:, :, :]))
                        dve.tensor_tensor(q_row2[:, :, 1, :].bitcast(F32R), q_row[:, :, :], q_row2[:, :, 0, :],
                                          ALU.subtract).then_inc(q_split, 1)
                    elif name == "out":
                        here = bass.ds((b - 1) * 2, 2)
                        dve.tensor_tensor(x1a[:, :, :], m[:, 0:S].rearrange("p (a d) -> p a d", a=2),
                                          residual[:, here, :], ALU.add).then_inc(free[bank], 1)
                        dve.wait_ge(free[bank], n)
                        link(dve.tensor_tensor(x1[:, :, :], x1a[:, :, :], rview["bout"].unsqueeze(1).to_broadcast((P, 2, D)), ALU.add))
                        dve.tensor_copy(residual[:, here, :], x1[:, :, :])
                    elif name == "router1":
                        logits(1, bank, rview["brouter1"])
                    elif name == "choose0":
                        top_two(kind, b, 0, "router0")
                    elif name == "choose1":
                        top_two(kind, b, 1, "router1")
                        q = top[1]
                        dve.tensor_tensor(chosen[:, :, :], q["oh"][:, :, 0, :], q["oh"][:, :, 1, :], ALU.add).then_inc(chosen_done, 1)
                    elif name == "prefix":
                        dve.tensor_copy(before[:, :, :], m[:, 0:3 * E].rearrange("p (t e) -> p t e", e=E)).then_inc(free[bank], 1)
                    elif name == "slots":
                        q = top[1]
                        dve.wait_ge(free[bank_of["prefix"]], bank_tally[bank_of["prefix"]](kind, b, "prefix"))
                        link(dve.tensor_tensor(pos[:, :, :], before[:, 0:2, :],
                                               counts[:, :].unsqueeze(1).to_broadcast((P, 2, E)), ALU.add))
                        dve.tensor_tensor(counts[:, :], counts[:, :], before[:, 2, :], ALU.add)
                        link(dve.tensor_tensor(posk[:, :, :, :], q["oh"][:, :, :, :],
                                               pos[:, :, :].unsqueeze(2).to_broadcast((P, 2, 2, E)), ALU.mult))
                        link(dve.tensor_reduce(pk[:, :, :], posk[:, :, :, :], AX.X, ALU.add))
                        link(dve.tensor_scalar(kept[:, :, :], pk[:, :, :], float(cap), None, ALU.is_lt))
                        link(dve.scalar_tensor_tensor(slot[:, :, :], q["idx"][:, :, :], float(cap), pk[:, :, :], ALU.mult, ALU.add))
                        link(dve.tensor_tensor(sk[:, :, :], slot[:, :, :], kept[:, :, :], ALU.mult))
                        dve.tensor_copy(slot_ids[:, bass.ds((b - 1) * 2, 2), :], sk[:, :, :])
                        link(dve.tensor_tensor(dumpk[:, :, :], dump_at[:, :, :], kept[:, :, :], ALU.mult))
                        link(dve.tensor_tensor(dumpk[:, :, :], dump_at[:, :, :], dumpk[:, :, :], ALU.subtract))
                        dve.tensor_scalar(dump_at[:, :, :], dump_at[:, :, :], float(S), None, ALU.add).then_inc(slots_done, 1)
                    elif name == "weights":
                        q = top[1]
                        top_softmax(kind, b, 1, "router1")
                        link(dve.tensor_tensor(gk[:, :, :], q["g"][:, :, :], kept[:, :, :], ALU.mult))
                        link(dve.tensor_tensor(gden[:, :], gk[:, :, 0], gk[:, :, 1], ALU.add))
                        link(dve.tensor_scalar(gden[:, :], gden[:, :], 1e-9, None, ALU.add))
                        link(dve.reciprocal(gden[:, :], gden[:, :]))
                        link(dve.tensor_tensor(slot_w[:, bass.ds((b - 1) * 2, 2), :], gk[:, :, :],
                                               gden[:, :].unsqueeze(2).to_broadcast((P, 2, 2)), ALU.mult))

                def body(kind, b, par):
                    t0 = dve.snap(b * NS) if kind == "mid" else b * NS
                    if kind != "pro":
                        dve.sem_clear(chain)
                        links[0] = 0
                    if kind == "pro":
                        dve.wait_ge(x_first, 16)
                    if kind == "last" or (kind == "mid" and par == 1):
                        dve.wait_ge(x_rest, XREST)
                        dve.wait_ge(zeroed, NZERO)
                    for s in steps(kind):
                        if s:
                            for name in jobs(kind, s - 1):
                                if LATE.get(name) != name:
                                    handle(kind, b, par, name)
                        if present(kind, s, 0):
                            dve.wait_ge(scored, t0 + s + 1)
                            dve.tensor_reduce(nmax[s % 4][:, :], S_ps[s % 2][:, :].rearrange("p (g k) -> p g k", g=GS),
                                              AX.X, ALU.max, negate=True).then_inc(maxed, 1)
                        if present(kind, s, 1) and not (kind == "end" and s >= 1):
                            r = (s - 1) % 4
                            dve.wait_ge(exped, t0 + s)
                            link(dve.reciprocal(rinv[r][:, :], rsum[r][:, :]))
                            dve.tensor_tensor(pick[r][:, :, :], cview["pick_query"].unsqueeze(1).to_broadcast((P, GS, QG)),
                                              rinv[r][:, :].unsqueeze(2).to_broadcast((P, GS, QG)), ALU.mult).then_inc(picked, 1)
                        if present(kind, s, 2) and not (kind == "end" and s >= 2):
                            o = O_ps[:, 0:GS * OW].rearrange("p (g w) -> p g w", g=GS)
                            dve.wait_ge(valued, t0 + s - 1)
                            link(dve.tensor_tensor(rel_m[s % 2][:, :, :, :],
                                                   o[:, :, D:OW].rearrange("p g (q c) -> p g q c", c=C),
                                                   cview["mask_query"].unsqueeze(1).unsqueeze(3).to_broadcast((P, GS, QG, C)),
                                                   ALU.mult))
                            link(dve.tensor_reduce(rel_s[s % 2][:, :, :],
                                                   rel_m[s % 2][:, :, :, :].rearrange("p g q c -> p g c q"), AX.X, ALU.add))
                            dve.tensor_tensor(z1[s % 2][:, :, :].rearrange("p g (h c) -> p g h c", c=C),
                                              o[:, :, 0:D].rearrange("p g (h c) -> p g h c", c=C),
                                              rel_s[s % 2][:, :, :].unsqueeze(2).to_broadcast((P, GS, H, C)),
                                              ALU.add).then_inc(merged, 1)
                        if present(kind, s, 0):
                            u = S // QG - GS * (s + 1)
                            f = rel_v[:, u:u + GS, :]
                            dve.tensor_copy(vf[par][:, :, s % 2, :, D:OW],
                                            bass.AP(tensor=f.tensor, offset=f.offset,
                                                    ap=[f.ap[0], [P // QG * QG * C, KT], [QG * C, GS], [1, QG * C]])).then_inc(placed, 1)
                        for name in jobs(kind, s - 1) if s else ():
                            if name in LATE:
                                handle(kind, b, par, LATE[name])
                        if "mid" in SECTIONS[kind] and s == 2:
                            handle(kind, b, par, "gates")
                        if "tail" in SECTIONS[kind]:
                            if s == 5:
                                layernorm_begin(lambda i: x1[:, i, :])
                            if s == 6:
                                dve.wait_ge(scattered, 64 * (one_tail(kind, b, "x") - 1) + 16)
                                layernorm_end(lambda i: x1[:, i, :], xn2, xn2_done)
                            if s == 12:
                                handle(kind, b, par, "weights")
                        if "front" in SECTIONS[kind]:
                            tile_of = lambda i: residual[:, bass.ds((b + 1) * 2 + i, 1), :].rearrange("p a d -> p (a d)")
                            if s == 0:
                                layernorm_begin(tile_of)
                            if s == 3:
                                layernorm_end(tile_of, xn, xn_done)
                bodies(dve, nb, body)

            @block.tensor
            def _(pe):
                pe.wait_ge(load_sem, LOADS)
                pe.wait_ge(dve_ready, 1)

                def project(kind, b, par, name):
                    bank = bank_of[name]
                    tally = bank_tally[bank]
                    m, n = M_ps[bank], tally(kind, b, name)
                    if not (isinstance(n, int) and n == 1):
                        pe.wait_ge(free[bank], n - 1)
                    w = wview

                    def moved_by(job):
                        pe.wait_ge(free[bank_of[job]], bank_tally[bank_of[job]](kind, b, job))

                    def mm(out, lhsT, rhs, start=True, stop=True):
                        return pe.matmul(out, lhsT, rhs, start=start, stop=stop)
                    if name == "router0":
                        for i in range(2):
                            ins = mm(m[:, i * E:(i + 1) * E], xnT[par][:, i * P:(i + 1) * P], w["wrouter0"])
                    elif name.startswith("up"):
                        k = int(name[2:])
                        mm(m[:, 0:S], w["wgate"][:, k * P:(k + 1) * P], xnT[par][:, :])
                        ins = mm(m[:, S:2 * S], w["wup"][:, k * P:(k + 1) * P], xnT[par][:, :])
                    elif name == "gateT":
                        pe.wait_ge(gates_done, one_mid(kind, b, "x"))
                        for i in range(2):
                            ins = pe.transpose(m[0:2 * E, i * P:(i + 1) * P], gates2[:, i, :, :].rearrange("p k e -> p (k e)"), ident)
                    elif name.startswith("spread"):
                        j = int(name[6:])
                        if j == 0:
                            moved_by("gateT")
                        for i in range(2):
                            k = 2 * j + i
                            ins = mm(m[:, i * S:(i + 1) * S], spread[:, k * P:(k + 1) * P].bitcast(F32R), gatesT[:, :].bitcast(F32R))
                    elif name == "shared":
                        ins = mm(m[:, 0:S], wshared[:, :], xnT[par][:, :])
                    elif name == "xnT":
                        pe.wait_ge(xn_done, one_front(kind, b, "x"))
                        for i in range(2):
                            ins = pe.transpose(m[:, i * P:(i + 1) * P], xn[:, i, :], ident)
                    elif name == "xn2T":
                        pe.wait_ge(xn2_done, one_tail(kind, b, "x"))
                        for i in range(2):
                            ins = pe.transpose(m[:, i * P:(i + 1) * P], xn2[:, i, :], ident)
                    elif name == "qk":
                        moved_by("xnT")
                        mm(m[:, 0:S], w["wqkv"][:, 0:D], xnT[1 - par][:, :])
                        ins = mm(m[:, S:2 * S], w["wqkv"][:, D:2 * D], xnT[1 - par][:, :])
                    elif name == "vq":
                        for i in range(KT):
                            mm(m[:, i * D:(i + 1) * D], xnT[1 - par][:, i * P:(i + 1) * P], w["wv_q"][:, 0:D])
                            ins = mm(m[:, S + i * D:S + (i + 1) * D], xnT[1 - par][:, i * P:(i + 1) * P], w["wv_q"][:, D:2 * D])
                    elif name == "out":
                        pe.wait_ge(ctx_moved, one_tail(kind, b, "x"))
                        nh = spr_tally("mid", 1, "shared") - spr_tally("first", 0, "shared")
                        pe.wait_ge(hid_done, nh * b)
                        for i in range(2):
                            o = m[:, i * D:(i + 1) * D]
                            mm(o, ctxT[:, i * P:(i + 1) * P], w["wout"], stop=False)
                            for k in range(NK):
                                ins = mm(o, hid[1 - par][:, k, i * P:(i + 1) * P], w["wdown"][:, k * D:(k + 1) * D],
                                         start=False, stop=(k == NK - 1))
                    elif name == "router1":
                        moved_by("xn2T")
                        for i in range(2):
                            ins = mm(m[:, i * E:(i + 1) * E], xn2T[:, i * P:(i + 1) * P], w["wrouter1"])
                    elif name == "prefix":
                        pe.wait_ge(chosen_done, one_tail(kind, b, "x"))
                        before, every = tri[:, 0:P], tri[:, P:2 * P]
                        mm(m[:, 0:E], before, chosen[:, 0, :])
                        mm(m[:, E:2 * E], before, chosen[:, 1, :], stop=False)
                        mm(m[:, E:2 * E], every, chosen[:, 0, :], start=False)
                        mm(m[:, 2 * E:3 * E], every, chosen[:, 0, :], stop=False)
                        ins = mm(m[:, 2 * E:3 * E], every, chosen[:, 1, :], start=False)
                    ins.then_inc(full[bank], 1)

                def body(kind, b, par):
                    t0 = pe.snap(b * NS) if kind == "mid" else b * NS
                    for s in steps(kind):
                        if present(kind, s, 0):
                            pe.wait_ge(built, t0 + s + 1)
                            if s == 0:
                                pe.wait_ge(q_placed, (b + 1) * (16 * QG))
                            if not (kind == "first" and s < 2):
                                pe.wait_ge(exped, t0 + s - 1)
                            for g in range(GS):
                                o = S_ps[s % 2][:, g * S:(g + 1) * S]
                                G = GS * s + g
                                off = S - QG - QG * G
                                qb, kk = q_blk[s % 2], kT[par]
                                for i, (x, y) in enumerate(((0, 0), (0, 1), (1, 0))):
                                    pe.matmul(o, qb[:, x, g, :].bitcast(F32R), kk[:, y, :].bitcast(F32R), start=(i == 0), stop=False)
                                for y in range(2):
                                    ins = pe.matmul(o, q_rel[par][:, G, :].bitcast(F32R), rel_k2[:, y, off:off + S].bitcast(F32R),
                                                    start=False, stop=(y == 1))
                            ins.then_inc(scored, 1)
                        if present(kind, s, 1) and not (kind == "end" and s >= 1):
                            r = (s - 1) % 2
                            pe.wait_ge(exped, t0 + s)
                            if not (kind == "first" and s < 3):
                                pe.wait_ge(moved, t0 + s - 2)
                            for kt in range(KT):
                                for g in range(GS):
                                    ins = pe.transpose(PT_ps[r][:, (kt * GS + g) * P:(kt * GS + g + 1) * P],
                                                       probs[r][:, g, kt * P:(kt + 1) * P], ident)
                            ins.then_inc(turned, 1)
                        if present(kind, s, 2) and not (kind == "end" and s >= 2):
                            r, sq = s % 2, (s - 2) % NS
                            vp = vf[par if s >= 2 else 1 - par]
                            pe.wait_ge(placed, t0 + s - 1)
                            if s == 2:
                                pe.wait_ge(values_placed, b + 1)
                            pe.wait_ge(moved, t0 + s - 1)
                            if not (kind == "first" and s < 3):
                                pe.wait_ge(merged, t0 + s - 2)
                            for g in range(GS):
                                G = GS * sq + g
                                for kt in range(KT):
                                    ins = pe.matmul(O_ps[:, g * OW:(g + 1) * OW], probsT[r][:, kt, g, :],
                                                    vp[:, kt, s % 2, GS - 1 - g, :], start=(kt == 0), stop=(kt == KT - 1))
                            ins.then_inc(valued, 1)
                        for name in jobs(kind, s):
                            project(kind, b, par, name)
                        if present(kind, s, 3) and not (kind == "end" and s >= 3):
                            sq = (s - 3) % NS
                            pe.wait_ge(picked, t0 + s - 2)
                            pe.wait_ge(masked, t0 + s - 2)
                            if s == 3 and "tail" in SECTIONS[kind]:
                                pe.wait_ge(ctx_moved, one_tail(kind, b, "x"))
                            for g in range(GS):
                                G = GS * sq + g
                                ins = pe.matmul(CTX_ps[:, QG * G:QG * G + QG], zz[(s - 3) % 2][:, g, :],
                                                pick[(s - 3) % 4][:, g, :], start=True, stop=True)
                            ins.then_inc(ctxed, 1)
                bodies(pe, nb, body)

        with ExitStack() as pc:
            def sc(name, shape, dt=F32):
                return pc.enter_context(nc.sbuf_tensor(name, shape, dt))

            def bank_c(name):
                return pc.enter_context(nc.psum_tensor(name, [P, 512], F32))

            T_ps = [bank_c(f"slotsT{i}") for i in range(2)]
            U_ps = [bank_c(f"up_{i}") for i in range(4)]
            Y_ps = [bank_c(f"down{i}") for i in range(2)]
            FT = FF // P
            b2 = sc("b2", [P, E, D])
            b1e = [sc(f"b1e{i}", [P, FT]) for i in range(2)]
            b1_moved = pc.enter_context(nc.semaphore("b1_moved"))
            xe = [sc(f"xe{i}", [P, JT, D]) for i in range(2)]
            w1 = [sc(f"w1_{i}", [P, FF]) for i in range(2)]
            w2 = [sc(f"w2_{i}", [P, FT, D]) for i in range(2)]
            xeT = sc("xeT", [P, cap])
            he = sc("he", [P, FT, cap])
            ye = [sc(f"ye{i}", [P, JT, D]) for i in range(2)]
            csem = {n: pc.enter_context(nc.semaphore(n + "_c")) for n in
                    ("b2_in", "in0", "in1", "out0", "out1", "tr", "tr_moved", "up", "gelu", "down", "y_moved")}
            b2_in, in0, in1, out0, out1, tr, tr_moved, up, gelu, down, y_moved = csem.values()
            loaded, stored = [in0, in1], [out0, out1]
            QT = [(j, min(4, JT - j)) for j in range(0, JT, 4)]
            NQ = len(QT)

            with nc.Block() as block:
                def experts(engine, body):
                    body(0, 0, True)
                    body(1, 1, True)
                    with engine.Fori(1, E // 2) as pair:
                        e = engine.snap(pair * 2)
                        body(e, 0, False)
                        body(e + 1, 1, False)

                packed_t = packed[0:SLOTS, :].rearrange("(e p j) d -> e p j d", p=P, j=JT)
                out_t = expert_out.rearrange("(e p j) d -> e p j d", p=P, j=JT)

                @block.sync
                def _(sp):
                    sp.dma_start(b2[:, :, :].rearrange("p e d -> p (e d)"), io["b2"].partition_broadcast(P)).then_inc(b2_in, 16)

                    def body(e, i, first):
                        if not first:
                            sp.wait_ge(down, (e - 1) * NQ)
                        sp.dma_start(xe[i][:, :, :], packed_t[bass.ds(e, 1)].rearrange("a p j d -> p (a j) d")).then_inc(loaded[i], 16)
                        sp.dma_start(w1[i][:, :], io["w1"][bass.ds(e, 1)].rearrange("a p f -> p (a f)")).then_inc(loaded[i], 16)
                        sp.dma_start(w2[i][:, :, :], io["w2"][bass.ds(e, 1)].rearrange("a (m p) d -> p (a m) d", p=P)).then_inc(loaded[i], 16)
                    experts(sp, body)

                @block.tensor
                def _(pe):
                    def body(e, i, first):
                        pe.wait_ge(loaded[i], 48 if first else e * 24 + (48 if i == 0 else 24))
                        for q, (j0, n) in enumerate(QT):
                            if not (first and i == 0 and q < 2):
                                pe.wait_ge(tr_moved, e * NQ + q - 1)
                            for j in range(n):
                                ins = pe.transpose(T_ps[(i * NQ + q) % 2][:, j * P:(j + 1) * P], xe[i][:, j0 + j, :], ident)
                            ins.then_inc(tr, 1)
                        for q, (j0, n) in enumerate(QT):
                            pe.wait_ge(tr_moved, e * NQ + q + 1)
                            for f in range(FT):
                                if not (first and i == 0 and q == 0):
                                    pe.wait_ge(gelu, (e * NQ + q) * FT + f - FT + 1)
                                pe.matmul(U_ps[f][:, 0:n * P], w1[i][:, f * P:(f + 1) * P], xeT[:, j0 * P:(j0 + n) * P],
                                          start=True, stop=True).then_inc(up, 1)
                        for q, (j0, n) in enumerate(QT):
                            pe.wait_ge(gelu, (e * NQ + q + 1) * FT)
                            if not (first and i == 0 and q < 2):
                                pe.wait_ge(y_moved, e * NQ + q - 1)
                            for j in range(n):
                                for f in range(FT):
                                    ins = pe.matmul(Y_ps[(i * NQ + q) % 2][:, j * D:(j + 1) * D],
                                                    he[:, f, (j0 + j) * P:(j0 + j + 1) * P], w2[i][:, f, :],
                                                    start=(f == 0), stop=(f == FT - 1))
                            ins.then_inc(down, 1)
                    experts(pe, body)

                @block.scalar
                def _(act):
                    def body(e, i, first):
                        for q, (j0, n) in enumerate(QT):
                            for f in range(FT):
                                act.wait_ge(up, (e * NQ + q) * FT + f + 1)
                                if q == 0 and f == 0 and not (first and i == 0):
                                    act.wait_ge(down, e * NQ)
                                act.activation(he[:, f, j0 * P:(j0 + n) * P], U_ps[f][:, 0:n * P], ACT.Gelu,
                                               bias=b1e[i][:, f:f + 1]).then_inc(gelu, 1)
                    b1v = wview["b1"].rearrange("p (e f) -> p e f", f=FT)

                    def with_bias(e, i, first):
                        act.copy(b1e[i][:, :], b1v[:, bass.ds(e, 1), :].rearrange("p a f -> p (a f)")).then_inc(b1_moved, 1)
                        act.wait_ge(b1_moved, e + 1)
                        body(e, i, first)
                    experts(act, with_bias)

                @block.vector
                def _(dve):
                    dve.wait_ge(b2_in, 16)

                    def body(e, i, first):
                        for q, (j0, n) in enumerate(QT):
                            dve.wait_ge(tr, e * NQ + q + 1)
                            if q == 0 and not (first and i == 0):
                                dve.wait_ge(up, e * NQ * FT)
                            dve.tensor_copy(xeT[:, j0 * P:(j0 + n) * P], T_ps[(i * NQ + q) % 2][:, 0:n * P]).then_inc(tr_moved, 1)
                        for q, (j0, n) in enumerate(QT):
                            dve.wait_ge(down, e * NQ + q + 1)
                            if q == 0 and not first:
                                dve.wait_ge(stored[i], e * 8 if i == 0 else (e - 1) * 8)
                            dve.tensor_tensor(ye[i][:, j0:j0 + n, :], Y_ps[(i * NQ + q) % 2][:, 0:n * D].rearrange("p (j d) -> p j d", d=D),
                                              b2[:, bass.ds(e, 1), :].to_broadcast((P, n, D)), ALU.add).then_inc(y_moved, 1)
                    experts(dve, body)

                @block.gpsimd
                def _(pool):
                    def body(e, i, first):
                        pool.wait_ge(y_moved, (e + 1) * NQ)
                        pool.dma_start(out_t[bass.ds(e, 1)].rearrange("a p j d -> p (a j) d"), ye[i][:, :, :]).then_inc(stored[i], 16)
                    experts(pool, body)
                    for i in range(2):
                        pool.wait_ge(stored[i], 16 * (E // 2))

        with ExitStack() as pb:
            def sbb(name, shape, dt=F32):
                return pb.enter_context(nc.sbuf_tensor(name, shape, dt))

            def bank_b(name):
                return pb.enter_context(nc.psum_tensor(name, [P, 512], F32))

            S_ps = [bank_b(f"scores1_{i}") for i in range(2)]
            PT_ps = [bank_b(f"probsT1_{i}") for i in range(2)]
            O_ps = bank_b("values1")
            CTX_ps = bank_b("context1")
            M_ps = [bank_b(f"spare1_{i}") for i in range(2)]
            xt = [sbb(f"xt1_{i}", [P, S]) for i in range(2)]
            qT = [sbb(f"qT1_{i}", [P, S]) for i in range(2)]
            kT = [sbb(f"kT1_{i}", [P, S]) for i in range(2)]
            vv = [sbb(f"v1_{i}", [P, KT, D]) for i in range(2)]
            q_blk = [sbb(f"q_blk1_{i}", [P, GS, P]) for i in range(2)]
            probs = [sbb(f"probs1_{i}", [P, GS, S]) for i in range(2)]
            probsT = [sbb(f"probsT1_s{i}", [P, KT, GS, P]) for i in range(2)]
            nmax = [sbb(f"nmax1_{i}", [P, GS]) for i in range(4)]
            rsum = [sbb(f"rsum1_{i}", [P, GS]) for i in range(4)]
            rinv = [sbb(f"rinv1_{i}", [P, GS]) for i in range(4)]
            pick = [sbb(f"pick1_{i}", [P, GS, QG]) for i in range(4)]
            zz = [sbb(f"zz1_{i}", [P, GS, D]) for i in range(2)]
            ctxT = sbb("ctxT1", [P, S])
            expert_rows = [sbb(f"expert_rows_{i}", [P, 2, 2, D]) for i in range(2)]
            ids = [sbb(f"ids_{i}", [P, 2, 2], U32) for i in range(2)]
            with_one = sbb("with_one", [P, 2, D])
            with_two = sbb("with_two", [P, 2, D])
            total = sbb("total", [P, 2, D])
            gathered = [pb.enter_context(nc.semaphore(f"gathered{i}")) for i in range(2)]
            written = pb.enter_context(nc.semaphore("written"))
            ids_at = pb.enter_context(nc.semaphore("ids_at"))
            bsem = {n: pb.enter_context(nc.semaphore(n + "_b")) for n in
                    ("built", "scored", "maxed", "exped", "turned", "moved", "valued", "picked", "merged",
                     "ctxed", "ctx_moved", "full0", "full1", "free0", "free1", "xt0_in", "xt1_in", "chain")}
            (built, scored, maxed, exped, turned, moved, valued, picked, merged, ctxed, ctx_moved, full0, full1,
             free0, free1, xt0_in, xt1_in, chain) = bsem.values()
            full, free, xt_in = [full0, full1], [free0, free1], [xt0_in, xt1_in]
            bank_of = {name: i % 2 for i, (_, name, _) in enumerate(JOBS_B)}
            bank_tally = [Tally(nb, [(n, s) for _, n, s in JOBS_B if bank_of[n] == i]) for i in range(2)]
            one_front = Tally(nb, [("x", "front")])
            one_tail = Tally(nb, [("x", "tail")])

            def jobs(kind, step):
                return [n for s, n, sec in JOBS_B if s == step and sec in SECTIONS[kind]]

            def present(kind, s, lag):
                return kind in (("first", "mid", "last") if s >= lag else ("mid", "last", "end"))

            def ktiles(s):
                return (GS * QG * (s % NS + 1) - 1) // P + 1

            block = pb.enter_context(nc.Block())

            @block.sync
            def _(sp):
                def body(kind, b, par):
                    if "front" in SECTIONS[kind]:
                        if kind == "mid":
                            sp.wait_ge(scored, b * NS)
                        sp.dma_start(xt[1 - par][:, :], xnT1[bass.ds(b + 1, 1)].rearrange("a p s -> p (a s)")).then_inc(xt_in[1 - par], 16)
                    if "tail" in SECTIONS[kind]:
                        bank = bank_of["out"]
                        sp.wait_ge(free[bank], bank_tally[bank](kind, b, "out"))
                        sp.dma_start(io["out"].rearrange("(b i p) d -> b p i d", i=2, p=P)[bass.ds(b - 1, 1)]
                                     .rearrange("a p i d -> p (a i) d"), total[:, :, :]).then_inc(written, 16)
                sp.dma_start(total[:, :, :], io["x"][0:2 * P, :].rearrange("(i p) d -> p i d", p=P)).then_inc(written, 16)
                bodies(sp, nb, body)
                sp.wait_ge(written, 16 * nb + 16)

            @block.gpsimd
            def _(pool):
                def build(s, par):
                    pool.tensor_tensor(q_blk[s % 2][:, :, :].rearrange("p g (q h) -> p (g q) h", h=H),
                                       qT[par][:, 16 * s:16 * s + 16].unsqueeze(2).to_broadcast((P, 16, H)),
                                       cview["mask_head_rows"].unsqueeze(1).to_broadcast((P, 16, H)), ALU.mult).then_inc(built, 1)

                def body(kind, b, par):
                    t0 = pool.snap(b * NS) if kind == "mid" else b * NS
                    if kind == "pro":
                        pool.wait_ge(free[bank_of["qk"]], bank_tally[bank_of["qk"]](kind, b, "qk"))
                        build(0, 0)
                        return
                    if kind == "end":
                        return
                    for s in range(NS):
                        if s == 1:
                            pool.wait_ge(maxed, t0 + 1)
                        if not (kind == "last" and s == NS - 1):
                            if s == NS - 1:
                                pool.wait_ge(free[bank_of["qk"]], bank_tally[bank_of["qk"]](kind, b, "qk"))
                            if not (kind == "first" and s == 0):
                                pool.wait_ge(scored, t0 + s)
                            build((s + 1) % NS, par if s < NS - 1 else 1 - par)
                        if s == 1:
                            pool.sem_clear(ids_at)
                            pool.tensor_copy(ids[par][:, :, :], slot_ids[:, bass.ds(b * 2, 2), :]).then_inc(ids_at, 1)
                            pool.wait_ge(ids_at, 1)
                        if 1 <= s <= 4:
                            i, k = (s - 1) // 2, (s - 1) % 2
                            pool.indirect_dma_start(out=expert_rows[par][:, i, k, :], out_offset=None, in_=expert_out,
                                                    in_offset=bass.IndirectOffsetOnAxis(ap=ids[par][:, i, k:k + 1], axis=0)
                                                    ).then_inc(gathered[par], 16)
                bodies(pool, nb, body)

            @block.scalar
            def _(act):
                def move(kind, b, par, name):
                    bank = bank_of[name]
                    m, n = M_ps[bank], bank_tally[bank](kind, b, name)
                    if name == "qk":
                        act.wait_ge(full[bank], n)
                        act.mul(qT[1 - par][:, :], m[:, 0:S], C ** -0.5)
                        act.copy(kT[1 - par][:, :], m[:, S:2 * S]).then_inc(free[bank], 1)
                    elif name == "v":
                        act.wait_ge(full[bank], n)
                        act.copy(vv[1 - par][:, :, :].rearrange("p a d -> p (a d)"), m[:, 0:S]).then_inc(free[bank], 1)

                def body(kind, b, par):
                    t0 = act.snap(b * NS) if kind == "mid" else b * NS
                    for s in range(NS):
                        if s:
                            for name in jobs(kind, s - 1):
                                move(kind, b, par, name)
                        if s == 3 and "tail" in SECTIONS[kind]:
                            act.wait_ge(ctxed, t0)
                            act.copy(ctxT[:, :], CTX_ps[:, 0:S]).then_inc(ctx_moved, 1)
                        if present(kind, s, 0):
                            w = ktiles(s) * P
                            act.wait_ge(maxed, t0 + s + 1)
                            for g in range(GS):
                                ins = act.activation(probs[s % 2][:, g, 0:w], S_ps[s % 2][:, g * w:(g + 1) * w], ACT.Exp,
                                                     bias=nmax[s % 4][:, g:g + 1], accum_out=rsum[s % 4][:, g:g + 1])
                            ins.then_inc(exped, 1)
                        if present(kind, s, 1) and not (kind == "end" and s >= 1):
                            w = ktiles(s - 1) * GS * P
                            act.wait_ge(turned, t0 + s)
                            act.copy(probsT[(s - 1) % 2][:, :, :, :].rearrange("p a b c -> p (a b c)")[:, 0:w],
                                     PT_ps[(s - 1) % 2][:, 0:w]).then_inc(moved, 1)
                bodies(act, nb, body)

            @block.vector
            def _(dve):
                links = [0]

                def link(ins):
                    links[0] += 1
                    ins.then_inc(chain, 1)
                    dve.wait_ge(chain, links[0])

                def body(kind, b, par):
                    t0 = dve.snap(b * NS) if kind == "mid" else b * NS
                    dve.sem_clear(chain)
                    links[0] = 0
                    for s in range(NS):
                        if present(kind, s, 0):
                            w = ktiles(s) * P
                            dve.wait_ge(scored, t0 + s + 1)
                            dve.tensor_reduce(nmax[s % 4][:, :], S_ps[s % 2][:, 0:GS * w].rearrange("p (g k) -> p g k", g=GS),
                                              AX.X, ALU.max, negate=True).then_inc(maxed, 1)
                        if present(kind, s, 1) and not (kind == "end" and s >= 1):
                            r = (s - 1) % 4
                            dve.wait_ge(exped, t0 + s)
                            link(dve.reciprocal(rinv[r][:, :], rsum[r][:, :]))
                            dve.tensor_tensor(pick[r][:, :, :], cview["pick_query"].unsqueeze(1).to_broadcast((P, GS, QG)),
                                              rinv[r][:, :].unsqueeze(2).to_broadcast((P, GS, QG)), ALU.mult).then_inc(picked, 1)
                        if present(kind, s, 2) and not (kind == "end" and s >= 2):
                            dve.wait_ge(valued, t0 + s - 1)
                            dve.tensor_tensor(zz[s % 2][:, :, :].rearrange("p g (h c) -> p g h c", c=C),
                                              O_ps[:, 0:GS * D].rearrange("p (g h c) -> p g h c", g=GS, c=C),
                                              cview["mask_head"].unsqueeze(1).unsqueeze(3).to_broadcast((P, GS, H, C)),
                                              ALU.mult).then_inc(merged, 1)
                        if s == 4 and "tail" in SECTIONS[kind]:
                            dve.wait_ge(gathered[1 - par], (b - 2 + par) * 32 + 64)
                            er = expert_rows[1 - par]
                            for i in range(2):
                                w = slot_w[:, bass.ds((b - 1) * 2 + i, 1), :].rearrange("p a k -> p (a k)")
                                ins = dve.scalar_tensor_tensor(with_one[:, i, :], er[:, i, 0, :], w[:, 0:1],
                                                               residual[:, bass.ds((b - 1) * 2 + i, 1), :].rearrange("p a d -> p (a d)"),
                                                               ALU.mult, ALU.add)
                            link(ins)
                            for i in range(2):
                                w = slot_w[:, bass.ds((b - 1) * 2 + i, 1), :].rearrange("p a k -> p (a k)")
                                ins = dve.scalar_tensor_tensor(with_two[:, i, :], er[:, i, 1, :], w[:, 1:2],
                                                               with_one[:, i, :], ALU.mult, ALU.add)
                            link(ins)
                        if s and "out" in jobs(kind, s - 1):
                            bank = bank_of["out"]
                            dve.wait_ge(full[bank], bank_tally[bank](kind, b, "out"))
                            dve.wait_ge(written, 16 * one_tail(kind, b, "x"))
                            dve.tensor_tensor(total[:, :, :], M_ps[bank][:, 0:S].rearrange("p (a d) -> p a d", a=2),
                                              with_two[:, :, :], ALU.add).then_inc(free[bank], 1)
                bodies(dve, nb, body)

            @block.tensor
            def _(pe):
                def project(kind, b, par, name):
                    bank = bank_of[name]
                    m, n = M_ps[bank], bank_tally[bank](kind, b, name)
                    if not (isinstance(n, int) and n == 1):
                        pe.wait_ge(free[bank], n - 1)
                    if name == "qk":
                        pe.wait_ge(xt_in[1 - par], 16 if kind in ("pro", "first") else 8 * b + 16 + 8 * par)
                        pe.matmul(m[:, 0:S], wview["q1"], xt[1 - par][:, :], start=True, stop=True)
                        ins = pe.matmul(m[:, S:2 * S], wview["k1"], xt[1 - par][:, :], start=True, stop=True)
                    elif name == "v":
                        for i in range(KT):
                            ins = pe.matmul(m[:, i * D:(i + 1) * D], xt[1 - par][:, i * P:(i + 1) * P], wview["v1"],
                                            start=True, stop=True)
                    elif name == "out":
                        pe.wait_ge(ctx_moved, one_tail(kind, b, "x"))
                        for i in range(2):
                            ins = pe.matmul(m[:, i * D:(i + 1) * D], ctxT[:, i * P:(i + 1) * P], wview["o1"],
                                            start=True, stop=True)
                    ins.then_inc(full[bank], 1)

                def body(kind, b, par):
                    t0 = pe.snap(b * NS) if kind == "mid" else b * NS
                    for s in range(NS):
                        if present(kind, s, 0):
                            w = ktiles(s) * P
                            pe.wait_ge(built, t0 + s + 1)
                            if not (kind == "first" and s < 2):
                                pe.wait_ge(exped, t0 + s - 1)
                            for g in range(GS):
                                o = S_ps[s % 2][:, g * w:(g + 1) * w]
                                off = S - QG - QG * (GS * s + g)
                                pe.matmul(o, q_blk[s % 2][:, g, :], kT[par][:, 0:w], start=True, stop=False)
                                ins = pe.matmul(o, alibi_l[:, :], alibi_r[:, off:off + w], start=False, stop=True)
                            ins.then_inc(scored, 1)
                        if present(kind, s, 1) and not (kind == "end" and s >= 1):
                            r = (s - 1) % 2
                            pe.wait_ge(exped, t0 + s)
                            if not (kind == "first" and s < 3):
                                pe.wait_ge(moved, t0 + s - 2)
                            for kt in range(ktiles(s - 1)):
                                for g in range(GS):
                                    ins = pe.transpose(PT_ps[r][:, (kt * GS + g) * P:(kt * GS + g + 1) * P],
                                                       probs[r][:, g, kt * P:(kt + 1) * P], ident)
                            ins.then_inc(turned, 1)
                        if present(kind, s, 2) and not (kind == "end" and s >= 2):
                            r, n = s % 2, ktiles(s - 2)
                            vp = vv[par if s >= 2 else 1 - par]
                            if s == 2:
                                bank = bank_of["v"]
                                tl = bank_tally[bank]
                                if kind == "first":
                                    pe.wait_ge(free[bank], tl("pro", -1, "v"))
                                elif kind == "last":
                                    pe.wait_ge(free[bank], tl("mid", b - 1, "v"))
                                else:
                                    pe.wait_ge(free[bank], tl("mid", b, "v") - tl.total("mid"))
                            pe.wait_ge(moved, t0 + s - 1)
                            if not (kind == "first" and s < 3):
                                pe.wait_ge(merged, t0 + s - 2)
                            for g in range(GS):
                                for kt in range(n):
                                    ins = pe.matmul(O_ps[:, g * D:(g + 1) * D], probsT[r][:, kt, g, :], vp[:, kt, :],
                                                    start=(kt == 0), stop=(kt == n - 1))
                            ins.then_inc(valued, 1)
                        for name in jobs(kind, s):
                            project(kind, b, par, name)
                        if present(kind, s, 3) and not (kind == "end" and s >= 3):
                            sq = (s - 3) % NS
                            pe.wait_ge(picked, t0 + s - 2)
                            pe.wait_ge(merged, t0 + s - 2)
                            if s == 3 and "tail" in SECTIONS[kind]:
                                pe.wait_ge(ctx_moved, one_tail(kind, b, "x"))
                            for g in range(GS):
                                G = GS * sq + g
                                ins = pe.matmul(CTX_ps[:, QG * G:QG * G + QG], zz[(s - 3) % 2][:, g, :],
                                                pick[(s - 3) % 4][:, g, :], start=True, stop=True)
                            ins.then_inc(ctxed, 1)
                bodies(pe, nb, body)


def shape_constants(nb, cap):
    T = nb * S
    p = np.arange(P)
    c = {
        "ident": np.eye(P),
        "mask_head_rows": p[:, None] // C == np.arange(H),
        "mask_head": p[:, None] % H == np.arange(H),
        "mask_query": p[:, None] // H == QG - 1 - np.arange(QG),
        "pick_query": p[:, None] // H == np.arange(QG),
        "iota": np.broadcast_to(np.arange(E), (P, E)),
        "dump": (E * cap + p[:, None, None] + P * np.arange(2)[None, :, None] + T * np.arange(2)[None, None, :]).reshape(P, 4),
    }
    consts = np.concatenate([np.asarray(c[n], np.float32) for n in CONSTS], axis=1)
    spread = np.tile(0.5 * (np.arange(E * HID)[None, :] // HID == np.arange(E)[:, None]), (2, 1))
    tri = np.concatenate([p[:, None] < p[None, :], np.ones((P, P))], axis=1)
    ratio = 2.0 ** (-8.0 / H)
    slopes = np.asarray([ratio ** (i + 1) for i in range(H)], np.float32)
    parts, rest = [], slopes.astype(np.float64)
    for _ in range(3):
        part = (rest.astype(np.float32).view(np.uint32) & np.uint32(0xFFFF0000)).view(np.float32).astype(np.float64)
        parts.append(part)
        rest = rest - part
    own = np.arange(QG)[:, None] == p[None, :] // H
    alibi_l = np.concatenate([own * np.tile(part, QG)[None, :] for part in parts], axis=0)
    j = np.arange(2 * S - QG)
    dist = j[None, :] - (S - QG) - np.arange(QG)[:, None]
    alibi_r = np.tile(np.where(dist <= 0, dist, -1e30), (3, 1))
    named = {"consts": consts, "spread": spread, "tri": tri, "alibi_l": alibi_l, "alibi_r": alibi_r}
    return {n: v.astype(np.float32) for n, v in named.items()}


def capacity(tokens):
    return max(1, int(math.ceil(1.25 * tokens * 2 / E)))


def kernel(**inputs):
    import concourse.bacc as bacc
    from concourse.bass_utils import run_bass_kernel_spmd

    a = {k: np.asarray(v) for k, v in inputs.items()}
    nb = a["L0_attn_x"].shape[0]
    T = nb * S
    cap = capacity(T)
    wqkv, bqkv = a["L0_attn_W_qkv"], a["L0_attn_b_qkv"]
    w = {
        "wqkv": wqkv,
        "wv_q": np.concatenate([wqkv[:, 2 * D:], wqkv[:, 0:D].reshape(D, H, C).transpose(0, 2, 1).reshape(D, D)], axis=1),
        "wout": a["L0_attn_W_out"],
        "wgate": np.concatenate([a["L0_ffn_We_gate"].reshape(E * HID, D), a["L0_ffn_Ws_gate"]], axis=0).T,
        "wup": np.concatenate([a["L0_ffn_We_up"].reshape(E * HID, D), a["L0_ffn_Ws_up"]], axis=0).T,
        "wdown": np.concatenate([a["L0_ffn_We_down"].transpose(0, 2, 1).reshape(E * HID, D), a["L0_ffn_Ws_down"].T],
                                axis=0).reshape(NK, P, D).transpose(1, 0, 2).reshape(P, NK * D),
        "wrouter0": a["L0_ffn_Wg"].T,
        "wshared_gate": a["L0_ffn_Wsg"].T,
        "bq": bqkv[0:D].reshape(P, 1),
        "bk": bqkv[D:2 * D].reshape(P, 1),
        "q1": a["L1_attn_q_w"], "k1": a["L1_attn_k_w"], "v1": a["L1_attn_v_w"], "o1": a["L1_attn_o_w"],
        "wrouter1": a["L1_ffn_router_w"].T,
        "b1": a["L1_ffn_b1"].reshape(E, FF // P, P).transpose(2, 0, 1).reshape(P, -1),
    }
    arrays = {
        "x": a["L0_attn_x"].reshape(T, D),
        "weights": np.concatenate([w[n] for n in WEIGHTS], axis=1),
        "rows": np.concatenate([bqkv[2 * D:3 * D], bqkv[0:D].reshape(H, C).T.reshape(-1), a["L0_attn_b_out"], a["L1_ffn_router_b"]]),
        "rel_k": a["L0_attn_rel_emb_k"].T,
        "rel_v": a["L0_attn_rel_emb_v"],
        "w1": a["L1_ffn_w1"], "w2": a["L1_ffn_w2"], "b2": a["L1_ffn_b2"].reshape(-1),
        **shape_constants(nb, cap),
    }
    arrays = {"in_" + k: np.ascontiguousarray(v) for k, v in arrays.items()}
    nc = bacc.Bacc("TRN2", target_bir_lowering=False, num_devices=1)
    io = {k[3:]: nc.dram_tensor(k, v.shape, mybir.dt.from_np(v.dtype), kind="ExternalInput").ap() for k, v in arrays.items()}
    io["out"] = nc.dram_tensor("out_0", (T, D), F32, kind="ExternalOutput").ap()
    program(nc, io, nb, cap)
    r = run_bass_kernel_spmd(nc, [arrays], core_ids=[0])
    return r.results[0]["out_0"].reshape(nb, S, D)
```

```python
import math
from contextlib import ExitStack

import numpy as np
import concourse.bass as bass
from concourse import mybir
from concourse.alu_op_type import AluOpType as ALU

F32 = mybir.dt.float32
BF16 = mybir.dt.bfloat16
F32R = mybir.dt.float32r
I32 = mybir.dt.int32
U32 = mybir.dt.uint32
ACT = mybir.ActivationFunctionType
AX = mybir.AxisListType

P = 128
S = 256
D = 128
H = 16
C = 8
R = 64
QG = 8
GS = 2
NS = S // (QG * GS)
KT = S // P
E = 16
HID = 64
SH = 256
NK = E * HID // P + SH // P
FF = 512
EPS = 1e-5
MAGIC = 0x5F3759DF
OW = D + QG * C

CONSTS = {"ident": P, "mask_head_rows": H, "mask_head": H, "mask_query": QG,
          "pick_query": QG, "head_channels": D, "iota": E, "dump": 4}
NCONST = sum(CONSTS.values())
WEIGHTS = {"wqkv": 3 * D, "wv_q": 2 * D, "wout": D, "wdown": NK * D,
           "wrouter0": E, "wshared_gate": 1, "bq": 1, "bk": 1, 
           "q1": D, "k1": D, "v1": D, "o1": D, "wrouter1": E, "b1": E * FF // P}
NWEIGHT = sum(WEIGHTS.values())
ROWS = {"bv": D, "bq_row": D, "bout": D, "brouter1": E}
NROW = sum(ROWS.values())

JOBS_A = [(0, "router0", "mid"), (0, "up0", "mid"), (1, "up1", "mid"), (2, "up2", "mid"), (3, "gateT", "mid"), (3, "up3", "mid"),
          (4, "xnT", "front"), (4, "up4", "mid"), (5, "out", "tail"), (6, "spread0", "mid"), (6, "qk", "front"),
          (7, "up5", "mid"), (7, "vq", "front"), (8, "xn2T", "tail"), (8, "spread1", "mid"), (9, "router1", "tail"),
          (9, "up6", "mid"), (10, "up7", "mid"), (11, "prefix", "tail"), (11, "spread2", "mid"), (12, "up8", "mid"),
          (13, "spread3", "mid"), (13, "up9", "mid"), (14, "shared", "mid")]
JOBS_B = [(5, "out", "tail"), (8, "qk", "front"), (9, "v", "front")]

SECTIONS = {"pro": {"front"}, "first": {"mid", "front"}, "mid": {"tail", "mid", "front"},
            "last": {"tail", "mid"}, "end": {"tail"}}


class Tally:

    def __init__(self, nb, events):
        self.nb, self.events = nb, events

    def total(self, kind):
        return sum(s in SECTIONS[kind] for _, s in self.events)

    def __call__(self, kind, b, name):
        present = [n for n, s in self.events if s in SECTIONS[kind]]
        rank = present.index(name) + 1
        if kind == "pro":
            return rank
        if kind == "first":
            return rank + self.total("pro")
        base = rank + self.total("pro") + self.total("first")
        if kind == "end":
            return base + self.total("mid") * (self.nb - 2) + self.total("last")
        return (b - 1) * self.total("mid") + base


def bodies(engine, nb, body):
    body("pro", -1, 1)
    body("first", 0, 0)
    with engine.Fori(0, (nb - 2) // 2) as i:
        b = engine.snap(2 * i + 1)
        body("mid", b, 1)
        body("mid", b + 1, 0)
    body("last", nb - 1, 1)
    body("end", nb, 0)


def program(nc, io, nb, cap):
    T = nb * S
    NT = T // P
    SLOTS = E * cap
    JT = cap // P
    ctx = ExitStack()
    with ctx:
        def sb(name, shape, dt=F32):
            return ctx.enter_context(nc.sbuf_tensor(name, shape, dt))

        def sem(name):
            return ctx.enter_context(nc.semaphore(name))

        packed = nc.dram_tensor("packed", (SLOTS + 2 * T, D), F32).ap()
        expert_out = nc.dram_tensor("expert_out", (SLOTS, D), F32).ap()
        xnT1 = nc.dram_tensor("xnT1", (nb, P, S), F32).ap()
        NU = 2 * S - 1
        rel_k_ext = nc.dram_tensor("rel_k_ext", (C, NU), F32).ap()
        q_rows = nc.dram_tensor("q_rows", (S, 2 * D), F32).ap()
        rel_v_ext = nc.dram_tensor("rel_v_ext", (NU, C), F32).ap()

        consts = sb("consts", [P, NCONST])
        weights = sb("weights", [P, NWEIGHT])
        rows = sb("rows", [P, NROW])
        cview, at = {}, 0
        for name, n in CONSTS.items():
            cview[name] = consts[:, at:at + n]
            at += n
        wview, at = {}, 0
        for name, n in WEIGHTS.items():
            wview[name] = weights[:, at:at + n]
            at += n
        rview, at = {}, 0
        for name, n in ROWS.items():
            rview[name] = rows[:, at:at + n]
            at += n
        ident = cview["ident"]
        spread = sb("spread", [2 * E, E * HID])
        tri = sb("tri", [P, 2 * P], BF16)
        alibi_l = sb("alibi_l", [3 * QG, P], BF16)
        alibi_r = sb("alibi_r", [3 * QG, S - QG + S], BF16)
        residual = sb("residual", [P, NT, D])
        slot_ids = sb("slot_ids", [P, NT, 2], U32)
        slot_w = sb("slot_w", [P, NT, 2])

        load_sem = sem("load")
        x_first = sem("x_first")
        x_rest = sem("x_rest")
        zeroed = sem("zeroed")

        with ExitStack() as pa:
            def sa(name, shape, dt=F32):
                return pa.enter_context(nc.sbuf_tensor(name, shape, dt))

            def pa_bank(name):
                return pa.enter_context(nc.psum_tensor(name, [P, 512], F32))

            S_ps = [pa_bank(f"scores{i}") for i in range(2)]
            PT_ps = [pa_bank(f"probsT{i}") for i in range(2)]
            O_ps = pa_bank("values")
            CTX_ps = pa_bank("context")
            M_ps = [pa_bank(f"spare{i}") for i in range(2)]

            rel_k2 = sa("rel_k2", [P, 2, 2 * S - QG])
            rel_v = sa("rel_v", [P, (S + P) // QG, QG * C])
            wshared = sa("wshared", [P, P])
            bq_s = sa("bq_s", [P, 1])
            bq_row_s = sa("bq_row_s", [P, D])
            ffn2 = sa("ffn2", [P, 2, 2 * NK * P])
            xnT = [sa(f"xnT_{i}", [P, S]) for i in range(2)]
            xnT2 = [sa(f"xnT_parts{i}", [P, 2, S]) for i in range(2)]
            qT = [sa(f"qT_{i}", [P, 2, S]) for i in range(2)]
            kT = [sa(f"kT_{i}", [P, 2, S]) for i in range(2)]
            v_new = sa("v_new", [P, KT, D])
            q_row = sa("q_row", [P, 2, D])
            q_row2 = sa("q_row2", [P, 2, 2, D])
            q_rel = [sa(f"q_rel_{i}", [P, S // QG, P]) for i in range(2)]
            vf = [sa(f"vf_{i}", [P, KT, 2, GS, OW]) for i in range(2)]
            hid = [sa(f"hid_{i}", [P, NK, S]) for i in range(2)]
            xn = sa("xn", [P, 2, D])
            q_blk = [sa(f"q_blk_{i}", [P, 2, GS, P]) for i in range(2)]
            probs = [sa(f"probs_{i}", [P, GS, S]) for i in range(2)]
            probsT = [sa(f"probsT_s{i}", [P, KT, GS, P]) for i in range(2)]
            nmax = [sa(f"nmax_{i}", [P, GS]) for i in range(4)]
            rsum = [sa(f"rsum_{i}", [P, GS]) for i in range(4)]
            rinv = [sa(f"rinv_{i}", [P, GS]) for i in range(4)]
            pick = [sa(f"pick_{i}", [P, GS, QG]) for i in range(8)]
            rel_m = [sa(f"rel_m_{i}", [P, GS, QG, C]) for i in range(2)]
            rel_s = [sa(f"rel_s_{i}", [P, GS, C]) for i in range(2)]
            z1 = [sa(f"z1_{i}", [P, GS, D]) for i in range(2)]
            zz = [sa(f"zz_{i}", [P, GS, D]) for i in range(2)]
            ctxT = sa("ctxT", [P, S])
            th = [sa(f"th_{i}", [P, S]) for i in range(2)]
            ga = sa("ga", [P, S])
            gate_bc = [sa(f"gate_bc_{i}", [P, 2, S]) for i in range(2)]
            shared_th = sa("shared_th", [P, S])
            gates = sa("gates", [P, 2, E])
            gates2 = sa("gates2", [P, 2, 2, E])
            gatesT = sa("gatesT", [2 * E, S])
            x1 = sa("x1", [P, 2, D])
            xn2 = sa("xn2", [P, 2, D])
            xn2T = sa("xn2T", [P, S])
            stats = sa("stats", [P, 2, 6])
            mv = sa("mv", [P, 2, 2])
            nw = sa("nw", [P, 5, 2])
            top = [{n: sa(f"{n}_{i}", sh, dt) for n, sh, dt in
                    (("seen", [P, 2, E], F32), ("logit", [P, 2, E], F32), ("m8", [P, 2, 8], F32), ("i8", [P, 2, 8], U32), ("idx", [P, 2, 2], F32),
                     ("gap", [P, 2], F32), ("ex", [P, 2], F32), ("den", [P, 2], F32), ("g", [P, 2, 2], F32),
                     ("oh", [P, 2, 2, E], F32), ("t0", [P, 2, E], F32), ("t1", [P, 2, E], F32))} for i in range(2)]
            chosen = sa("chosen", [P, 2, E], BF16)
            counts = sa("counts", [P, E])
            before = sa("before", [P, 3, E])
            pos = sa("pos", [P, 2, E])
            posk = sa("posk", [P, 2, 2, E])
            pk = sa("pk", [P, 2, 2])
            kept = sa("kept", [P, 2, 2])
            slot = sa("slot", [P, 2, 2])
            sk = sa("sk", [P, 2, 2])
            dumpk = sa("dumpk", [P, 2, 2])
            dump_at = sa("dump_at", [P, 2, 2])
            gk = sa("gk", [P, 2, 2])
            gden = sa("gden", [P, 2])
            scat_f = sa("scat_f", [P, 2, 2])
            scat = sa("scat", [P, 2, 2], U32)
            zeros = hid[1]
            free_hid = hid[0][:, :, :].rearrange("p a b -> p (a b)")
            ffn_in = hid[1][:, :, :].rearrange("p a b -> p (a b)")
            free_gate = gate_bc[0][:, :, :].rearrange("p a b -> p (a b)")
            W = 2 * S - QG
            at = E * HID
            spread_f = free_hid[0:2 * E, 0:at]
            rel_k_row = free_hid[0:C, at:at + NU]
            rel_k = free_hid[:, at + NU + 1:at + NU + 1 + W]
            alibi_rf = free_hid[0:3 * QG, at + NU + 1 + W:at + NU + 1 + 2 * W]
            tri_f = free_gate[:, 0:2 * P]
            alibi_lf = free_gate[0:3 * QG, 2 * P:3 * P]

            cleared = sem("zeros_cleared")
            act_ready = sem("biases_scaled")
            dve_ready = sem("weights_prepared")
            ffn_loaded = sem("ffn_loaded")
            ffn_split = sem("ffn_split")
            split_ready = sem("relative_keys_split")
            built = sem("queries_built")
            scored = sem("scores_ready")
            maxed = sem("max_ready")
            exped = sem("probs_ready")
            turned = sem("probsT_ready")
            moved = sem("probsT_moved")
            inverted = sem("inverse_sums_ready")
            valued = sem("values_ready")
            picked = sem("pick_ready")
            merged = sem("z1_ready")
            masked = sem("z_ready")
            ctxed = sem("context_done")
            ctx_moved = sem("context_moved")
            full = [sem("spare0_full"), sem("spare1_full")]
            free = [sem("spare0_free"), sem("spare1_free")]
            th_done = sem("tanh_done")
            uppers_done = sem("upper_parts_done")
            xn_uppers = sem("xn_upper_part_done")
            values_done = sem("values_done")
            values_placed = sem("values_placed")
            q_split = sem("query_rows_split")
            q_stored = sem("query_rows_stored")
            q_placed = sem("query_blocks_placed")
            q_zeroed = sem("query_blocks_zeroed")
            placed = sem("relative_values_placed")
            hid_done = sem("hidden_done")
            xn_done = sem("xn_done")
            gates_done = sem("gates_done")
            gap_done = sem("gap_done")
            ex_done = sem("ex_done")
            xn2_done = sem("xn2_done")
            chosen_done = sem("chosen_done")
            xnT1_stored = sem("xnT1_stored")
            slots_done = sem("slots_done")
            scattered = sem("scattered")
            rows_known = sem("rows_known")
            chain = sem("dve_chain")
            ext_sem = sem("ext")
            row_sem = sem("row_loaded")
            row_extended = sem("row_extended")

            bank_of = {name: i % 2 for i, (_, name, _) in enumerate(JOBS_A)}
            bank_events = [[(n, s) for _, n, s in JOBS_A if bank_of[n] == i] for i in range(2)]
            bank_tally = [Tally(nb, ev) for ev in bank_events]
            ups = [(n, s) for _, n, s in JOBS_A if n.startswith("up")]
            th_tally = Tally(nb, ups)
            spr_tally = Tally(nb, [(n, s) for _, n, s in JOBS_A if n.startswith("spread") or n == "shared"])
            one_front = Tally(nb, [("x", "front")])
            one_tail = Tally(nb, [("x", "tail")])
            one_mid = Tally(nb, [("x", "mid")])
            two = Tally(nb, [("router0", "mid"), ("router1", "tail")])
            idx_of = {n: i for i, (_, n, _) in enumerate(JOBS_A)}

            def jobs(kind, step):
                return [n for s, n, sec in JOBS_A if s == step and sec in SECTIONS[kind]]

            def present(kind, s, lag):
                return kind in (("first", "mid", "last") if s >= lag else ("mid", "last", "end"))

            def steps(kind):
                return range(NS)

            block = pa.enter_context(nc.Block())

            @block.sync
            def _(sp):
                sp.dma_start(residual[:, 0:4, :], io["x"][0:512, :].rearrange("(n p) d -> p n d", p=P)).then_inc(x_first, 16)
                sp.dma_start(consts[:, :], io["consts"]).then_inc(load_sem, 16)
                sp.dma_start(weights[:, :], io["weights"]).then_inc(load_sem, 16)
                sp.dma_start(rows[:, :], io["rows"].partition_broadcast(P)).then_inc(load_sem, 16)
                sp.dma_start(spread_f[:, :], io["spread"]).then_inc(load_sem, 16)
                sp.dma_start(tri_f[:, :], io["tri"]).then_inc(load_sem, 16)
                sp.dma_start(alibi_lf[:, :], io["alibi_l"]).then_inc(load_sem, 16)
                sp.dma_start(alibi_rf[:, :], io["alibi_r"]).then_inc(load_sem, 16)
                lo, n = S - 1 - R, 2 * R + 1
                ek, ev = io["rel_k"], io["rel_v"]
                sp.dma_start(rel_k_row[:, lo:lo + n], ek).then_inc(row_sem, 16)
                sp.dma_start(rel_v_ext[lo:lo + n, :], ev).then_inc(ext_sem, 16)
                sp.dma_start(rel_v_ext[0:lo, :], ev[0:1, :].to_broadcast((lo, C))).then_inc(ext_sem, 16)
                sp.dma_start(rel_v_ext[lo + n:NU, :], ev[n - 1:n, :].to_broadcast((lo, C))).then_inc(ext_sem, 16)
                sp.wait_ge(row_extended, 2)
                sp.dma_start(rel_k_ext, rel_k_row[:, :]).then_inc(ext_sem, 16)
                sp.wait_ge(ext_sem, 64)
                for q in range(QG):
                    for part in range(2):
                        p0 = (2 * q + part) * C
                        sp.dma_start(rel_k[p0:p0 + C, :], rel_k_ext[:, QG - 1 - q:QG - 1 - q + W]).then_inc(load_sem, 16)
                sp.dma_start(rel_v[:, :, :].rearrange("p u w -> p (u w)"),
                             bass.AP(tensor=rel_v_ext.tensor, offset=0, ap=[[C, P], [1, (S + P) * C]])).then_inc(load_sem, 16)
                sp.dma_start(ffn_in, io["ffn_in"]).then_inc(ffn_loaded, 16)
                sp.wait_ge(q_zeroed, 2)

                def body(kind, b, par):
                    if "front" in SECTIONS[kind]:
                        place_queries(kind, b, par)
                    if kind == "pro":
                        load_rest()
                    if "tail" in SECTIONS[kind]:
                        bank = bank_of["xn2T"]
                        sp.wait_ge(free[bank], bank_tally[bank](kind, b, "xn2T"))
                        sp.dma_start(xnT1[bass.ds(b - 1, 1)].rearrange("a p s -> p (a s)"), xn2T[:, :]).then_inc(xnT1_stored, 16)

                def load_rest():
                    for n in range(4, NT, 4):
                        m = min(4, NT - n)
                        sp.dma_start(residual[:, n:n + m, :],
                                     io["x"][P * n:P * (n + m), :].rearrange("(n p) d -> p n d", p=P)).then_inc(x_rest, 16)
                    sp.wait_ge(cleared, 1)
                    nz = NK * S // D * P
                    flat = zeros[:, :, :].rearrange("p a b -> p (a b)")
                    for r0 in range(0, SLOTS, nz):
                        m = min(nz, SLOTS - r0)
                        sp.dma_start(packed[r0:r0 + m, :].rearrange("(p a) d -> p (a d)", p=P),
                                     flat[:, 0:m // P * D]).then_inc(zeroed, 16)

                def place_queries(kind, b, par):
                    sp.wait_ge(q_split, one_front(kind, b, "x"))
                    sp.dma_start(q_rows.rearrange("(i p) w -> p i w", p=P),
                                 q_row2[:, :, :, :].rearrange("p i k w -> p i (k w)")).then_inc(q_stored, 16)
                    sp.wait_ge(q_stored, (b + 2) * 16)
                    for q in range(QG):
                        sp.dma_start(q_rel[1 - par][2 * C * q:2 * C * (q + 1), :, H * q:H * (q + 1)],
                                     bass.AP(tensor=q_rows.tensor, offset=q * 2 * D,
                                             ap=[[H, 2 * C], [QG * 2 * D, S // QG], [1, H]])).then_inc(q_placed, 16)
                sp.dma_start(xn2T[:, :], io["x"][0:2 * P, :].rearrange("(p a) d -> p (a d)", a=2)).then_inc(xnT1_stored, 16)
                bodies(sp, nb, body)
                sp.wait_ge(xnT1_stored, 16 * nb + 16)
            LOADS = 16 * (7 + 2 * QG + 1)
            NZERO = 16 * -(-SLOTS // (NK * S // D * P))
            XREST = 16 * len(range(4, NT, 4))

            @block.gpsimd
            def _(pool):
                for i in range(2):
                    pool.memset(q_rel[i][:, :, :], 0.0).then_inc(q_zeroed, 1)
                pool.wait_ge(load_sem, LOADS)

                def build(s, par):
                    for part in range(2):
                        ins = pool.tensor_tensor(q_blk[s % 2][:, part, :, :].rearrange("p g (q h) -> p (g q) h", h=H).bitcast(F32R),
                                                 qT[par][:, part, 16 * s:16 * s + 16].unsqueeze(2).to_broadcast((P, 16, H)),
                                                 cview["mask_head_rows"].unsqueeze(1).to_broadcast((P, 16, H)), ALU.mult)
                    ins.then_inc(built, 1)

                def body(kind, b, par):
                    t0 = pool.snap(b * NS) if kind == "mid" else b * NS
                    if kind == "pro":
                        pool.wait_ge(free[bank_of["qk"]], bank_tally[bank_of["qk"]](kind, b, "qk"))
                        build(0, 0)
                        return
                    for s in steps(kind):
                        if kind != "end" and not (kind == "last" and s == NS - 1):
                            if s == NS - 1:
                                pool.wait_ge(free[bank_of["qk"]], bank_tally[bank_of["qk"]](kind, b, "qk"))
                            if not (kind == "first" and s == 0):
                                pool.wait_ge(scored, t0 + s)
                            build((s + 1) % NS, par if s < NS - 1 else 1 - par)
                        if present(kind, s, 3) and not (kind == "end" and s >= 3):
                            pool.wait_ge(merged, t0 + s - 2)
                            pool.tensor_tensor(zz[s % 2][:, :, :].rearrange("p g (h c) -> p g h c", c=C),
                                               z1[s % 2][:, :, :].rearrange("p g (h c) -> p g h c", c=C),
                                               cview["mask_head"].unsqueeze(1).unsqueeze(3).to_broadcast((P, GS, H, C)),
                                               ALU.mult).then_inc(masked, 1)
                        if present(kind, s, 1) and not (kind == "end" and s >= 1):
                            pool.wait_ge(inverted, t0 + s)
                            pool.tensor_tensor(pick[(s - 1) % 8][:, :, :], cview["pick_query"].unsqueeze(1).to_broadcast((P, GS, QG)),
                                               rinv[(s - 1) % 4][:, :].unsqueeze(2).to_broadcast((P, GS, QG)), ALU.mult).then_inc(picked, 1)
                        tail = "tail" in SECTIONS[kind]
                        if s == 13 and tail:
                            pool.sem_clear(rows_known)
                            pool.wait_ge(slots_done, one_tail(kind, b, "x"))
                            pool.tensor_tensor(scat_f[:, :, :], dumpk[:, :, :], sk[:, :, :], ALU.add).then_inc(rows_known, 1)
                            pool.wait_ge(rows_known, 1)
                            pool.tensor_copy(scat[:, :, :], scat_f[:, :, :]).then_inc(rows_known, 1)
                            pool.wait_ge(rows_known, 2)
                            if kind == "mid" and par == 1:
                                pool.wait_ge(zeroed, NZERO)
                        if tail:
                            for i, k in {13: [(0, 0)], 14: [(0, 1)], 15: [(1, 0), (1, 1)]}.get(s, ()):
                                pool.indirect_dma_start(
                                    out=packed, out_offset=bass.IndirectOffsetOnAxis(ap=scat[:, i, k:k + 1], axis=0),
                                    in_=xn2[:, i, :], in_offset=None).then_inc(scattered, 16)
                pool.dma_start(xn2[:, 0, :], io["x"][0:P, :]).then_inc(scattered, 16)
                bodies(pool, nb, body)
                pool.wait_ge(scattered, 64 * nb + 16)

            @block.scalar
            def _(act):
                act.wait_ge(load_sem, LOADS)
                act.mul(bq_s[:, :], wview["bq"], C ** -0.5)
                act.mul(bq_row_s[:, :], rview["bq_row"], C ** -0.5).then_inc(act_ready, 1)
                act.wait_ge(act_ready, 1)

                def move(kind, b, par, name):
                    bank = bank_of[name]
                    m, n = M_ps[bank], bank_tally[bank](kind, b, name)
                    if name.startswith("up"):
                        k = int(name[2:])
                        act.wait_ge(full[bank], n)
                        act.activation(th[k % 2][:, :], m[:, 0:S], ACT.Tanh, scale=0.5).then_inc(th_done, 1)
                    elif name == "gateT":
                        act.wait_ge(full[bank], n)
                        act.copy(gatesT[:, :].bitcast(F32R), m[0:2 * E, 0:S]).then_inc(free[bank], 1)
                    elif name.startswith("spread"):
                        j = int(name[6:])
                        act.wait_ge(full[bank], n)
                        if j >= 2:
                            act.wait_ge(hid_done, spr_tally(kind, b, f"spread{j - 2}"))
                        elif kind != "first":
                            act.wait_ge(hid_done, (4 + 1) * b)
                        act.copy(gate_bc[j % 2][:, :, :], m[:, 0:2 * S].rearrange("p (a b) -> p a b", a=2)).then_inc(free[bank], 1)
                    elif name == "shared":
                        act.wait_ge(full[bank], n)
                        act.activation(shared_th[:, :], m[:, 0:S], ACT.Tanh, scale=0.5).then_inc(free[bank], 1)
                    elif name == "xnT":
                        act.wait_ge(full[bank], n)
                        act.copy(xnT[1 - par][:, :], m[:, 0:S])
                        act.copy(xnT2[1 - par][:, 0, :].bitcast(F32R), m[:, 0:S]).then_inc(xn_uppers, 1)
                    elif name == "xn2T":
                        act.wait_ge(full[bank], n)
                        act.wait_ge(xnT1_stored, 16 * one_tail(kind, b, "x"))
                        act.copy(xn2T[:, :], m[:, 0:S]).then_inc(free[bank], 1)
                    elif name == "qk":
                        act.wait_ge(full[bank], n)
                        act.activation(qT[1 - par][:, 0, :].bitcast(F32R), m[:, 0:S], ACT.Identity, bias=bq_s[:, 0:1])
                        act.activation(kT[1 - par][:, 0, :].bitcast(F32R), m[:, S:2 * S], ACT.Identity,
                                       bias=wview["bk"]).then_inc(uppers_done, 1)

                def body(kind, b, par):
                    t0 = act.snap(b * NS) if kind == "mid" else b * NS
                    for s in steps(kind):
                        if s:
                            for name in jobs(kind, s - 1):
                                move(kind, b, par, name)
                        if s == 4 and "tail" in SECTIONS[kind]:
                            act.wait_ge(ctxed, t0)
                            act.copy(ctxT[:, :], CTX_ps[:, 0:S]).then_inc(ctx_moved, 1)
                        if present(kind, s, 2) and not (kind == "end" and s >= 2):
                            act.wait_ge(turned, t0 + s - 1)
                            act.copy(probsT[s % 2][:, :, :, :].rearrange("p a b c -> p (a b c)"),
                                     PT_ps[s % 2][:, :]).then_inc(moved, 1)
                        if present(kind, s, 0):
                            act.wait_ge(maxed, t0 + s + 1)
                            for g in range(GS):
                                ins = act.activation(probs[s % 2][:, g, :], S_ps[s % 2][:, g * S:(g + 1) * S], ACT.Exp,
                                                     bias=nmax[s % 4][:, g:g + 1], accum_out=rsum[s % 4][:, g:g + 1])
                            ins.then_inc(exped, 1)
                        if present(kind, s, 1) and not (kind == "end" and s >= 1):
                            sq, own = (s - 1) % NS, vf[par if s >= 1 else 1 - par]
                            u = S // QG - GS * (sq + 1)
                            f = rel_v[:, u:u + GS, :]
                            if not (kind == "first" and s < 3):
                                act.wait_ge(valued, t0 + s - 2)
                            act.copy(own[:, :, sq % 2, :, D:OW],
                                            bass.AP(tensor=f.tensor, offset=f.offset,
                                                    ap=[f.ap[0], [P // QG * QG * C, KT], [QG * C, GS], [1, QG * C]])).then_inc(placed, 1)
                        if s == 9 and "front" in SECTIONS[kind]:
                            act.wait_ge(values_done, one_front(kind, b, "x"))
                            for a in range(KT):
                                ins = act.copy(vf[1 - par][:, a, :, :, 0:D].rearrange("p r g d -> p (r g) d"),
                                               v_new[:, a, :].unsqueeze(1).to_broadcast((P, 2 * GS, D)))
                            ins.then_inc(values_placed, 1)
                        for i, at, section in ((0, 2, "mid"), (1, 11, "tail")):
                            if s == at and section in SECTIONS[kind]:
                                act.wait_ge(gap_done, two(kind, b, f"router{i}"))
                                act.activation(top[i]["ex"][:, :], top[i]["gap"][:, :], ACT.Exp).then_inc(ex_done, 1)
                bodies(act, nb, body)

            @block.vector
            def _(dve):
                lo, n = S - 1 - R, 2 * R + 1
                dve.wait_ge(row_sem, 16)
                dve.tensor_copy(rel_k_row[:, 0:lo], rel_k_row[:, lo:lo + 1].to_broadcast((C, lo))).then_inc(row_extended, 1)
                dve.tensor_copy(rel_k_row[:, lo + n:NU], rel_k_row[:, lo + n - 1:lo + n].to_broadcast((C, lo))).then_inc(row_extended, 1)
                dve.wait_ge(load_sem, LOADS)
                for wq in (wview["wqkv"][:, 0:D], wview["wv_q"][:, D:2 * D]):
                    dve.tensor_scalar(wq, wq, C ** -0.5, None, ALU.mult)
                dve.tensor_copy(rel_k2[:, 0, :].bitcast(F32R), rel_k[:, :]).then_inc(split_ready, 1)
                dve.wait_ge(split_ready, 1)
                dve.tensor_tensor(rel_k2[:, 1, :].bitcast(F32R), rel_k[:, :], rel_k2[:, 0, :], ALU.subtract)
                dve.tensor_copy(spread[:, :].bitcast(F32R), spread_f[:, :])
                for half, whole in ((tri, tri_f), (alibi_l, alibi_lf), (alibi_r, alibi_rf)):
                    dve.tensor_copy(half[:, :], whole[:, :])
                dve.tensor_copy(wshared[:, :], wview["wshared_gate"].to_broadcast((P, P))).then_inc(dve_ready, 1)
                dve.tensor_copy(dump_at[:, :, :], cview["dump"].rearrange("p (i k) -> p i k", k=2))
                dve.memset(counts[:, :], 0.0).then_inc(dve_ready, 1)
                dve.wait_ge(dve_ready, 2)
                links = [0]
                LATE = {"router0": "choose0", "router1": "choose1", "prefix": "slots", "vq": "split"}
                LATE.update({name: name for name in ("spread0", "spread1", "spread2", "spread3", "shared")})

                def link(ins):
                    links[0] += 1
                    ins.then_inc(chain, 1)
                    dve.wait_ge(chain, links[0])

                def layernorm_begin(tile_of):
                    for i in range(2):
                        ins = dve.bn_stats(stats[:, i, :], tile_of(i))
                    link(ins)
                    for i in range(2):
                        ins = dve.bn_aggr(mv[:, i, :], stats[:, i, :])
                    link(ins)
                    v, y, a, c = nw[:, 0, :], nw[:, 1, :], nw[:, 2, :], nw[:, 3, :]
                    link(dve.tensor_scalar(v, mv[:, :, 1], EPS, None, ALU.add))
                    link(dve.tensor_scalar(a.bitcast(I32), v.bitcast(I32), 1, None, ALU.logical_shift_right))
                    link(dve.tensor_scalar(y.bitcast(I32), a.bitcast(I32), -1.0, float(MAGIC), ALU.mult, ALU.add))
                    newton(1)

                def newton(times):
                    v, y, a, c = nw[:, 0, :], nw[:, 1, :], nw[:, 2, :], nw[:, 3, :]
                    for _ in range(times):
                        link(dve.tensor_tensor(a, y, y, ALU.mult))
                        link(dve.scalar_tensor_tensor(c, a, -0.5, v, ALU.mult, ALU.mult))
                        link(dve.scalar_tensor_tensor(y, c, 1.5, y, ALU.add, ALU.mult))

                def layernorm_end(tile_of, normalised, done):
                    newton(2)
                    y = nw[:, 1, :]
                    for i in range(2):
                        ins = dve.tensor_scalar(normalised[:, i, :], tile_of(i), mv[:, i, 0:1], y[:, i:i + 1], ALU.subtract, ALU.mult)
                    ins.then_inc(done, 1)

                def logits(i, bank, bias):
                    q = top[i]
                    m = M_ps[bank][:, 0:2 * E].rearrange("p (t e) -> p t e", e=E)
                    if bias is None:
                        ins = dve.tensor_copy(q["seen"][:, :, :], m)
                    else:
                        ins = dve.tensor_tensor(q["seen"][:, :, :], m, bias.unsqueeze(1).to_broadcast((P, 2, E)), ALU.add)
                    ins.then_inc(free[bank], 1)

                def top_two(kind, b, i, name):
                    q = top[i]
                    dve.wait_ge(free[bank_of[name]], bank_tally[bank_of[name]](kind, b, name))
                    link(dve.tensor_copy(q["logit"][:, :, :], q["seen"][:, :, :]))
                    dve.max(q["m8"][:, 0, :], q["logit"][:, 0, :])
                    link(dve.max(q["m8"][:, 1, :], q["logit"][:, 1, :]))
                    dve.tensor_tensor(q["gap"][:, :], q["m8"][:, :, 1], q["m8"][:, :, 0], ALU.subtract).then_inc(gap_done, 1)
                    for j in range(2):
                        ins = dve.max_index(q["i8"][:, j, :], q["m8"][:, j, :], q["logit"][:, j, :])
                    link(ins)
                    link(dve.tensor_copy(q["idx"][:, :, :], q["i8"][:, :, 0:2]))
                    for k in range(2):
                        ins = dve.tensor_tensor(q["oh"][:, :, k, :], cview["iota"].unsqueeze(1).to_broadcast((P, 2, E)),
                                                q["idx"][:, :, k:k + 1].to_broadcast((P, 2, E)), ALU.is_equal)
                    link(ins)

                def top_softmax(kind, b, i, name):
                    q = top[i]
                    dve.wait_ge(ex_done, two(kind, b, name))
                    link(dve.tensor_scalar(q["den"][:, :], q["ex"][:, :], 1.0, None, ALU.add))
                    link(dve.reciprocal(q["g"][:, :, 0], q["den"][:, :]))
                    link(dve.tensor_tensor(q["g"][:, :, 1], q["g"][:, :, 0], q["ex"][:, :], ALU.mult))

                def handle(kind, b, par, name):
                    if name not in ("gateT", "xn2T", "spread0",
                                    "spread1", "spread2", "spread3", "shared", "gates", "weights",
                                    "choose0", "choose1", "slots", "split"):
                        bank = bank_of[name]
                        m, n = M_ps[bank], bank_tally[bank](kind, b, name)
                        dve.wait_ge(full[bank], n)
                    if name == "router0":
                        logits(0, bank, None)
                    elif name == "gates":
                        top_softmax(kind, b, 0, "router0")
                        q = top[0]
                        for k, t in ((0, q["t0"]), (1, q["t1"])):
                            ins = dve.tensor_tensor(t[:, :, :], q["oh"][:, :, k, :],
                                                    q["g"][:, :, k:k + 1].to_broadcast((P, 2, E)), ALU.mult)
                        link(ins)
                        link(dve.tensor_tensor(gates[:, :, :], q["t0"][:, :, :], q["t1"][:, :, :], ALU.add))
                        link(dve.tensor_copy(gates2[:, :, 0, :].bitcast(F32R), gates[:, :, :]))
                        dve.tensor_tensor(gates2[:, :, 1, :].bitcast(F32R), gates[:, :, :], gates2[:, :, 0, :],
                                          ALU.subtract).then_inc(gates_done, 1)
                    elif name.startswith("up"):
                        k = int(name[2:])
                        dve.wait_ge(th_done, th_tally(kind, b, name))
                        link(dve.scalar_tensor_tensor(ga[:, :], th[k % 2][:, :], 1.0, m[:, 0:S], ALU.add, ALU.mult))
                        ins = dve.tensor_tensor(hid[par][:, k, :], ga[:, :], m[:, S:2 * S], ALU.mult)
                        ins.then_inc(free[bank], 1)
                        dve.wait_ge(free[bank], n)
                    elif name.startswith("spread"):
                        j = int(name[6:])
                        bk = bank_of[name]
                        dve.wait_ge(free[bk], bank_tally[bk](kind, b, name))
                        dve.tensor_tensor(hid[par][:, 2 * j:2 * j + 2, :], hid[par][:, 2 * j:2 * j + 2, :],
                                          gate_bc[j % 2][:, :, :], ALU.mult).then_inc(hid_done, 1)
                    elif name == "shared":
                        bk = bank_of[name]
                        dve.wait_ge(free[bk], bank_tally[bk](kind, b, name))
                        link(dve.tensor_scalar(shared_th[:, :], shared_th[:, :], 0.25, 0.25, ALU.mult, ALU.add))
                        dve.tensor_tensor(hid[par][:, NK - 2:NK, :], hid[par][:, NK - 2:NK, :],
                                          shared_th[:, :].unsqueeze(1).to_broadcast((P, 2, S)), ALU.mult).then_inc(hid_done, 1)
                    elif name == "xnT":
                        dve.wait_ge(xn_uppers, one_front(kind, b, "x"))
                        dve.tensor_tensor(xnT2[1 - par][:, 1, :].bitcast(F32R), m[:, 0:S], xnT2[1 - par][:, 0, :],
                                          ALU.subtract).then_inc(free[bank], 1)
                    elif name == "qk":
                        dve.wait_ge(uppers_done, one_front(kind, b, "x"))
                        dve.scalar_tensor_tensor(qT[1 - par][:, 1, :].bitcast(F32R), m[:, 0:S], bq_s[:, 0:1],
                                                 qT[1 - par][:, 0, :], ALU.add, ALU.subtract)
                        dve.scalar_tensor_tensor(kT[1 - par][:, 1, :].bitcast(F32R), m[:, S:2 * S], wview["bk"],
                                                 kT[1 - par][:, 0, :], ALU.add, ALU.subtract).then_inc(free[bank], 1)
                    elif name == "vq":
                        dve.tensor_tensor(v_new[:, :, :], m[:, 0:S].rearrange("p (a d) -> p a d", a=KT),
                                          rview["bv"].unsqueeze(1).to_broadcast((P, KT, D)), ALU.add).then_inc(values_done, 1)
                        dve.tensor_tensor(q_row[:, :, :], m[:, S:2 * S].rearrange("p (a d) -> p a d", a=2),
                                          bq_row_s[:, :].unsqueeze(1).to_broadcast((P, 2, D)), ALU.add).then_inc(free[bank], 1)
                    elif name == "split":
                        dve.wait_ge(free[bank_of["vq"]], bank_tally[bank_of["vq"]](kind, b, "vq"))
                        if kind != "pro":
                            dve.wait_ge(q_placed, (b + 1) * (16 * QG))
                        link(dve.tensor_copy(q_row2[:, :, 0, :].bitcast(F32R), q_row[:, :, :]))
                        dve.tensor_tensor(q_row2[:, :, 1, :].bitcast(F32R), q_row[:, :, :], q_row2[:, :, 0, :],
                                          ALU.subtract).then_inc(q_split, 1)
                    elif name == "out":
                        here = bass.ds((b - 1) * 2, 2)
                        dve.tensor_tensor(x1[:, :, :], m[:, 0:S].rearrange("p (a d) -> p a d", a=2),
                                          residual[:, here, :], ALU.add).then_inc(free[bank], 1)
                        dve.wait_ge(free[bank], n)
                        link(dve.tensor_tensor(x1[:, :, :], x1[:, :, :], rview["bout"].unsqueeze(1).to_broadcast((P, 2, D)), ALU.add))
                        dve.tensor_copy(residual[:, here, :], x1[:, :, :])
                    elif name == "router1":
                        logits(1, bank, rview["brouter1"])
                    elif name == "choose0":
                        top_two(kind, b, 0, "router0")
                    elif name == "choose1":
                        top_two(kind, b, 1, "router1")
                        q = top[1]
                        dve.tensor_tensor(chosen[:, :, :], q["oh"][:, :, 0, :], q["oh"][:, :, 1, :], ALU.add).then_inc(chosen_done, 1)
                    elif name == "prefix":
                        dve.tensor_copy(before[:, :, :], m[:, 0:3 * E].rearrange("p (t e) -> p t e", e=E)).then_inc(free[bank], 1)
                    elif name == "slots":
                        q = top[1]
                        dve.wait_ge(free[bank_of["prefix"]], bank_tally[bank_of["prefix"]](kind, b, "prefix"))
                        link(dve.tensor_tensor(pos[:, :, :], before[:, 0:2, :],
                                               counts[:, :].unsqueeze(1).to_broadcast((P, 2, E)), ALU.add))
                        dve.tensor_tensor(counts[:, :], counts[:, :], before[:, 2, :], ALU.add)
                        link(dve.tensor_tensor(posk[:, :, :, :], q["oh"][:, :, :, :],
                                               pos[:, :, :].unsqueeze(2).to_broadcast((P, 2, 2, E)), ALU.mult))
                        link(dve.tensor_reduce(pk[:, :, :], posk[:, :, :, :], AX.X, ALU.add))
                        link(dve.tensor_scalar(kept[:, :, :], pk[:, :, :], float(cap), None, ALU.is_lt))
                        link(dve.scalar_tensor_tensor(slot[:, :, :], q["idx"][:, :, :], float(cap), pk[:, :, :], ALU.mult, ALU.add))
                        link(dve.tensor_tensor(sk[:, :, :], slot[:, :, :], kept[:, :, :], ALU.mult))
                        dve.tensor_copy(slot_ids[:, bass.ds((b - 1) * 2, 2), :], sk[:, :, :])
                        link(dve.tensor_tensor(dumpk[:, :, :], dump_at[:, :, :], kept[:, :, :], ALU.mult))
                        link(dve.tensor_tensor(dumpk[:, :, :], dump_at[:, :, :], dumpk[:, :, :], ALU.subtract))
                        dve.tensor_scalar(dump_at[:, :, :], dump_at[:, :, :], float(S), None, ALU.add).then_inc(slots_done, 1)
                    elif name == "weights":
                        q = top[1]
                        link(dve.tensor_tensor(gk[:, :, :], q["g"][:, :, :], kept[:, :, :], ALU.mult))
                        link(dve.tensor_tensor(gden[:, :], gk[:, :, 0], gk[:, :, 1], ALU.add))
                        link(dve.tensor_scalar(gden[:, :], gden[:, :], 1e-9, None, ALU.add))
                        link(dve.reciprocal(gden[:, :], gden[:, :]))
                        link(dve.tensor_tensor(slot_w[:, bass.ds((b - 1) * 2, 2), :], gk[:, :, :],
                                               gden[:, :].unsqueeze(2).to_broadcast((P, 2, 2)), ALU.mult))

                def body(kind, b, par):
                    t0 = dve.snap(b * NS) if kind == "mid" else b * NS
                    if kind != "pro":
                        dve.sem_clear(chain)
                        links[0] = 0
                    if kind == "pro":
                        dve.wait_ge(x_first, 16)
                    if kind == "last" or (kind == "mid" and par == 1):
                        dve.wait_ge(x_rest, XREST)
                        dve.wait_ge(zeroed, NZERO)
                    for s in steps(kind):
                        if s:
                            for name in jobs(kind, s - 1):
                                if LATE.get(name) != name:
                                    handle(kind, b, par, name)
                        if present(kind, s, 0):
                            dve.wait_ge(scored, t0 + s + 1)
                            dve.tensor_reduce(nmax[s % 4][:, :], S_ps[s % 2][:, :].rearrange("p (g k) -> p g k", g=GS),
                                              AX.X, ALU.max, negate=True).then_inc(maxed, 1)
                        if present(kind, s, 1) and not (kind == "end" and s >= 1):
                            r = (s - 1) % 4
                            dve.wait_ge(exped, t0 + s)
                            dve.reciprocal(rinv[r][:, :], rsum[r][:, :]).then_inc(inverted, 1)
                        if present(kind, s, 3) and not (kind == "end" and s >= 3):
                            o = O_ps[:, 0:GS * OW].rearrange("p (g w) -> p g w", g=GS)
                            dve.wait_ge(valued, t0 + s - 2)
                            link(dve.tensor_tensor(rel_m[s % 2][:, :, :, :],
                                                   o[:, :, D:OW].rearrange("p g (q c) -> p g q c", c=C),
                                                   cview["mask_query"].unsqueeze(1).unsqueeze(3).to_broadcast((P, GS, QG, C)),
                                                   ALU.mult))
                            link(dve.tensor_reduce(rel_s[s % 2][:, :, :],
                                                   rel_m[s % 2][:, :, :, :].rearrange("p g q c -> p g c q"), AX.X, ALU.add))
                            dve.tensor_tensor(z1[s % 2][:, :, :].rearrange("p g (h c) -> p g h c", c=C),
                                              o[:, :, 0:D].rearrange("p g (h c) -> p g h c", c=C),
                                              rel_s[s % 2][:, :, :].unsqueeze(2).to_broadcast((P, GS, H, C)),
                                              ALU.add).then_inc(merged, 1)
                        if kind == "pro" and s == NS - 1:
                            dve.wait_ge(ffn_loaded, 16)
                            dve.tensor_copy(ffn2[:, 0, :].bitcast(F32R), ffn_in).then_inc(ffn_split, 1)
                            dve.wait_ge(ffn_split, 1)
                            dve.tensor_tensor(ffn2[:, 1, :].bitcast(F32R), ffn_in, ffn2[:, 0, :], ALU.subtract).then_inc(ffn_split, 1)
                            dve.wait_ge(ffn_split, 2)
                            dve.memset(zeros[:, :, :], 0.0).then_inc(cleared, 1)
                        for name in jobs(kind, s - 1) if s else ():
                            if name in LATE:
                                handle(kind, b, par, LATE[name])
                        if "mid" in SECTIONS[kind] and s == 2:
                            handle(kind, b, par, "gates")
                        if "tail" in SECTIONS[kind]:
                            if s == 6:
                                layernorm_begin(lambda i: x1[:, i, :])
                            if s == 7:
                                dve.wait_ge(scattered, 64 * (one_tail(kind, b, "x") - 1) + 16)
                                layernorm_end(lambda i: x1[:, i, :], xn2, xn2_done)
                            if s == 13:
                                top_softmax(kind, b, 1, "router1")
                            if s == 14:
                                handle(kind, b, par, "weights")
                        if "front" in SECTIONS[kind]:
                            tile_of = lambda i: residual[:, bass.ds((b + 1) * 2 + i, 1), :].rearrange("p a d -> p (a d)")
                            if s == 0:
                                layernorm_begin(tile_of)
                            if s == 3:
                                layernorm_end(tile_of, xn, xn_done)
                bodies(dve, nb, body)

            @block.tensor
            def _(pe):
                pe.wait_ge(load_sem, LOADS)
                pe.wait_ge(dve_ready, 1)

                def project(kind, b, par, name):
                    bank = bank_of[name]
                    tally = bank_tally[bank]
                    m, n = M_ps[bank], tally(kind, b, name)
                    if not (isinstance(n, int) and n == 1):
                        pe.wait_ge(free[bank], n - 1)
                    w = wview

                    def moved_by(job):
                        pe.wait_ge(free[bank_of[job]], bank_tally[bank_of[job]](kind, b, job))

                    def mm(out, lhsT, rhs, start=True, stop=True):
                        return pe.matmul(out, lhsT, rhs, start=start, stop=stop)
                    if name == "router0":
                        for i in range(2):
                            ins = mm(m[:, i * E:(i + 1) * E], xnT[par][:, i * P:(i + 1) * P], w["wrouter0"])
                    elif name.startswith("up"):
                        k = int(name[2:])
                        if kind == "first" and k == 0:
                            pe.wait_ge(ffn_split, 2)
                        for half in range(2):
                            for i, (x, y) in enumerate(((0, 0), (0, 1), (1, 0))):
                                ins = mm(m[:, half * S:(half + 1) * S], ffn2[:, x, (half * NK + k) * P:(half * NK + k + 1) * P].bitcast(F32R),
                                         xnT2[par][:, y, :].bitcast(F32R), start=(i == 0), stop=(i == 2))
                    elif name == "gateT":
                        pe.wait_ge(gates_done, one_mid(kind, b, "x"))
                        for i in range(2):
                            ins = pe.transpose(m[0:2 * E, i * P:(i + 1) * P], gates2[:, i, :, :].rearrange("p k e -> p (k e)"), ident)
                    elif name.startswith("spread"):
                        j = int(name[6:])
                        if j == 0:
                            moved_by("gateT")
                        for i in range(2):
                            k = 2 * j + i
                            ins = mm(m[:, i * S:(i + 1) * S], spread[:, k * P:(k + 1) * P].bitcast(F32R), gatesT[:, :].bitcast(F32R))
                    elif name == "shared":
                        ins = mm(m[:, 0:S], wshared[:, :], xnT[par][:, :])
                    elif name == "xnT":
                        pe.wait_ge(xn_done, one_front(kind, b, "x"))
                        for i in range(2):
                            ins = pe.transpose(m[:, i * P:(i + 1) * P], xn[:, i, :], ident)
                    elif name == "xn2T":
                        pe.wait_ge(xn2_done, one_tail(kind, b, "x"))
                        for i in range(2):
                            ins = pe.transpose(m[:, i * P:(i + 1) * P], xn2[:, i, :], ident)
                    elif name == "qk":
                        moved_by("xnT")
                        mm(m[:, 0:S], w["wqkv"][:, 0:D], xnT[1 - par][:, :])
                        ins = mm(m[:, S:2 * S], w["wqkv"][:, D:2 * D], xnT[1 - par][:, :])
                    elif name == "vq":
                        for i in range(KT):
                            mm(m[:, i * D:(i + 1) * D], xnT[1 - par][:, i * P:(i + 1) * P], w["wv_q"][:, 0:D])
                            ins = mm(m[:, S + i * D:S + (i + 1) * D], xnT[1 - par][:, i * P:(i + 1) * P], w["wv_q"][:, D:2 * D])
                    elif name == "out":
                        pe.wait_ge(ctx_moved, one_tail(kind, b, "x"))
                        nh = spr_tally("mid", 1, "shared") - spr_tally("first", 0, "shared")
                        pe.wait_ge(hid_done, nh * b)
                        for i in range(2):
                            o = m[:, i * D:(i + 1) * D]
                            mm(o, ctxT[:, i * P:(i + 1) * P], w["wout"], stop=False)
                            for k in range(NK):
                                ins = mm(o, hid[1 - par][:, k, i * P:(i + 1) * P], w["wdown"][:, k * D:(k + 1) * D],
                                         start=False, stop=(k == NK - 1))
                    elif name == "router1":
                        moved_by("xn2T")
                        for i in range(2):
                            ins = mm(m[:, i * E:(i + 1) * E], xn2T[:, i * P:(i + 1) * P], w["wrouter1"])
                    elif name == "prefix":
                        pe.wait_ge(chosen_done, one_tail(kind, b, "x"))
                        before, every = tri[:, 0:P], tri[:, P:2 * P]
                        mm(m[:, 0:E], before, chosen[:, 0, :])
                        mm(m[:, E:2 * E], before, chosen[:, 1, :], stop=False)
                        mm(m[:, E:2 * E], every, chosen[:, 0, :], start=False)
                        mm(m[:, 2 * E:3 * E], every, chosen[:, 0, :], stop=False)
                        ins = mm(m[:, 2 * E:3 * E], every, chosen[:, 1, :], start=False)
                    ins.then_inc(full[bank], 1)

                def body(kind, b, par):
                    t0 = pe.snap(b * NS) if kind == "mid" else b * NS
                    for s in steps(kind):
                        if present(kind, s, 0):
                            pe.wait_ge(built, t0 + s + 1)
                            if s == 0:
                                pe.wait_ge(q_placed, (b + 1) * (16 * QG))
                            if not (kind == "first" and s < 2):
                                pe.wait_ge(exped, t0 + s - 1)
                            for g in range(GS):
                                o = S_ps[s % 2][:, g * S:(g + 1) * S]
                                G = GS * s + g
                                off = S - QG - QG * G
                                qb, kk = q_blk[s % 2], kT[par]
                                for i, (x, y) in enumerate(((0, 0), (0, 1), (1, 0))):
                                    pe.matmul(o, qb[:, x, g, :].bitcast(F32R), kk[:, y, :].bitcast(F32R), start=(i == 0), stop=False)
                                for y in range(2):
                                    ins = pe.matmul(o, q_rel[par][:, G, :].bitcast(F32R), rel_k2[:, y, off:off + S].bitcast(F32R),
                                                    start=False, stop=(y == 1))
                            ins.then_inc(scored, 1)
                        if present(kind, s, 2) and not (kind == "end" and s >= 2):
                            r = s % 2
                            pe.wait_ge(exped, t0 + s - 1)
                            if not (kind == "first" and s < 4):
                                pe.wait_ge(moved, t0 + s - 3)
                            for kt in range(KT):
                                for g in range(GS):
                                    ins = pe.transpose(PT_ps[r][:, (kt * GS + g) * P:(kt * GS + g + 1) * P],
                                                       probs[r][:, g, kt * P:(kt + 1) * P], ident)
                            ins.then_inc(turned, 1)
                        if present(kind, s, 3) and not (kind == "end" and s >= 3):
                            r, sq = (s - 3) % 2, (s - 3) % NS
                            vp = vf[par if s >= 3 else 1 - par]
                            pe.wait_ge(placed, t0 + s - 2)
                            if s == 3:
                                pe.wait_ge(values_placed, b + 1)
                            pe.wait_ge(moved, t0 + s - 2)
                            if not (kind == "first" and s < 4):
                                pe.wait_ge(merged, t0 + s - 3)
                            for g in range(GS):
                                G = GS * sq + g
                                for kt in range(KT):
                                    ins = pe.matmul(O_ps[:, g * OW:(g + 1) * OW], probsT[r][:, kt, g, :],
                                                    vp[:, kt, r, GS - 1 - g, :], start=(kt == 0), stop=(kt == KT - 1))
                            ins.then_inc(valued, 1)
                        for name in jobs(kind, s):
                            project(kind, b, par, name)
                        if present(kind, s, 4) and not (kind == "end" and s >= 4):
                            sq = (s - 4) % NS
                            pe.wait_ge(picked, t0 + s - 3)
                            pe.wait_ge(masked, t0 + s - 3)
                            if s == 4 and "tail" in SECTIONS[kind]:
                                pe.wait_ge(ctx_moved, one_tail(kind, b, "x"))
                            for g in range(GS):
                                G = GS * sq + g
                                ins = pe.matmul(CTX_ps[:, QG * G:QG * G + QG], zz[(s - 1) % 2][:, g, :],
                                                pick[(s - 4) % 8][:, g, :], start=True, stop=True)
                            ins.then_inc(ctxed, 1)
                bodies(pe, nb, body)

        with ExitStack() as pc:
            def sc(name, shape, dt=F32):
                return pc.enter_context(nc.sbuf_tensor(name, shape, dt))

            def bank_c(name):
                return pc.enter_context(nc.psum_tensor(name, [P, 512], F32))

            T_ps = [bank_c(f"slotsT{i}") for i in range(2)]
            U_ps = [bank_c(f"up_{i}") for i in range(4)]
            Y_ps = [bank_c(f"down{i}") for i in range(2)]
            FT = FF // P
            b2 = sc("b2", [P, E, D])
            b1e = [sc(f"b1e{i}", [P, FT]) for i in range(2)]
            b1_moved = pc.enter_context(nc.semaphore("b1_moved"))
            xe = [sc(f"xe{i}", [P, JT, D]) for i in range(2)]
            w1 = [sc(f"w1_{i}", [P, FF]) for i in range(2)]
            w2 = [sc(f"w2_{i}", [P, FT, D]) for i in range(2)]
            xeT = sc("xeT", [P, cap])
            he = sc("he", [P, FT, cap])
            ye = [sc(f"ye{i}", [P, JT, D]) for i in range(2)]
            csem = {n: pc.enter_context(nc.semaphore(n + "_c")) for n in
                    ("b2_in", "in0", "in1", "out0", "out1", "tr", "tr_moved", "up", "gelu", "down", "y_moved")}
            b2_in, in0, in1, out0, out1, tr, tr_moved, up, gelu, down, y_moved = csem.values()
            loaded, stored = [in0, in1], [out0, out1]
            QT = [(j, min(4, JT - j)) for j in range(0, JT, 4)]
            NQ = len(QT)

            with nc.Block() as block:
                def experts(engine, body):
                    body(0, 0, True)
                    body(1, 1, True)
                    with engine.Fori(1, E // 2) as pair:
                        e = engine.snap(pair * 2)
                        body(e, 0, False)
                        body(e + 1, 1, False)

                packed_t = packed[0:SLOTS, :].rearrange("(e p j) d -> e p j d", p=P, j=JT)
                out_t = expert_out.rearrange("(e p j) d -> e p j d", p=P, j=JT)

                @block.sync
                def _(sp):
                    sp.dma_start(b2[:, :, :].rearrange("p e d -> p (e d)"), io["b2"].partition_broadcast(P)).then_inc(b2_in, 16)

                    def body(e, i, first):
                        if not first:
                            sp.wait_ge(down, (e - 1) * NQ)
                        sp.dma_start(xe[i][:, :, :], packed_t[bass.ds(e, 1)].rearrange("a p j d -> p (a j) d")).then_inc(loaded[i], 16)
                        sp.dma_start(w1[i][:, :], io["w1"][bass.ds(e, 1)].rearrange("a p f -> p (a f)")).then_inc(loaded[i], 16)
                        sp.dma_start(w2[i][:, :, :], io["w2"][bass.ds(e, 1)].rearrange("a (m p) d -> p (a m) d", p=P)).then_inc(loaded[i], 16)
                    experts(sp, body)

                @block.tensor
                def _(pe):
                    def body(e, i, first):
                        pe.wait_ge(loaded[i], 48 if first else e * 24 + (48 if i == 0 else 24))
                        for q, (j0, n) in enumerate(QT):
                            if not (first and i == 0 and q < 2):
                                pe.wait_ge(tr_moved, e * NQ + q - 1)
                            for j in range(n):
                                ins = pe.transpose(T_ps[(i * NQ + q) % 2][:, j * P:(j + 1) * P], xe[i][:, j0 + j, :], ident)
                            ins.then_inc(tr, 1)
                        for q, (j0, n) in enumerate(QT):
                            pe.wait_ge(tr_moved, e * NQ + q + 1)
                            for f in range(FT):
                                if not (first and i == 0 and q == 0):
                                    pe.wait_ge(gelu, (e * NQ + q) * FT + f - FT + 1)
                                pe.matmul(U_ps[f][:, 0:n * P], w1[i][:, f * P:(f + 1) * P], xeT[:, j0 * P:(j0 + n) * P],
                                          start=True, stop=True).then_inc(up, 1)
                        for q, (j0, n) in enumerate(QT):
                            pe.wait_ge(gelu, (e * NQ + q + 1) * FT)
                            if not (first and i == 0 and q < 2):
                                pe.wait_ge(y_moved, e * NQ + q - 1)
                            for j in range(n):
                                for f in range(FT):
                                    ins = pe.matmul(Y_ps[(i * NQ + q) % 2][:, j * D:(j + 1) * D],
                                                    he[:, f, (j0 + j) * P:(j0 + j + 1) * P], w2[i][:, f, :],
                                                    start=(f == 0), stop=(f == FT - 1))
                            ins.then_inc(down, 1)
                    experts(pe, body)

                @block.scalar
                def _(act):
                    def body(e, i, first):
                        for q, (j0, n) in enumerate(QT):
                            for f in range(FT):
                                act.wait_ge(up, (e * NQ + q) * FT + f + 1)
                                if q == 0 and f == 0 and not (first and i == 0):
                                    act.wait_ge(down, e * NQ)
                                act.activation(he[:, f, j0 * P:(j0 + n) * P], U_ps[f][:, 0:n * P], ACT.Gelu,
                                               bias=b1e[i][:, f:f + 1]).then_inc(gelu, 1)
                    b1v = wview["b1"].rearrange("p (e f) -> p e f", f=FT)

                    def with_bias(e, i, first):
                        act.copy(b1e[i][:, :], b1v[:, bass.ds(e, 1), :].rearrange("p a f -> p (a f)")).then_inc(b1_moved, 1)
                        act.wait_ge(b1_moved, e + 1)
                        body(e, i, first)
                    experts(act, with_bias)

                @block.vector
                def _(dve):
                    dve.wait_ge(b2_in, 16)

                    def body(e, i, first):
                        for q, (j0, n) in enumerate(QT):
                            dve.wait_ge(tr, e * NQ + q + 1)
                            if q == 0 and not (first and i == 0):
                                dve.wait_ge(up, e * NQ * FT)
                            dve.tensor_copy(xeT[:, j0 * P:(j0 + n) * P], T_ps[(i * NQ + q) % 2][:, 0:n * P]).then_inc(tr_moved, 1)
                        for q, (j0, n) in enumerate(QT):
                            dve.wait_ge(down, e * NQ + q + 1)
                            if q == 0 and not first:
                                dve.wait_ge(stored[i], e * 8 if i == 0 else (e - 1) * 8)
                            dve.tensor_tensor(ye[i][:, j0:j0 + n, :], Y_ps[(i * NQ + q) % 2][:, 0:n * D].rearrange("p (j d) -> p j d", d=D),
                                              b2[:, bass.ds(e, 1), :].to_broadcast((P, n, D)), ALU.add).then_inc(y_moved, 1)
                    experts(dve, body)

                @block.gpsimd
                def _(pool):
                    def body(e, i, first):
                        pool.wait_ge(y_moved, (e + 1) * NQ)
                        pool.dma_start(out_t[bass.ds(e, 1)].rearrange("a p j d -> p (a j) d"), ye[i][:, :, :]).then_inc(stored[i], 16)
                    experts(pool, body)
                    for i in range(2):
                        pool.wait_ge(stored[i], 16 * (E // 2))

        with ExitStack() as pb:
            def sbb(name, shape, dt=F32):
                return pb.enter_context(nc.sbuf_tensor(name, shape, dt))

            def bank_b(name):
                return pb.enter_context(nc.psum_tensor(name, [P, 512], F32))

            S_ps = [bank_b(f"scores1_{i}") for i in range(2)]
            PT_ps = [bank_b(f"probsT1_{i}") for i in range(2)]
            O_ps = [bank_b(f"values1_{i}") for i in range(2)]
            M_ps = [bank_b(f"spare1_{i}") for i in range(2)]
            xt = [sbb(f"xt1_{i}", [P, S]) for i in range(2)]
            qT = [sbb(f"qT1_{i}", [P, P]) for i in range(2)]
            kT = [sbb(f"kT1_{i}", [P, P]) for i in range(2)]
            v0 = [sbb(f"v1_{i}", [P, D]) for i in range(2)]
            qT2 = [sbb(f"qT1_parts{i}", [P, 2, P]) for i in range(2)]
            kT2 = [sbb(f"kT1_parts{i}", [P, 2, S]) for i in range(2)]
            v2 = [sbb(f"v1_parts{i}", [P, 2, KT, D]) for i in range(2)]
            q_blk = [sbb(f"q_blk1_{i}", [P, GS, P]) for i in range(2)]
            q_blk2 = [sbb(f"q_blk1_parts{i}", [P, 2, GS, P]) for i in range(2)]
            probs = [sbb(f"probs1_{i}", [P, GS, S]) for i in range(2)]
            probsT = [sbb(f"probsT1_s{i}", [P, GS * P]) for i in range(2)]
            probsT2 = [sbb(f"probsT1_parts{i}", [P, 2, KT, GS * P]) for i in range(2)]
            nmax = [sbb(f"nmax1_{i}", [P, GS]) for i in range(4)]
            rsum = [sbb(f"rsum1_{i}", [P, GS]) for i in range(4)]
            rinv = [sbb(f"rinv1_{i}", [P, GS]) for i in range(4)]
            pick = [sbb(f"pick1_{i}", [P, GS, QG]) for i in range(4)]
            zz = sbb("zz1", [P, GS * QG, H])
            weighted = sbb("weighted1", [P, GS * QG])
            ctxT = [sbb(f"ctxT1_{i}", [P, S]) for i in range(2)]
            expert_rows = [sbb(f"expert_rows_{i}", [P, 2, 2, D]) for i in range(2)]
            ids = [sbb(f"ids_{i}", [P, 2, 2], U32) for i in range(2)]
            with_one = sbb("with_one", [P, 2, D])
            with_two = sbb("with_two", [P, 2, D])
            total = sbb("total", [P, 2, D])
            gathered = [pb.enter_context(nc.semaphore(f"gathered{i}")) for i in range(2)]
            written = pb.enter_context(nc.semaphore("written"))
            ids_at = pb.enter_context(nc.semaphore("ids_at"))
            bsem = {n: pb.enter_context(nc.semaphore(n + "_b")) for n in
                    ("built", "scored", "maxed", "exped", "turned", "moved", "valued", "picked", "merged",
                     "full0", "full1", "free0", "free1", "xt0_in", "xt1_in", "chain", "uppers_done", "lowers", "inverted")}
            (built, scored, maxed, exped, turned, moved, valued, picked, merged, full0, full1,
             free0, free1, xt0_in, xt1_in, chain, uppers_done, lowers, inverted) = bsem.values()
            full, free, xt_in = [full0, full1], [free0, free1], [xt0_in, xt1_in]
            bank_of = {name: i % 2 for i, (_, name, _) in enumerate(JOBS_B)}
            bank_tally = [Tally(nb, [(n, s) for _, n, s in JOBS_B if bank_of[n] == i]) for i in range(2)]
            one_front = Tally(nb, [("x", "front")])
            one_tail = Tally(nb, [("x", "tail")])

            def jobs(kind, step):
                return [n for s, n, sec in JOBS_B if s == step and sec in SECTIONS[kind]]

            def present(kind, s, lag):
                return kind in (("first", "mid", "last") if s >= lag else ("mid", "last", "end"))

            def ktiles(s):
                return (GS * QG * (s % NS + 1) - 1) // P + 1

            HEAVY = NS // 2

            def lower_count(b, x):
                return b * HEAVY + (x - HEAVY + 1 if x >= HEAVY else x + 1)

            block = pb.enter_context(nc.Block())

            @block.sync
            def _(sp):
                def body(kind, b, par):
                    if "front" in SECTIONS[kind]:
                        if kind == "mid":
                            sp.wait_ge(scored, b * NS)
                        sp.dma_start(xt[1 - par][:, :], xnT1[bass.ds(b + 1, 1)].rearrange("a p s -> p (a s)")).then_inc(xt_in[1 - par], 16)
                    if "tail" in SECTIONS[kind]:
                        bank = bank_of["out"]
                        sp.wait_ge(free[bank], bank_tally[bank](kind, b, "out"))
                        sp.dma_start(io["out"].rearrange("(b i p) d -> b p i d", i=2, p=P)[bass.ds(b - 1, 1)]
                                     .rearrange("a p i d -> p (a i) d"), total[:, :, :]).then_inc(written, 16)
                sp.dma_start(total[:, :, :], io["x"][0:2 * P, :].rearrange("(i p) d -> p i d", p=P)).then_inc(written, 16)
                bodies(sp, nb, body)
                sp.wait_ge(written, 16 * nb + 16)

            @block.gpsimd
            def _(pool):
                def build(s, par):
                    for part in range(ktiles(s)):
                        src = (qT[par][:, 16 * s:16 * s + 16] if s < HEAVY
                               else qT2[par][:, part, 16 * (s - HEAVY):16 * (s - HEAVY) + 16])
                        dst = q_blk[s % 2][:, :, :] if s < HEAVY else q_blk2[s % 2][:, part, :, :].bitcast(F32R)
                        ins = pool.tensor_tensor(dst.rearrange("p g (q h) -> p (g q) h", h=H), src.unsqueeze(2).to_broadcast((P, 16, H)),
                                                 cview["mask_head_rows"].unsqueeze(1).to_broadcast((P, 16, H)), ALU.mult)
                    ins.then_inc(built, 1)

                def body(kind, b, par):
                    t0 = pool.snap(b * NS) if kind == "mid" else b * NS
                    if kind == "pro":
                        pool.wait_ge(free[bank_of["qk"]], bank_tally[bank_of["qk"]](kind, b, "qk"))
                        build(0, 0)
                        return
                    for s in range(NS):
                        if kind == "end":
                            pool.wait_ge(inverted, t0)
                            pool.tensor_tensor(pick[3][:, :, :], cview["pick_query"].unsqueeze(1).to_broadcast((P, GS, QG)),
                                               rinv[3][:, :].unsqueeze(2).to_broadcast((P, GS, QG)), ALU.mult).then_inc(picked, 1)
                            return
                        if s == 1:
                            pool.wait_ge(maxed, t0 + 1)
                        if not (kind == "last" and s == NS - 1):
                            if s == NS - 1:
                                pool.wait_ge(free[bank_of["qk"]], bank_tally[bank_of["qk"]](kind, b, "qk"))
                            if not (kind == "first" and s == 0):
                                pool.wait_ge(scored, t0 + s)
                            build((s + 1) % NS, par if s < NS - 1 else 1 - par)
                        if not (kind == "first" and s == 0):
                            r = (s - 1) % 4
                            pool.wait_ge(inverted, t0 + s)
                            pool.tensor_tensor(pick[r][:, :, :], cview["pick_query"].unsqueeze(1).to_broadcast((P, GS, QG)),
                                               rinv[r][:, :].unsqueeze(2).to_broadcast((P, GS, QG)), ALU.mult).then_inc(picked, 1)
                        if s == 9:
                            pool.sem_clear(ids_at)
                            pool.tensor_copy(ids[par][:, :, :], slot_ids[:, bass.ds(b * 2, 2), :]).then_inc(ids_at, 1)
                            pool.wait_ge(ids_at, 1)
                        if 9 <= s <= 12:
                            i, k = (s - 9) // 2, (s - 9) % 2
                            pool.indirect_dma_start(out=expert_rows[par][:, i, k, :], out_offset=None, in_=expert_out,
                                                    in_offset=bass.IndirectOffsetOnAxis(ap=ids[par][:, i, k:k + 1], axis=0)
                                                    ).then_inc(gathered[par], 16)
                bodies(pool, nb, body)

            @block.scalar
            def _(act):
                def move(kind, b, par, name):
                    bank = bank_of[name]
                    m, n = M_ps[bank], bank_tally[bank](kind, b, name)
                    if name == "qk":
                        act.wait_ge(full[bank], n)
                        act.mul(qT2[1 - par][:, 0, :].bitcast(F32R), m[:, P:S], C ** -0.5)
                        act.copy(kT2[1 - par][:, 0, :].bitcast(F32R), m[:, S:2 * S])
                        act.mul(qT[1 - par][:, :], m[:, 0:P], C ** -0.5)
                        act.copy(kT[1 - par][:, :], m[:, S:S + P]).then_inc(uppers_done, 1)
                    elif name == "v":
                        act.wait_ge(full[bank], n)
                        act.copy(v2[1 - par][:, 0, :, :].rearrange("p a d -> p (a d)").bitcast(F32R), m[:, 0:S])
                        act.copy(v0[1 - par][:, :], m[:, 0:D]).then_inc(uppers_done, 1)

                def body(kind, b, par):
                    t0 = act.snap(b * NS) if kind == "mid" else b * NS
                    for s in range(NS):
                        if s:
                            for name in jobs(kind, s - 1):
                                move(kind, b, par, name)
                        if present(kind, s, 2) and not (kind == "end" and s >= 2):
                            w = ktiles(s - 2) * GS * P
                            upper = probsT2[s % 2][:, 0, :, :].rearrange("p a b -> p (a b)").bitcast(F32R)
                            act.wait_ge(turned, t0 + s - 1)
                            act.copy(probsT[s % 2][:, :] if ktiles(s - 2) == 1 else upper,
                                     PT_ps[s % 2][:, 0:w]).then_inc(moved, 1)
                        if present(kind, s, 0):
                            w = ktiles(s) * P
                            act.wait_ge(maxed, t0 + s + 1)
                            for g in range(GS):
                                ins = act.activation(probs[s % 2][:, g, 0:w], S_ps[s % 2][:, g * w:(g + 1) * w], ACT.Exp,
                                                     bias=nmax[s % 4][:, g:g + 1], accum_out=rsum[s % 4][:, g:g + 1])
                            ins.then_inc(exped, 1)
                bodies(act, nb, body)

            @block.vector
            def _(dve):
                links = [0]

                def link(ins):
                    links[0] += 1
                    ins.then_inc(chain, 1)
                    dve.wait_ge(chain, links[0])

                def body(kind, b, par):
                    t0 = dve.snap(b * NS) if kind == "mid" else b * NS
                    dve.sem_clear(chain)
                    links[0] = 0
                    for s in range(NS):
                        if present(kind, s, 0):
                            w = ktiles(s) * P
                            dve.wait_ge(scored, t0 + s + 1)
                            dve.tensor_reduce(nmax[s % 4][:, :], S_ps[s % 2][:, 0:GS * w].rearrange("p (g k) -> p g k", g=GS),
                                              AX.X, ALU.max, negate=True).then_inc(maxed, 1)
                        if present(kind, s, 1) and not (kind == "end" and s >= 1):
                            r = (s - 1) % 4
                            dve.wait_ge(exped, t0 + s)
                            dve.reciprocal(rinv[r][:, :], rsum[r][:, :]).then_inc(inverted, 1)
                        if present(kind, s, 2) and not (kind == "end" and s >= 2) and ktiles(s - 2) == 2:
                            w, pt = 2 * GS * P, probsT2[s % 2]
                            dve.wait_ge(moved, t0 + s - 1)
                            dve.tensor_tensor(pt[:, 1, :, :].rearrange("p a b -> p (a b)").bitcast(F32R), PT_ps[s % 2][:, 0:w],
                                              pt[:, 0, :, :].rearrange("p a b -> p (a b)"), ALU.subtract).then_inc(lowers, 1)
                        if present(kind, s, 3) and not (kind == "end" and s >= 3):
                            dve.wait_ge(valued, t0 + s - 2)
                            sq, own = (s - 3) % NS, ctxT[par if s >= 3 else 1 - par]
                            link(dve.tensor_tensor(zz[:, :, :], O_ps[s % 2][:, 0:GS * P].rearrange("p (q h) -> p q h", h=H),
                                                   cview["mask_head_rows"].unsqueeze(1).to_broadcast((P, GS * QG, H)), ALU.mult))
                            link(dve.tensor_reduce(weighted[:, :], zz[:, :, :], AX.X, ALU.add))
                            dve.tensor_tensor(own[:, 16 * sq:16 * sq + 16], weighted[:, :], O_ps[s % 2][:, GS * P:GS * P + GS * QG],
                                              ALU.mult).then_inc(merged, 1)
                        ready = {"qk": 1, "v": 2}
                        for name in jobs(kind, s - 1) if s else ():
                            if name in ready:
                                m, bank = M_ps[bank_of[name]], bank_of[name]
                                dve.wait_ge(uppers_done, 2 * (one_front(kind, b, "x") - 1) + ready[name])
                            if name == "qk":
                                dve.scalar_tensor_tensor(qT2[1 - par][:, 1, :].bitcast(F32R), m[:, P:S], C ** -0.5,
                                                         qT2[1 - par][:, 0, :], ALU.mult, ALU.subtract)
                                dve.tensor_tensor(kT2[1 - par][:, 1, :].bitcast(F32R), m[:, S:2 * S], kT2[1 - par][:, 0, :],
                                                  ALU.subtract).then_inc(free[bank], 1)
                            if name == "v":
                                dve.tensor_tensor(v2[1 - par][:, 1, :, :].rearrange("p a d -> p (a d)").bitcast(F32R), m[:, 0:S],
                                                  v2[1 - par][:, 0, :, :].rearrange("p a d -> p (a d)"),
                                                  ALU.subtract).then_inc(free[bank], 1)
                        if s == 4 and "tail" in SECTIONS[kind]:
                            dve.wait_ge(gathered[1 - par], (b - 2 + par) * 32 + 64)
                            er = expert_rows[1 - par]
                            for i in range(2):
                                w = slot_w[:, bass.ds((b - 1) * 2 + i, 1), :].rearrange("p a k -> p (a k)")
                                ins = dve.scalar_tensor_tensor(with_one[:, i, :], er[:, i, 0, :], w[:, 0:1],
                                                               residual[:, bass.ds((b - 1) * 2 + i, 1), :].rearrange("p a d -> p (a d)"),
                                                               ALU.mult, ALU.add)
                            link(ins)
                            for i in range(2):
                                w = slot_w[:, bass.ds((b - 1) * 2 + i, 1), :].rearrange("p a k -> p (a k)")
                                ins = dve.scalar_tensor_tensor(with_two[:, i, :], er[:, i, 1, :], w[:, 1:2],
                                                               with_one[:, i, :], ALU.mult, ALU.add)
                            link(ins)
                        if s and "out" in jobs(kind, s - 1):
                            bank = bank_of["out"]
                            dve.wait_ge(full[bank], bank_tally[bank](kind, b, "out"))
                            dve.wait_ge(written, 16 * one_tail(kind, b, "x"))
                            dve.tensor_tensor(total[:, :, :], M_ps[bank][:, 0:S].rearrange("p (a d) -> p a d", a=2),
                                              with_two[:, :, :], ALU.add).then_inc(free[bank], 1)
                bodies(dve, nb, body)

            @block.tensor
            def _(pe):
                def project(kind, b, par, name):
                    bank = bank_of[name]
                    m, n = M_ps[bank], bank_tally[bank](kind, b, name)
                    if not (isinstance(n, int) and n == 1):
                        pe.wait_ge(free[bank], n - 1)
                    if name == "qk":
                        pe.wait_ge(xt_in[1 - par], 16 if kind in ("pro", "first") else 8 * b + 16 + 8 * par)
                        pe.matmul(m[:, 0:S], wview["q1"], xt[1 - par][:, :], start=True, stop=True)
                        ins = pe.matmul(m[:, S:2 * S], wview["k1"], xt[1 - par][:, :], start=True, stop=True)
                    elif name == "v":
                        for i in range(KT):
                            ins = pe.matmul(m[:, i * D:(i + 1) * D], xt[1 - par][:, i * P:(i + 1) * P], wview["v1"],
                                            start=True, stop=True)
                    elif name == "out":
                        pe.wait_ge(merged, b * NS)
                        for i in range(2):
                            ins = pe.matmul(m[:, i * D:(i + 1) * D], ctxT[1 - par][:, i * P:(i + 1) * P], wview["o1"],
                                            start=True, stop=True)
                    ins.then_inc(full[bank], 1)

                def body(kind, b, par):
                    t0 = pe.snap(b * NS) if kind == "mid" else b * NS
                    for s in range(NS):
                        if present(kind, s, 0):
                            w = ktiles(s) * P
                            pe.wait_ge(built, t0 + s + 1)
                            if not (kind == "first" and s < 2):
                                pe.wait_ge(exped, t0 + s - 1)
                            for g in range(GS):
                                o = S_ps[s % 2][:, g * w:(g + 1) * w]
                                off = S - QG - QG * (GS * s + g)
                                if s < HEAVY:
                                    pe.matmul(o, q_blk[s % 2][:, g, :], kT[par][:, :], start=True, stop=False)
                                else:
                                    for i, (x, y) in enumerate(((0, 0), (0, 1), (1, 0))):
                                        pe.matmul(o, q_blk2[s % 2][:, x, g, :].bitcast(F32R), kT2[par][:, y, :].bitcast(F32R),
                                                  start=(i == 0), stop=False)
                                ins = pe.matmul(o, alibi_l[:, :], alibi_r[:, off:off + w], start=False, stop=True)
                            ins.then_inc(scored, 1)
                        if present(kind, s, 2) and not (kind == "end" and s >= 2):
                            r = s % 2
                            pe.wait_ge(exped, t0 + s - 1)
                            if not (kind == "first" and s < 4):
                                if ktiles(s - 4) == 2:
                                    pe.wait_ge(lowers, lower_count(b, s - 4))
                                else:
                                    pe.wait_ge(moved, t0 + s - 3)
                            for kt in range(ktiles(s - 2)):
                                for g in range(GS):
                                    ins = pe.transpose(PT_ps[r][:, (kt * GS + g) * P:(kt * GS + g + 1) * P],
                                                       probs[r][:, g, kt * P:(kt + 1) * P], ident)
                            ins.then_inc(turned, 1)
                        if present(kind, s, 3) and not (kind == "end" and s >= 3):
                            r, n = (s - 3) % 2, ktiles(s - 3)
                            own = par if s >= 3 else 1 - par
                            if s == 3:
                                bank = bank_of["v"]
                                tl = bank_tally[bank]
                                if kind == "first":
                                    pe.wait_ge(free[bank], tl("pro", -1, "v"))
                                elif kind == "last":
                                    pe.wait_ge(free[bank], tl("mid", b - 1, "v"))
                                else:
                                    pe.wait_ge(free[bank], tl("mid", b, "v") - tl.total("mid"))
                            if n == 2:
                                pe.wait_ge(lowers, lower_count(b, s - 3))
                            else:
                                pe.wait_ge(moved, t0 + s - 2)
                            pe.wait_ge(picked, t0 + s - 2)
                            if not (kind == "first" and s < 5):
                                pe.wait_ge(merged, t0 + s - 4)
                            o = O_ps[s % 2][:, 0:GS * P]
                            if n == 1:
                                pe.matmul(o, v0[own][:, :], probsT[r][:, :], start=True, stop=True)
                            else:
                                parts = [(kt, x, y) for kt in range(n) for x, y in ((0, 0), (0, 1), (1, 0))]
                                for part in parts:
                                    kt, x, y = part
                                    pe.matmul(o, v2[own][:, x, kt, :].bitcast(F32R), probsT2[r][:, y, kt, :].bitcast(F32R),
                                              start=(part == parts[0]), stop=(part == parts[-1]))
                            ins = pe.matmul(O_ps[s % 2][:, GS * P:GS * P + GS * QG], cview["head_channels"],
                                            pick[(s - 3) % 4][:, :, :].rearrange("p g q -> p (g q)"), start=True, stop=True)
                            ins.then_inc(valued, 1)
                        for name in jobs(kind, s):
                            project(kind, b, par, name)
                bodies(pe, nb, body)


def shape_constants(nb, cap):
    T = nb * S
    p = np.arange(P)
    c = {
        "ident": np.eye(P),
        "mask_head_rows": p[:, None] // C == np.arange(H),
        "mask_head": p[:, None] % H == np.arange(H),
        "mask_query": p[:, None] // H == QG - 1 - np.arange(QG),
        "pick_query": p[:, None] // H == np.arange(QG),
        "head_channels": p[:, None] % H == p[None, :] // C,
        "iota": np.broadcast_to(np.arange(E), (P, E)),
        "dump": (E * cap + p[:, None, None] + P * np.arange(2)[None, :, None] + T * np.arange(2)[None, None, :]).reshape(P, 4),
    }
    consts = np.concatenate([np.asarray(c[n], np.float32) for n in CONSTS], axis=1)
    spread = np.tile(0.5 * (np.arange(E * HID)[None, :] // HID == np.arange(E)[:, None]), (2, 1))
    tri = np.concatenate([p[:, None] < p[None, :], np.ones((P, P))], axis=1)
    ratio = 2.0 ** (-8.0 / H)
    slopes = np.asarray([ratio ** (i + 1) for i in range(H)], np.float32)
    parts, rest = [], slopes.astype(np.float64)
    for _ in range(3):
        part = (rest.astype(np.float32).view(np.uint32) & np.uint32(0xFFFF0000)).view(np.float32).astype(np.float64)
        parts.append(part)
        rest = rest - part
    own = np.arange(QG)[:, None] == p[None, :] // H
    alibi_l = np.concatenate([own * np.tile(part, QG)[None, :] for part in parts], axis=0)
    j = np.arange(2 * S - QG)
    dist = j[None, :] - (S - QG) - np.arange(QG)[:, None]
    alibi_r = np.tile(np.where(dist <= 0, dist, -1e30), (3, 1))
    named = {"consts": consts, "spread": spread, "tri": tri, "alibi_l": alibi_l, "alibi_r": alibi_r}
    return {n: v.astype(np.float32) for n, v in named.items()}


def capacity(tokens):
    return max(1, int(math.ceil(1.25 * tokens * 2 / E)))


def kernel(**inputs):
    import concourse.bacc as bacc
    from concourse.bass_utils import run_bass_kernel_spmd

    a = {k: np.asarray(v) for k, v in inputs.items()}
    nb = a["L0_attn_x"].shape[0]
    T = nb * S
    cap = capacity(T)
    wqkv, bqkv = a["L0_attn_W_qkv"], a["L0_attn_b_qkv"]
    w = {
        "wqkv": wqkv,
        "wv_q": np.concatenate([wqkv[:, 2 * D:], wqkv[:, 0:D].reshape(D, H, C).transpose(0, 2, 1).reshape(D, D)], axis=1),
        "wout": a["L0_attn_W_out"],
        "wdown": np.concatenate([a["L0_ffn_We_down"].transpose(0, 2, 1).reshape(E * HID, D), a["L0_ffn_Ws_down"].T],
                                axis=0).reshape(NK, P, D).transpose(1, 0, 2).reshape(P, NK * D),
        "wrouter0": a["L0_ffn_Wg"].T,
        "wshared_gate": a["L0_ffn_Wsg"].T,
        "bq": bqkv[0:D].reshape(P, 1),
        "bk": bqkv[D:2 * D].reshape(P, 1),
        "q1": a["L1_attn_q_w"], "k1": a["L1_attn_k_w"], "v1": a["L1_attn_v_w"], "o1": a["L1_attn_o_w"],
        "wrouter1": a["L1_ffn_router_w"].T,
        "b1": a["L1_ffn_b1"].reshape(E, FF // P, P).transpose(2, 0, 1).reshape(P, -1),
    }
    arrays = {
        "x": a["L0_attn_x"].reshape(T, D),
        "weights": np.concatenate([w[n] for n in WEIGHTS], axis=1),
        "ffn_in": np.concatenate([a["L0_ffn_We_gate"].reshape(E * HID, D), a["L0_ffn_Ws_gate"],
                                  a["L0_ffn_We_up"].reshape(E * HID, D), a["L0_ffn_Ws_up"]], axis=0).T,
        "rows": np.concatenate([bqkv[2 * D:3 * D], bqkv[0:D].reshape(H, C).T.reshape(-1), a["L0_attn_b_out"], a["L1_ffn_router_b"]]),
        "rel_k": a["L0_attn_rel_emb_k"].T,
        "rel_v": a["L0_attn_rel_emb_v"],
        "w1": a["L1_ffn_w1"], "w2": a["L1_ffn_w2"], "b2": a["L1_ffn_b2"].reshape(-1),
        **shape_constants(nb, cap),
    }
    arrays = {"in_" + k: np.ascontiguousarray(v) for k, v in arrays.items()}
    nc = bacc.Bacc("TRN2", target_bir_lowering=False, num_devices=1)
    io = {k[3:]: nc.dram_tensor(k, v.shape, mybir.dt.from_np(v.dtype), kind="ExternalInput").ap() for k, v in arrays.items()}
    io["out"] = nc.dram_tensor("out_0", (T, D), F32, kind="ExternalOutput").ap()
    program(nc, io, nb, cap)
    r = run_bass_kernel_spmd(nc, [arrays], core_ids=[0])
    return r.results[0]["out_0"].reshape(nb, S, D)
```
